# Optimizing a Trainium2 kernel written in Bass

```python
import numpy as np
import jax
import jax.numpy as jnp

def _softmax(x, axis=-1):
    return jax.nn.softmax(x, axis=axis)

def _gelu(x):
    return jax.nn.gelu(x, approximate=True)

def _silu(x):
    return jax.nn.silu(x)

def _sigmoid(x):
    return jax.nn.sigmoid(x)

def _layernorm(x, axis=-1, eps=1e-05):
    m = jnp.mean(x, axis=axis, keepdims=True)
    v = jnp.var(x, axis=axis, keepdims=True)
    return (x - m) / jnp.sqrt(v + eps)

def _scatter_add(tgt, idx, src, axis=0):
    return tgt.at[idx].add(src)

def _segment_sum(src, seg, n):
    return jax.ops.segment_sum(src, seg, n)
kernel_name = 'mk_vit_tower_cls_d4_tok_img768_r4_4fb596'

def setup_inputs(seed: int=0):
    np.random.seed(seed)
    _w = jnp.asarray

    def _rec_inputs():
        import jax
        import jax.numpy as jnp
        _rk = jax.random.key(seed)
        x = 7.57192e-06 + 1.00007 * jax.random.normal(jax.random.fold_in(_rk, 1), (16, 3, 112, 112), jnp.float32)
        cls_tok = 0.02 * jax.random.normal(jax.random.fold_in(_rk, 5), (1, 1, 192), jnp.float32)
        return (x, cls_tok)
    x, cls_tok = _rec_inputs()

    def _L0_tok_setup():
        import jax, jax.numpy as jnp
        import numpy as np
        B, IN, IMG = (64, 3, 224)
        PATCH, LEVELS, D = (16, 4, 192)
        ISQ2 = 0.7071067811865476
        DN = ('NCHW', 'OIHW', 'NCHW')

        def conv(x, w, b=None, stride=1, pad=((0, 0), (0, 0)), groups=1):
            y = jax.lax.conv_general_dilated(x, w, (stride, stride), pad, dimension_numbers=DN, feature_group_count=groups)
            return y if b is None else y + b[None, :, None, None]

        def dwconv(x, wd, wp, bp):
            y = conv(x, wd, pad=((1, 1), (1, 1)), groups=x.shape[1])
            return conv(y, wp, bp)

        def haar_dwt2(x):
            xe, xo = (x[..., ::2], x[..., 1::2])
            lo_w, hi_w = ((xe + xo) * ISQ2, (xe - xo) * ISQ2)

            def split_h(t):
                te, to = (t[..., ::2, :], t[..., 1::2, :])
                return ((te + to) * ISQ2, (te - to) * ISQ2)
            ll, lh = split_h(lo_w)
            hl, hh = split_h(hi_w)
            return (ll, lh, hl, hh)

        def wavelet_packet(x):
            f = x
            for _ in range(LEVELS):
                b, k, h, w = f.shape
                ll, lh, hl, hh = haar_dwt2(f)
                bands = jnp.stack([ll, lh, hl, hh], axis=1)
                bands = bands.reshape(b, 4, k // IN, IN, h // 2, w // 2)
                f = jnp.transpose(bands, (0, 2, 1, 3, 4, 5)).reshape(b, 4 * k, h // 2, w // 2)
            return f

        def gelu(x):
            return jax.nn.gelu(x, approximate=False)

        def forward(x, pl_w, pl_b, pl_dw, pl_pw, pl_pwb, pg_w1, pg_b1, pg_dw, pg_pw, pg_pwb, pg_w2, pg_b2, alpha, f1_dw, f1_pw, f1_pwb, f2_dw, f2_pw, f2_pwb, f3_dw, f3_pw, f3_pwb, ln_g, ln_b, cls):
            loc = conv(x, pl_w, pl_b, stride=PATCH)
            loc = dwconv(gelu(loc), pl_dw, pl_pw, pl_pwb)
            g = wavelet_packet(x)
            g = gelu(conv(g, pg_w1, pg_b1))
            g = gelu(dwconv(g, pg_dw, pg_pw, pg_pwb))
            glob = conv(g, pg_w2, pg_b2)
            gate = 0.5 * (jnp.tanh(alpha) + 1.0)
            h = (1.0 - gate) * loc + gate * glob
            h = jax.nn.relu(dwconv(h, f1_dw, f1_pw, f1_pwb))
            h = jax.nn.relu(dwconv(h, f2_dw, f2_pw, f2_pwb))
            h = dwconv(loc + h, f3_dw, f3_pw, f3_pwb)
            t = jnp.transpose(h.reshape(h.shape[0], D, -1), (0, 2, 1))
            mu = jnp.mean(t, -1, keepdims=True)
            var = jnp.mean((t - mu) ** 2, -1, keepdims=True)
            t = (t - mu) / jnp.sqrt(var + 1e-05) * ln_g + ln_b
            cls_tok = jnp.broadcast_to(cls, (t.shape[0], 1, D))
            return jnp.concatenate([cls_tok, t], axis=1)
        key = jax.random.key(seed)
        ks = jax.random.split(key, 32)

        def rn(i, shape, s=0.02):
            return jax.random.normal(ks[i], shape, jnp.float32) * s
        KW = IN * 4 ** LEVELS
        return {'x': jax.random.normal(ks[0], (B, IN, IMG, IMG), jnp.float32), 'pl_w': rn(1, (D, IN, PATCH, PATCH)), 'pl_b': rn(2, (D,)), 'pl_dw': rn(3, (D, 1, 3, 3)), 'pl_pw': rn(4, (D, D, 1, 1)), 'pl_pwb': rn(5, (D,)), 'pg_w1': rn(6, (D, KW, 1, 1)), 'pg_b1': rn(7, (D,)), 'pg_dw': rn(8, (D, 1, 3, 3)), 'pg_pw': rn(9, (D, D, 1, 1)), 'pg_pwb': rn(10, (D,)), 'pg_w2': rn(11, (D, D, 1, 1)), 'pg_b2': rn(12, (D,)), 'alpha': jnp.zeros((1, D, 1, 1), jnp.float32), 'f1_dw': rn(13, (D, 1, 3, 3)), 'f1_pw': rn(14, (D, D, 1, 1)), 'f1_pwb': rn(15, (D,)), 'f2_dw': rn(16, (D, 1, 3, 3)), 'f2_pw': rn(17, (D, D, 1, 1)), 'f2_pwb': rn(18, (D,)), 'f3_dw': rn(19, (D, 1, 3, 3)), 'f3_pw': rn(20, (D, D, 1, 1)), 'f3_pwb': rn(21, (D,)), 'ln_g': jnp.ones((D,), jnp.float32), 'ln_b': jnp.zeros((D,), jnp.float32), 'cls': rn(22, (1, 1, D))}
    _L0_tok_all = _L0_tok_setup()
    _L0_tok_in = {k: v for k, v in _L0_tok_all.items() if k in ('pl_w', 'pl_b', 'pl_dw', 'pl_pw', 'pl_pwb', 'pg_w1', 'pg_b1', 'pg_dw', 'pg_pw', 'pg_pwb', 'pg_w2', 'pg_b2', 'alpha', 'f1_dw', 'f1_pw', 'f1_pwb', 'f2_dw', 'f2_pw', 'f2_pwb', 'f3_dw', 'f3_pw', 'f3_pwb', 'ln_g', 'ln_b', 'cls')}
    del _L0_tok_all

    def _L0_attn_setup():
        import jax, jax.numpy as jnp
        import numpy as np
        import math
        N_LAYER, N_EMBD, LAYER_ID = (12, 192, 0)
        B, T, C = (32, 256, N_EMBD)

        def _init_params():
            r01 = LAYER_ID / (N_LAYER - 1)
            r1a0 = 1.0 - LAYER_ID / N_LAYER
            h = np.arange(C, dtype=np.float32)
            time_decay = (-5.0 + 8.0 * (h / (C - 1)) ** (0.7 + 1.3 * r01)).astype(np.float32)
            zigzag = np.array([(i + 1) % 3 - 1 for i in range(C)], dtype=np.float32) * 0.5
            time_first = (np.ones(C, dtype=np.float32) * math.log(0.3) + zigzag).astype(np.float32)
            xlin = (np.arange(C, dtype=np.float32) / C).reshape(1, 1, C)
            time_mix_k = np.power(xlin, r1a0).astype(np.float32)
            time_mix_v = (np.power(xlin, r1a0) + 0.3 * r01).astype(np.float32)
            time_mix_r = np.power(xlin, 0.5 * r1a0).astype(np.float32)
            return (time_decay, time_first, time_mix_k, time_mix_v, time_mix_r)

        def _wkv(w, u, k, v):

            def step(carry, kv):
                p, q, o = carry
                kt, vt = kv
                no = jnp.maximum(o, u + kt)
                A = jnp.exp(o - no)
                Bc = jnp.exp(u + kt - no)
                y = (A * p + Bc * vt) / (A * q + Bc)
                no2 = jnp.maximum(w + o, kt)
                A2 = jnp.exp(w + o - no2)
                B2 = jnp.exp(kt - no2)
                return ((A2 * p + B2 * vt, A2 * q + B2, no2), y)
            b = k.shape[0]
            init = (jnp.zeros((b, C), jnp.float32), jnp.zeros((b, C), jnp.float32), jnp.full((b, C), -1e+38, jnp.float32))
            kT = jnp.swapaxes(k, 0, 1)
            vT = jnp.swapaxes(v, 0, 1)
            _, ys = jax.lax.scan(step, init, (kT, vT))
            return jnp.swapaxes(ys, 0, 1)
        key = jax.random.key(seed)
        ks = jax.random.split(key, 5)
        td, tf, tmk, tmv, tmr = _init_params()
        scale = 0.02
        return {'x': jax.random.normal(ks[0], (B, T, C), dtype=jnp.float32), 'time_decay': jnp.asarray(td), 'time_first': jnp.asarray(tf), 'time_mix_k': jnp.asarray(tmk), 'time_mix_v': jnp.asarray(tmv), 'time_mix_r': jnp.asarray(tmr), 'Wk': jax.random.normal(ks[1], (C, C), dtype=jnp.float32) * scale, 'Wv': jax.random.normal(ks[2], (C, C), dtype=jnp.float32) * scale, 'Wr': jax.random.normal(ks[3], (C, C), dtype=jnp.float32) * scale, 'Wo': jax.random.normal(ks[4], (C, C), dtype=jnp.float32) * scale}
    _L0_attn_all = _L0_attn_setup()
    _L0_attn_in = {k: v for k, v in _L0_attn_all.items() if k in ('time_decay', 'time_first', 'time_mix_k', 'time_mix_v', 'time_mix_r', 'Wk', 'Wv', 'Wr', 'Wo')}
    del _L0_attn_all

    def _L0_ffn_setup():
        import jax, jax.numpy as jnp
        import numpy as np
        B, S, D_IN, D_HID, D_OUT = (32, 128, 192, 768, 192)
        key = jax.random.key(seed)
        k1, k2, k3, k4 = jax.random.split(key, 4)
        init_k = float(np.sqrt(1.0 / D_IN))
        init_k2 = float(np.sqrt(1.0 / D_HID))
        x = jax.random.normal(k1, (B, S, D_IN), dtype=jnp.float32)
        in_weight = jax.random.uniform(k2, (D_HID, D_IN), dtype=jnp.float32, minval=-init_k, maxval=init_k)
        in_bias = jax.random.uniform(k3, (D_HID,), dtype=jnp.float32, minval=-init_k, maxval=init_k)
        out_weight = jax.random.uniform(k4, (D_HID, D_OUT), dtype=jnp.float32, minval=-init_k2, maxval=init_k2)
        return {'x': x, 'in_weight': in_weight, 'in_bias': in_bias, 'out_weight': out_weight}
    _L0_ffn_all = _L0_ffn_setup()
    _L0_ffn_in = {k: v for k, v in _L0_ffn_all.items() if k in ('in_weight', 'in_bias', 'out_weight')}
    del _L0_ffn_all

    def _L1_attn_setup():
        import jax, jax.numpy as jnp
        import numpy as np
        NUM_HEADS = 8

        def _attn(q, k, v, scale):
            a = jax.nn.softmax(jnp.einsum('bhqd,bhkd->bhqk', q, k) * scale, axis=-1)
            return jnp.einsum('bhqk,bhkd->bhqd', a, v)
        key = jax.random.key(seed)
        k1, k2, k3 = jax.random.split(key, 3)
        B, N, C = (8, 256, 192)
        x = jax.random.normal(k1, (B, N, C), dtype=jnp.float32)
        w_qkv = jax.random.normal(k2, (3 * C, C), dtype=jnp.float32) * 0.02
        w_proj = jax.random.normal(k3, (C, C), dtype=jnp.float32) * 0.02
        b_proj = jnp.zeros((C,), dtype=jnp.float32)
        return {'x': x, 'w_qkv': w_qkv, 'w_proj': w_proj, 'b_proj': b_proj}
    _L1_attn_all = _L1_attn_setup()
    _L1_attn_in = {k: v for k, v in _L1_attn_all.items() if k in ('w_qkv', 'w_proj', 'b_proj')}
    del _L1_attn_all

    def _L1_ffn_setup():
        import jax, jax.numpy as jnp
        import numpy as np
        S, B, DIM = (256, 4, 192)
        N_EXPERTS = 8
        HID = 512
        key = jax.random.key(seed)
        ks = jax.random.split(key, 6)
        scale = 0.02
        return {'hidden_states': jax.random.normal(ks[0], (S, B, DIM), dtype=jnp.float32), 'router_w': jax.random.normal(ks[1], (DIM, N_EXPERTS), dtype=jnp.float32) * scale, 'router_b': jnp.zeros((N_EXPERTS,), dtype=jnp.float32), 'w1': jax.random.normal(ks[2], (N_EXPERTS, DIM, HID), dtype=jnp.float32) * scale, 'w2': jax.random.normal(ks[3], (N_EXPERTS, DIM, HID), dtype=jnp.float32) * scale, 'w3': jax.random.normal(ks[4], (N_EXPERTS, HID, DIM), dtype=jnp.float32) * scale}
    _L1_ffn_all = _L1_ffn_setup()
    _L1_ffn_in = {k: v for k, v in _L1_ffn_all.items() if k in ('router_w', 'router_b', 'w1', 'w2', 'w3')}
    del _L1_ffn_all

    def _L2_attn_setup():
        import jax, jax.numpy as jnp
        import numpy as np
        import math
        B, N, DIM = (4, 512, 192)
        HEADS, DIM_HEAD = (12, 64)
        SCALE = math.sqrt(DIM_HEAD)

        def _split_heads(t):
            b, n, _ = t.shape
            return t.reshape(b, n, HEADS, DIM_HEAD).transpose(0, 2, 1, 3)
        key = jax.random.key(seed)
        ks = jax.random.split(key, 5)
        inner = HEADS * DIM_HEAD
        x = jax.random.normal(ks[0], (B, N, DIM), dtype=jnp.float32)
        w_q = jax.random.normal(ks[1], (DIM, inner), dtype=jnp.float32) * 0.02
        w_k = jax.random.normal(ks[2], (DIM, inner), dtype=jnp.float32) * 0.02
        w_v = jax.random.normal(ks[3], (DIM, inner), dtype=jnp.float32) * 0.02
        w_o = jax.random.normal(ks[4], (inner, DIM), dtype=jnp.float32) * 0.02
        b_o = jnp.zeros((DIM,), dtype=jnp.float32)
        return {'x': x, 'w_q': w_q, 'w_k': w_k, 'w_v': w_v, 'w_o': w_o, 'b_o': b_o}
    _L2_attn_all = _L2_attn_setup()
    _L2_attn_in = {k: v for k, v in _L2_attn_all.items() if k in ('w_q', 'w_k', 'w_v', 'w_o', 'b_o')}
    del _L2_attn_all

    def _L2_ffn_setup():
        import jax, jax.numpy as jnp
        import numpy as np
        key = jax.random.key(seed)
        ks = jax.random.split(key, 6)
        B, N, D, E, S, H = (4, 1024, 192, 4, 256, 768)
        sc = lambda d: 1.0 / np.sqrt(d)
        return {'x': jax.random.normal(ks[0], (B, N, D), dtype=jnp.float32), 'phi': jax.random.normal(ks[1], (E, S, D), dtype=jnp.float32) * sc(D), 'w1': jax.random.normal(ks[2], (E, D, H), dtype=jnp.float32) * sc(D), 'b1': jnp.zeros((E, H), dtype=jnp.float32), 'w2': jax.random.normal(ks[3], (E, H, D), dtype=jnp.float32) * sc(H), 'b2': jnp.zeros((E, D), dtype=jnp.float32)}
    _L2_ffn_all = _L2_ffn_setup()
    _L2_ffn_in = {k: v for k, v in _L2_ffn_all.items() if k in ('phi', 'w1', 'b1', 'w2', 'b2')}
    del _L2_ffn_all

    def _L3_attn_setup():
        import jax, jax.numpy as jnp
        import numpy as np
        B, T, C = (2, 512, 192)
        N_HEADS = 12
        D_K = C // N_HEADS
        key = jax.random.key(seed)
        k1, k2, k3, k4, k5 = jax.random.split(key, 5)
        x = jax.random.normal(k1, (B, T, C), dtype=jnp.float32)
        query_mat = jax.random.normal(k2, (C, N_HEADS, D_K), dtype=jnp.float32) * (2.0 / (C + D_K)) ** 0.5
        key_mat = jax.random.normal(k3, (C, N_HEADS, D_K), dtype=jnp.float32) * (2.0 / (C + D_K)) ** 0.5
        value_mat = jax.random.normal(k4, (C, N_HEADS, D_K), dtype=jnp.float32) * (2.0 / (C + D_K)) ** 0.5
        linear_m1 = jax.random.normal(k5, (C, C), dtype=jnp.float32) * (2.0 / (C + C)) ** 0.5
        return {'x': x, 'query_mat': query_mat, 'key_mat': key_mat, 'value_mat': value_mat, 'linear_m1': linear_m1}
    _L3_attn_all = _L3_attn_setup()
    _L3_attn_in = {k: v for k, v in _L3_attn_all.items() if k in ('query_mat', 'key_mat', 'value_mat', 'linear_m1')}
    del _L3_attn_all

    def _L3_ffn_setup():
        import jax, jax.numpy as jnp
        import numpy as np
        B, S, D = (4, 256, 192)
        E = 8
        H = 192
        HS = 768
        TOPK_ROUTED = 2
        key = jax.random.key(seed)
        ks = jax.random.split(key, 10)
        w = lambda k, shape: jax.random.normal(k, shape, dtype=jnp.float32) * 0.02
        return {'x': jax.random.normal(ks[0], (B, S, D), dtype=jnp.float32), 'router_w': w(ks[1], (D, E)), 'w_gate': w(ks[2], (E, D, H)), 'w_up': w(ks[3], (E, D, H)), 'w_down': w(ks[4], (E, H, D)), 'ws_gate': w(ks[5], (D, HS)), 'ws_up': w(ks[6], (D, HS)), 'ws_down': w(ks[7], (HS, D)), 'sg_w': w(ks[8], (D, 1)), 'sg_b': jnp.zeros((1,), jnp.float32)}
    _L3_ffn_all = _L3_ffn_setup()
    _L3_ffn_in = {k: v for k, v in _L3_ffn_all.items() if k in ('router_w', 'w_gate', 'w_up', 'w_down', 'ws_gate', 'ws_up', 'ws_down', 'sg_w', 'sg_b')}
    del _L3_ffn_all
    return {'x': x, 'cls_tok': cls_tok, 'L0_tok_pl_w': _L0_tok_in['pl_w'], 'L0_tok_pl_b': _L0_tok_in['pl_b'], 'L0_tok_pl_dw': _L0_tok_in['pl_dw'], 'L0_tok_pl_pw': _L0_tok_in['pl_pw'], 'L0_tok_pl_pwb': _L0_tok_in['pl_pwb'], 'L0_tok_pg_w1': _L0_tok_in['pg_w1'], 'L0_tok_pg_b1': _L0_tok_in['pg_b1'], 'L0_tok_pg_dw': _L0_tok_in['pg_dw'], 'L0_tok_pg_pw': _L0_tok_in['pg_pw'], 'L0_tok_pg_pwb': _L0_tok_in['pg_pwb'], 'L0_tok_pg_w2': _L0_tok_in['pg_w2'], 'L0_tok_pg_b2': _L0_tok_in['pg_b2'], 'L0_tok_alpha': _L0_tok_in['alpha'], 'L0_tok_f1_dw': _L0_tok_in['f1_dw'], 'L0_tok_f1_pw': _L0_tok_in['f1_pw'], 'L0_tok_f1_pwb': _L0_tok_in['f1_pwb'], 'L0_tok_f2_dw': _L0_tok_in['f2_dw'], 'L0_tok_f2_pw': _L0_tok_in['f2_pw'], 'L0_tok_f2_pwb': _L0_tok_in['f2_pwb'], 'L0_tok_f3_dw': _L0_tok_in['f3_dw'], 'L0_tok_f3_pw': _L0_tok_in['f3_pw'], 'L0_tok_f3_pwb': _L0_tok_in['f3_pwb'], 'L0_tok_ln_g': _L0_tok_in['ln_g'], 'L0_tok_ln_b': _L0_tok_in['ln_b'], 'L0_tok_cls': _L0_tok_in['cls'], 'L0_attn_time_decay': _L0_attn_in['time_decay'], 'L0_attn_time_first': _L0_attn_in['time_first'], 'L0_attn_time_mix_k': _L0_attn_in['time_mix_k'], 'L0_attn_time_mix_v': _L0_attn_in['time_mix_v'], 'L0_attn_time_mix_r': _L0_attn_in['time_mix_r'], 'L0_attn_Wk': _L0_attn_in['Wk'], 'L0_attn_Wv': _L0_attn_in['Wv'], 'L0_attn_Wr': _L0_attn_in['Wr'], 'L0_attn_Wo': _L0_attn_in['Wo'], 'L0_ffn_in_weight': _L0_ffn_in['in_weight'], 'L0_ffn_in_bias': _L0_ffn_in['in_bias'], 'L0_ffn_out_weight': _L0_ffn_in['out_weight'], 'L1_attn_w_qkv': _L1_attn_in['w_qkv'], 'L1_attn_w_proj': _L1_attn_in['w_proj'], 'L1_attn_b_proj': _L1_attn_in['b_proj'], 'L1_ffn_router_w': _L1_ffn_in['router_w'], 'L1_ffn_router_b': _L1_ffn_in['router_b'], 'L1_ffn_w1': _L1_ffn_in['w1'], 'L1_ffn_w2': _L1_ffn_in['w2'], 'L1_ffn_w3': _L1_ffn_in['w3'], 'L2_attn_w_q': _L2_attn_in['w_q'], 'L2_attn_w_k': _L2_attn_in['w_k'], 'L2_attn_w_v': _L2_attn_in['w_v'], 'L2_attn_w_o': _L2_attn_in['w_o'], 'L2_attn_b_o': _L2_attn_in['b_o'], 'L2_ffn_phi': _L2_ffn_in['phi'], 'L2_ffn_w1': _L2_ffn_in['w1'], 'L2_ffn_b1': _L2_ffn_in['b1'], 'L2_ffn_w2': _L2_ffn_in['w2'], 'L2_ffn_b2': _L2_ffn_in['b2'], 'L3_attn_query_mat': _L3_attn_in['query_mat'], 'L3_attn_key_mat': _L3_attn_in['key_mat'], 'L3_attn_value_mat': _L3_attn_in['value_mat'], 'L3_attn_linear_m1': _L3_attn_in['linear_m1'], 'L3_ffn_router_w': _L3_ffn_in['router_w'], 'L3_ffn_w_gate': _L3_ffn_in['w_gate'], 'L3_ffn_w_up': _L3_ffn_in['w_up'], 'L3_ffn_w_down': _L3_ffn_in['w_down'], 'L3_ffn_ws_gate': _L3_ffn_in['ws_gate'], 'L3_ffn_ws_up': _L3_ffn_in['ws_up'], 'L3_ffn_ws_down': _L3_ffn_in['ws_down'], 'L3_ffn_sg_w': _L3_ffn_in['sg_w'], 'L3_ffn_sg_b': _L3_ffn_in['sg_b']}

def reference(x, cls_tok, L0_tok_pl_w, L0_tok_pl_b, L0_tok_pl_dw, L0_tok_pl_pw, L0_tok_pl_pwb, L0_tok_pg_w1, L0_tok_pg_b1, L0_tok_pg_dw, L0_tok_pg_pw, L0_tok_pg_pwb, L0_tok_pg_w2, L0_tok_pg_b2, L0_tok_alpha, L0_tok_f1_dw, L0_tok_f1_pw, L0_tok_f1_pwb, L0_tok_f2_dw, L0_tok_f2_pw, L0_tok_f2_pwb, L0_tok_f3_dw, L0_tok_f3_pw, L0_tok_f3_pwb, L0_tok_ln_g, L0_tok_ln_b, L0_tok_cls, L0_attn_time_decay, L0_attn_time_first, L0_attn_time_mix_k, L0_attn_time_mix_v, L0_attn_time_mix_r, L0_attn_Wk, L0_attn_Wv, L0_attn_Wr, L0_attn_Wo, L0_ffn_in_weight, L0_ffn_in_bias, L0_ffn_out_weight, L1_attn_w_qkv, L1_attn_w_proj, L1_attn_b_proj, L1_ffn_router_w, L1_ffn_router_b, L1_ffn_w1, L1_ffn_w2, L1_ffn_w3, L2_attn_w_q, L2_attn_w_k, L2_attn_w_v, L2_attn_w_o, L2_attn_b_o, L2_ffn_phi, L2_ffn_w1, L2_ffn_b1, L2_ffn_w2, L2_ffn_b2, L3_attn_query_mat, L3_attn_key_mat, L3_attn_value_mat, L3_attn_linear_m1, L3_ffn_router_w, L3_ffn_w_gate, L3_ffn_w_up, L3_ffn_w_down, L3_ffn_ws_gate, L3_ffn_ws_up, L3_ffn_ws_down, L3_ffn_sg_w, L3_ffn_sg_b):
    import jax
    import jax.numpy as jnp

    def _L0_tok_ref(x, pl_w, pl_b, pl_dw, pl_pw, pl_pwb, pg_w1, pg_b1, pg_dw, pg_pw, pg_pwb, pg_w2, pg_b2, alpha, f1_dw, f1_pw, f1_pwb, f2_dw, f2_pw, f2_pwb, f3_dw, f3_pw, f3_pwb, ln_g, ln_b, cls):
        import jax, jax.numpy as jnp
        import numpy as np
        B, IN, IMG = (64, 3, 224)
        PATCH, LEVELS, D = (16, 4, 192)
        ISQ2 = 0.7071067811865476
        DN = ('NCHW', 'OIHW', 'NCHW')

        def conv(x, w, b=None, stride=1, pad=((0, 0), (0, 0)), groups=1):
            y = jax.lax.conv_general_dilated(x, w, (stride, stride), pad, dimension_numbers=DN, feature_group_count=groups)
            return y if b is None else y + b[None, :, None, None]

        def dwconv(x, wd, wp, bp):
            y = conv(x, wd, pad=((1, 1), (1, 1)), groups=x.shape[1])
            return conv(y, wp, bp)

        def haar_dwt2(x):
            xe, xo = (x[..., ::2], x[..., 1::2])
            lo_w, hi_w = ((xe + xo) * ISQ2, (xe - xo) * ISQ2)

            def split_h(t):
                te, to = (t[..., ::2, :], t[..., 1::2, :])
                return ((te + to) * ISQ2, (te - to) * ISQ2)
            ll, lh = split_h(lo_w)
            hl, hh = split_h(hi_w)
            return (ll, lh, hl, hh)

        def wavelet_packet(x):
            f = x
            for _ in range(LEVELS):
                b, k, h, w = f.shape
                ll, lh, hl, hh = haar_dwt2(f)
                bands = jnp.stack([ll, lh, hl, hh], axis=1)
                bands = bands.reshape(b, 4, k // IN, IN, h // 2, w // 2)
                f = jnp.transpose(bands, (0, 2, 1, 3, 4, 5)).reshape(b, 4 * k, h // 2, w // 2)
            return f

        def gelu(x):
            return jax.nn.gelu(x, approximate=False)

        def forward(x, pl_w, pl_b, pl_dw, pl_pw, pl_pwb, pg_w1, pg_b1, pg_dw, pg_pw, pg_pwb, pg_w2, pg_b2, alpha, f1_dw, f1_pw, f1_pwb, f2_dw, f2_pw, f2_pwb, f3_dw, f3_pw, f3_pwb, ln_g, ln_b, cls):
            loc = conv(x, pl_w, pl_b, stride=PATCH)
            loc = dwconv(gelu(loc), pl_dw, pl_pw, pl_pwb)
            g = wavelet_packet(x)
            g = gelu(conv(g, pg_w1, pg_b1))
            g = gelu(dwconv(g, pg_dw, pg_pw, pg_pwb))
            glob = conv(g, pg_w2, pg_b2)
            gate = 0.5 * (jnp.tanh(alpha) + 1.0)
            h = (1.0 - gate) * loc + gate * glob
            h = jax.nn.relu(dwconv(h, f1_dw, f1_pw, f1_pwb))
            h = jax.nn.relu(dwconv(h, f2_dw, f2_pw, f2_pwb))
            h = dwconv(loc + h, f3_dw, f3_pw, f3_pwb)
            t = jnp.transpose(h.reshape(h.shape[0], D, -1), (0, 2, 1))
            mu = jnp.mean(t, -1, keepdims=True)
            var = jnp.mean((t - mu) ** 2, -1, keepdims=True)
            t = (t - mu) / jnp.sqrt(var + 1e-05) * ln_g + ln_b
            cls_tok = jnp.broadcast_to(cls, (t.shape[0], 1, D))
            return jnp.concatenate([cls_tok, t], axis=1)
        return forward(x, pl_w, pl_b, pl_dw, pl_pw, pl_pwb, pg_w1, pg_b1, pg_dw, pg_pw, pg_pwb, pg_w2, pg_b2, alpha, f1_dw, f1_pw, f1_pwb, f2_dw, f2_pw, f2_pwb, f3_dw, f3_pw, f3_pwb, ln_g, ln_b, cls)

    def _L0_attn_ref(x, time_decay, time_first, time_mix_k, time_mix_v, time_mix_r, Wk, Wv, Wr, Wo):
        import jax, jax.numpy as jnp
        import numpy as np
        import math
        N_LAYER, N_EMBD, LAYER_ID = (12, 192, 0)
        B, T, C = (32, 256, N_EMBD)

        def _init_params():
            r01 = LAYER_ID / (N_LAYER - 1)
            r1a0 = 1.0 - LAYER_ID / N_LAYER
            h = np.arange(C, dtype=np.float32)
            time_decay = (-5.0 + 8.0 * (h / (C - 1)) ** (0.7 + 1.3 * r01)).astype(np.float32)
            zigzag = np.array([(i + 1) % 3 - 1 for i in range(C)], dtype=np.float32) * 0.5
            time_first = (np.ones(C, dtype=np.float32) * math.log(0.3) + zigzag).astype(np.float32)
            xlin = (np.arange(C, dtype=np.float32) / C).reshape(1, 1, C)
            time_mix_k = np.power(xlin, r1a0).astype(np.float32)
            time_mix_v = (np.power(xlin, r1a0) + 0.3 * r01).astype(np.float32)
            time_mix_r = np.power(xlin, 0.5 * r1a0).astype(np.float32)
            return (time_decay, time_first, time_mix_k, time_mix_v, time_mix_r)

        def _wkv(w, u, k, v):

            def step(carry, kv):
                p, q, o = carry
                kt, vt = kv
                no = jnp.maximum(o, u + kt)
                A = jnp.exp(o - no)
                Bc = jnp.exp(u + kt - no)
                y = (A * p + Bc * vt) / (A * q + Bc)
                no2 = jnp.maximum(w + o, kt)
                A2 = jnp.exp(w + o - no2)
                B2 = jnp.exp(kt - no2)
                return ((A2 * p + B2 * vt, A2 * q + B2, no2), y)
            b = k.shape[0]
            init = (jnp.zeros((b, C), jnp.float32), jnp.zeros((b, C), jnp.float32), jnp.full((b, C), -1e+38, jnp.float32))
            kT = jnp.swapaxes(k, 0, 1)
            vT = jnp.swapaxes(v, 0, 1)
            _, ys = jax.lax.scan(step, init, (kT, vT))
            return jnp.swapaxes(ys, 0, 1)
        xx = jnp.pad(x, ((0, 0), (1, 0), (0, 0)))[:, :-1, :]
        xk = x * time_mix_k + xx * (1.0 - time_mix_k)
        xv = x * time_mix_v + xx * (1.0 - time_mix_v)
        xr = x * time_mix_r + xx * (1.0 - time_mix_r)
        k = jnp.einsum('btc,oc->bto', xk, Wk)
        v = jnp.einsum('btc,oc->bto', xv, Wv)
        r = jnp.einsum('btc,oc->bto', xr, Wr)
        sr = jax.nn.sigmoid(r)
        y = _wkv(time_decay, time_first, k, v)
        return jnp.einsum('btc,oc->bto', sr * y, Wo)

    def _L0_ffn_ref(x, in_weight, in_bias, out_weight):
        import jax, jax.numpy as jnp
        import numpy as np
        B, S, D_IN, D_HID, D_OUT = (32, 128, 192, 768, 192)
        lead = x.shape[:-1]
        xt = x.reshape(-1, in_weight.shape[1])
        h = jax.nn.gelu(jnp.einsum('td,hd->th', xt, in_weight) + in_bias, approximate=False)
        out = jnp.einsum('th,ho->to', h, out_weight)
        return out.reshape(*lead, out_weight.shape[1])

    def _L1_attn_ref(x, w_qkv, w_proj, b_proj):
        import jax, jax.numpy as jnp
        import numpy as np
        NUM_HEADS = 8

        def _attn(q, k, v, scale):
            a = jax.nn.softmax(jnp.einsum('bhqd,bhkd->bhqk', q, k) * scale, axis=-1)
            return jnp.einsum('bhqk,bhkd->bhqd', a, v)
        B, N, C = x.shape
        H = NUM_HEADS
        hd = C // H
        g = hd // 3
        scale = hd ** (-0.5)
        qkv = (x @ w_qkv.T).reshape(B, N, 3, H, hd).transpose(2, 0, 3, 1, 4)
        q, k, v = (qkv[0], qkv[1], qkv[2])
        q3, q4, q5 = (q[..., :g], q[..., g:2 * g], q[..., 2 * g:])
        k3, k4, k5 = (k[..., :g], k[..., g:2 * g], k[..., 2 * g:])
        v3, v4, v5 = (v[..., :g], v[..., g:2 * g], v[..., 2 * g:])

        def merge(o):
            return o.transpose(0, 2, 1, 3).reshape(B, N, C // 3)
        x3 = merge(_attn(q4, jnp.concatenate([k3, k4], axis=2), jnp.concatenate([v3, v4], axis=2), scale))
        x4 = merge(_attn(q5, jnp.concatenate([k3, k5], axis=2), jnp.concatenate([v3, v5], axis=2), scale))
        x5 = merge(_attn(q5, jnp.concatenate([k4, k5], axis=2), jnp.concatenate([v4, v5], axis=2), scale))
        out = jnp.concatenate([x3, x4, x5], axis=2)
        return out @ w_proj.T + b_proj

    def _L1_ffn_ref(hidden_states, router_w, router_b, w1, w2, w3):
        import jax, jax.numpy as jnp
        import numpy as np
        S, B, DIM = (256, 4, 192)
        N_EXPERTS = 8
        HID = 512
        s, b, h = hidden_states.shape
        route = jax.nn.softmax(hidden_states @ router_w + router_b, axis=2)
        max_prob = jnp.max(route, axis=2).reshape(-1, 1)
        max_ind = jnp.argmax(route, axis=2).reshape(-1)
        x = hidden_states.reshape(-1, h)
        out = jnp.zeros_like(x)
        for e in range(N_EXPERTS):
            mask = (max_ind == e)[:, None]
            xe = jnp.where(mask, x, 0.0)
            oe = jax.nn.silu(xe @ w1[e]) * (xe @ w2[e]) @ w3[e]
            out = out + jnp.where(mask, oe, 0.0)
        out = out.astype(jnp.bfloat16) * max_prob
        return out.reshape(s, b, h)

    def _L2_attn_ref(x, w_q, w_k, w_v, w_o, b_o):
        import jax, jax.numpy as jnp
        import numpy as np
        import math
        B, N, DIM = (4, 512, 192)
        HEADS, DIM_HEAD = (12, 64)
        SCALE = math.sqrt(DIM_HEAD)

        def _split_heads(t):
            b, n, _ = t.shape
            return t.reshape(b, n, HEADS, DIM_HEAD).transpose(0, 2, 1, 3)
        q = _split_heads(x @ w_q)
        k = _split_heads(x @ w_k)
        v = _split_heads(x @ w_v)
        scores = jnp.einsum('bhnd,bhmd->bhnm', q, k) / SCALE
        attn = jax.nn.softmax(scores, axis=-1)
        h = jnp.einsum('bhnm,bhmd->bhnd', attn, v)
        H = h.transpose(0, 2, 1, 3).reshape(x.shape[0], x.shape[1], HEADS * DIM_HEAD)
        out = H @ w_o + b_o
        return out

    def _L2_ffn_ref(x, phi, w1, b1, w2, b2):
        import jax, jax.numpy as jnp
        import numpy as np
        logits = jnp.einsum('bnd,esd->bnes', x, phi)
        B, N, E, S = logits.shape
        dispatch = jax.nn.softmax(logits, axis=1)
        combine = jax.nn.softmax(logits.reshape(B, N, E * S), axis=-1).reshape(B, N, E, S)
        slots = jnp.einsum('bnd,bnes->besd', x, dispatch)
        h = jax.nn.gelu(jnp.einsum('besd,edh->besh', slots, w1) + b1[None, :, None, :])
        y = jnp.einsum('besh,ehd->besd', h, w2) + b2[None, :, None, :]
        out = jnp.einsum('besd,bnes->bnd', y, combine)
        return out

    def _L3_attn_ref(x, query_mat, key_mat, value_mat, linear_m1):
        import jax, jax.numpy as jnp
        import numpy as np
        B, T, C = (2, 512, 192)
        N_HEADS = 12
        D_K = C // N_HEADS
        b, t, c = x.shape
        h, d_k = (query_mat.shape[1], query_mat.shape[2])
        q = jnp.einsum('btc,chd->bhtd', x, query_mat)
        k = jnp.einsum('btc,chd->bhtd', x, key_mat)
        v = jnp.einsum('btc,chd->bhtd', x, value_mat)
        w = jnp.einsum('bhtd,bhzd->bhtz', q, k) * d_k ** 0.5
        causal = jnp.tril(jnp.ones((t, t), dtype=bool))
        w = jnp.where(causal, w, -jnp.inf)
        w = jax.nn.softmax(w, axis=-1)
        o = jnp.einsum('bhtz,bhzd->bhtd', w, v)
        o = jnp.transpose(o, (0, 2, 1, 3)).reshape(b, t, h * d_k)
        return jnp.einsum('btc,cz->btz', o, linear_m1)

    def _L3_ffn_ref(x, router_w, w_gate, w_up, w_down, ws_gate, ws_up, ws_down, sg_w, sg_b):
        import jax, jax.numpy as jnp
        import numpy as np
        B, S, D = (4, 256, 192)
        E = 8
        H = 192
        HS = 768
        TOPK_ROUTED = 2
        probs = jax.nn.softmax(x @ router_w, axis=-1)
        gates, idx = jax.lax.top_k(probs, TOPK_ROUTED)
        gates = gates / jnp.sum(gates, axis=-1, keepdims=True)
        n_exp = router_w.shape[1]
        dense_g = jnp.sum(jax.nn.one_hot(idx, n_exp, dtype=x.dtype) * gates[..., None], axis=-2)
        g = jax.nn.silu(jnp.einsum('bsd,edh->bseh', x, w_gate))
        u = jnp.einsum('bsd,edh->bseh', x, w_up)
        expert_out = jnp.einsum('bseh,ehd->bsed', g * u, w_down)
        routed = jnp.einsum('bse,bsed->bsd', dense_g, expert_out)
        shared = jax.nn.silu(x @ ws_gate) * (x @ ws_up) @ ws_down
        alpha = jax.nn.sigmoid(x @ sg_w + sg_b)
        return alpha * shared + (1.0 - alpha) * routed
    h = _L0_tok_ref(x, L0_tok_pl_w, L0_tok_pl_b, L0_tok_pl_dw, L0_tok_pl_pw, L0_tok_pl_pwb, L0_tok_pg_w1, L0_tok_pg_b1, L0_tok_pg_dw, L0_tok_pg_pw, L0_tok_pg_pwb, L0_tok_pg_w2, L0_tok_pg_b2, L0_tok_alpha, L0_tok_f1_dw, L0_tok_f1_pw, L0_tok_f1_pwb, L0_tok_f2_dw, L0_tok_f2_pw, L0_tok_f2_pwb, L0_tok_f3_dw, L0_tok_f3_pw, L0_tok_f3_pwb, L0_tok_ln_g, L0_tok_ln_b, L0_tok_cls)
    h = jnp.concatenate([jnp.broadcast_to(cls_tok, (h.shape[0], 1, h.shape[2])), h], axis=1)
    h = h + _L0_attn_ref(_layernorm(h, axis=-1), L0_attn_time_decay, L0_attn_time_first, L0_attn_time_mix_k, L0_attn_time_mix_v, L0_attn_time_mix_r, L0_attn_Wk, L0_attn_Wv, L0_attn_Wr, L0_attn_Wo)
    h = h + _L0_ffn_ref(_layernorm(h, axis=-1), L0_ffn_in_weight, L0_ffn_in_bias, L0_ffn_out_weight)
    h = h + _L1_attn_ref(_layernorm(h, axis=-1), L1_attn_w_qkv, L1_attn_w_proj, L1_attn_b_proj)
    h = h + _L1_ffn_ref(_layernorm(h, axis=-1), L1_ffn_router_w, L1_ffn_router_b, L1_ffn_w1, L1_ffn_w2, L1_ffn_w3)
    h = h + _L2_attn_ref(_layernorm(h, axis=-1), L2_attn_w_q, L2_attn_w_k, L2_attn_w_v, L2_attn_w_o, L2_attn_b_o)
    h = h + _L2_ffn_ref(_layernorm(h, axis=-1), L2_ffn_phi, L2_ffn_w1, L2_ffn_b1, L2_ffn_w2, L2_ffn_b2)
    h = h + _L3_attn_ref(_layernorm(h, axis=-1), L3_attn_query_mat, L3_attn_key_mat, L3_attn_value_mat, L3_attn_linear_m1)
    h = h + _L3_ffn_ref(_layernorm(h, axis=-1), L3_ffn_router_w, L3_ffn_w_gate, L3_ffn_w_up, L3_ffn_w_down, L3_ffn_ws_gate, L3_ffn_ws_up, L3_ffn_ws_down, L3_ffn_sg_w, L3_ffn_sg_b)
    return h

_drawn_inputs = setup_inputs


def setup_inputs(seed=0):
    import zlib

    import numpy as np

    out = dict(_drawn_inputs(seed))
    spreads = {'L0_tok_alpha': (0.0, 0.8),
     'L0_tok_ln_g': (1.0, 0.2),
     'L0_tok_ln_b': (0.0, 0.1),
     'L1_attn_b_proj': (0.0, 0.1),
     'L1_ffn_router_b': (0.0, 0.8),
     'L2_attn_b_o': (0.0, 0.1),
     'L2_ffn_b1': (0.0, 0.759),
     'L2_ffn_b2': (0.0, 0.39)}
    factors = {'x': 8.0,
     'L0_tok_pl_w': 8.0,
     'L0_tok_pl_b': 8.0,
     'L0_tok_pl_dw': 8.0,
     'L0_tok_pl_pw': 8.0,
     'L0_tok_pl_pwb': 4.021,
     'L0_tok_pg_w1': 8.0,
     'L0_tok_pg_b1': 8.0,
     'L0_tok_pg_dw': 8.0,
     'L0_tok_pg_pw': 8.0,
     'L0_tok_pg_pwb': 40.146,
     'L0_tok_pg_w2': 8.0,
     'L0_tok_pg_b2': 30.956,
     'L0_tok_f1_dw': 8.0,
     'L0_tok_f1_pw': 8.0,
     'L0_tok_f1_pwb': 28.719,
     'L0_tok_f2_dw': 8.0,
     'L0_tok_f2_pw': 8.0,
     'L0_tok_f2_pwb': 8.0,
     'L0_tok_f3_dw': 3.03,
     'L0_attn_time_decay': 2.97,
     'L0_attn_time_mix_k': 6.345,
     'L0_attn_time_mix_r': 5.205,
     'L0_attn_Wk': 3.703,
     'L1_ffn_router_w': 8.0,
     'L1_ffn_w1': 8.0,
     'L1_ffn_w2': 8.0,
     'L1_ffn_w3': 8.0,
     'L2_attn_w_q': 8.0,
     'L2_attn_w_k': 8.0,
     'L3_ffn_router_w': 8.0,
     'L3_ffn_w_gate': 8.0,
     'L3_ffn_w_up': 8.0,
     'L3_ffn_w_down': 8.0,
     'L3_ffn_ws_gate': 7.075,
     'L3_ffn_ws_up': 7.641,
     'L3_ffn_ws_down': 7.345,
     'L3_ffn_sg_w': 8.0,
     'L0_attn_time_first': 3.981,
     'L2_ffn_phi': 8.0,
     'L2_ffn_w1': 2.914}
    for name, (base, spread) in spreads.items():
        noise = np.random.default_rng([zlib.crc32(name.encode()), seed]).standard_normal(out[name].shape)
        drawn = base * np.exp(spread * noise) if base else spread * noise
        out[name] = jnp.asarray(drawn.astype(out[name].dtype))
    for name, factor in factors.items():
        out[name] = (out[name] * factor).astype(out[name].dtype)
    return out
```

```python
from contextlib import ExitStack

import numpy as np
import concourse.bass as bass
from concourse import mybir

F32 = mybir.dt.float32
BF16 = mybir.dt.bfloat16
ALU = mybir.AluOpType
ACT = mybir.ActivationFunctionType
AX = mybir.AxisListType

NB = 16
SIDE = 7
NP = SIDE * SIDE
T = NP + 2
TP = 64
NJ = NB // 2
D = 192
DH = D // 2
HALF = NB // 2
NEG = -1e38
EPS = 1e-5
LN = "layernorm"

VEC = {n: i for i, n in enumerate(
    ["pl_b", "pl_pwb", "pg_b1", "pg_pwb", "pg_b2", "alpha", "f1_pwb", "f2_pwb", "decay", "first", "mk", "mv", "mr"])}
TAPS = {n: len(VEC) + 9 * i for i, n in enumerate(["pl", "pg", "f1", "f2", "f3"])}
NVEC = len(VEC) + 45
ROWS = {}
_at = 0
for _n, _w in [("f3_pwb", D), ("ln_g", D), ("ln_b", D), ("l1_b", D), ("l2_b", D), ("l2_b2", 4 * D),
               ("router_b", 8), ("sg_b", 1), ("rank", 8)]:
    ROWS[_n] = (_at, _w)
    _at += _w
NROW = _at


def cut(area, at, *dims, rows=128):
    size = int(np.prod(dims))
    v = area[0:rows, at:at + size]
    if len(dims) == 1:
        return v
    names = "abcde"[:len(dims)]
    return v.rearrange(f"p ({' '.join(names)}) -> p {' '.join(names)}", **dict(zip(names, dims)))


class Chain:

    def __init__(self, eng, sem):
        self.eng, self.sem, self.n = eng, sem, 0

    def link(self, ins):
        self.n += 1
        ins.then_inc(self.sem, 1)
        self.eng.wait_ge(self.sem, self.n)


def vit_tower(nc, a, out, upto=99):
    ctx = ExitStack()
    with ctx:
        def sb(name, *shape):
            return ctx.enter_context(nc.sbuf_tensor(name, list(shape), F32))

        def sem(name):
            return ctx.enter_context(nc.semaphore(name))

        ps = ctx.enter_context(nc.psum_tensor("ps", [128, 8, 512], F32))
        h = sb("h", 128, NJ, D)
        xn = sb("xn", 128, NJ, D)
        xt_store = sb("xt_store", DH + 1, 2, 1 + NB * TP)
        ht = sb("ht", 128, 8, NB * TP)
        wa = sb("wa", 128, 5800)
        wb = sb("wb", 128, 7680)
        s = sb("s", 128, 22700)
        ident = sb("ident", 128, 128)
        rows = sb("rows", 128, NROW)
        vec = sb("vec", DH, 2, NVEC)
        clsrow = sb("clsrow", 128, D)
        live = sb("live", 128, 2)
        inb = sb("inb", 128, 6)
        b1 = sb("b1", 128, 24)
        wrouter = sb("wrouter", DH, 2, 17)
        cmask = sb("cmask", 128, T)
        eps = sb("eps", 128, 1)
        stats = sb("stats", 128, NJ, 6)
        mv = sb("mv", 128, NJ, 2)
        std = sb("std", 128, NJ)
        rstd = sb("rstd", 128, NJ)
        small = sb("small", 128, 640)

        xt = xt_store[0:DH, :, 1:1 + NB * TP]
        xt97 = xt_store[:, :, 1:1 + NB * TP]
        xtp = xt_store[0:DH, :, 0:NB * TP]

        def tok(view):
            return view.rearrange("p (b t) -> p b t", t=TP)

        def row(name):
            at, w = ROWS[name]
            return rows[:, at:at + w]

        def col(name, half):
            return vec[:, half, VEC[name]:VEC[name] + 1]

        S = {n: sem(n) for n in (
            "consts_loaded tok_loaded patches_loaded l0_loaded zeroed dve_chain act_chain pool_chain "
            "tok_mm tok_ev dw_done tok_mix f3_mm cls_ready "
            "ln_stat ln_std ln_xn ln_tp ln_xt_act ln_xt_dve proj_mm resid "
            "mix_ready kvr_mm kvr_ev wkv_arg wkv_exp z_ready ffn_mm ffn_ev out_done").split()}

        block = ctx.enter_context(nc.Block())
        dve_chain = Chain(nc.vector, S["dve_chain"])
        act_chain = Chain(nc.scalar, S["act_chain"])

        pl_w = cut(wa, 0, 6, D)
        pg_w1 = cut(wa, 1152, 2, 3, D)
        haar = cut(wa, 2304, 2, 256)
        pw = cut(wa, 2816, 6, 2, D, rows=DH)
        patches = cut(s, 0, 6, NB * NP)
        img_a = cut(s, 4704, 2, 9, 9 * NB, rows=DH)
        img_b = cut(s, 7296, 2, 9, 9 * NB, rows=DH)
        dwo = [cut(s, 9888 + 1568 * i, 2, NB * NP, rows=DH) for i in range(2)]
        loc = cut(s, 13024, 2, NB * NP, rows=DH)
        g2 = cut(s, 14592, 2, NB * NP, rows=DH)
        glob = cut(s, 16160, 2, NB * NP, rows=DH)
        weff = cut(s, 17728, 6, D)
        dw3 = cut(s, 18880, 2, NB * TP, rows=DH)
        RB = SIDE * NB
        YS = [(0, 4), (4, 3)]

        def window(img, half, dy=1, dx=1, y0=0, ny=SIDE):
            return img[:, half, dy + y0:dy + y0 + ny, dx * NB:dx * NB + RB]

        def spread(view):
            return view.rearrange("p (y c) -> p y c", c=RB)

        TOK = ["weff"] * 6 + ["loc"] * 4 + ["glob1"] * 4 + ["pl_pw"] * 4 + ["pg_pw"] * 4 + ["pg_w2"] * 4 + \
              ["f1"] * 4 + ["f2"] * 4
        FIRST = {n: TOK.index(n) for n in TOK}

        def tokenizer_pe(pe):
            t = 0

            def bank():
                if t >= 8:
                    pe.wait_ge(S["tok_ev"], t - 7)
                return ps[:, t % 8, :]
            pe.wait_ge(S["tok_loaded"], 16 * 4)
            for c in range(3):
                for half in range(2):
                    o = bank()
                    for k in range(2):
                        m = pe.matmul(o[:, 0:D], haar[:, k, half * 128:half * 128 + 128], pg_w1[:, k, c, :],
                                      start=k == 0, stop=k == 1)
                    m.then_inc(S["tok_mm"], 1)
                    t += 1
            pe.wait_ge(S["patches_loaded"], 32)
            for w, need in ((pl_w, 0), (weff, 6)):
                if need:
                    pe.wait_ge(S["tok_ev"], need)
                for oh in range(2):
                    for nh in range(2):
                        o = bank()
                        y0, ny = YS[nh]
                        for k in range(6):
                            m = pe.matmul(o[0:DH, 0:ny * RB], w[:, k, oh * DH:oh * DH + DH],
                                          patches[:, k, y0 * RB:(y0 + ny) * RB], start=k == 0, stop=k == 5)
                        m.then_inc(S["tok_mm"], 1)
                        t += 1
            for i, (src, dws, evs) in enumerate([(dwo[0], 1, 0), (dwo[1], 2, 0), (g2, 2, FIRST["pg_w2"]),
                                                 (dwo[0], 3, 0), (dwo[1], 4, 0)]):
                pe.wait_ge(S["dw_done"], dws)
                if evs:
                    pe.wait_ge(S["tok_ev"], evs)
                for oh in range(2):
                    for nh in range(2):
                        o = bank()
                        y0, ny = YS[nh]
                        for k in range(2):
                            m = pe.matmul(o[0:DH, 0:ny * RB], pw[:, i, k, oh * DH:oh * DH + DH],
                                          src[:, k, y0 * RB:(y0 + ny) * RB], start=k == 0, stop=k == 1)
                        m.then_inc(S["tok_mm"], 1)
                        t += 1
            pe.wait_ge(S["tok_mix"], 2)
            pe.wait_ge(S["tok_ev"], len(TOK))
            for j in range(NJ):
                for k in range(2):
                    m = pe.matmul(ps[:, j, 0:D], dw3[:, k, 2 * TP * j:2 * TP * j + 128], pw[:, 5, k, :],
                                  start=k == 0, stop=k == 1)
                m.then_inc(S["f3_mm"], 1)

        def tokenizer_act(act):
            t = 0
            act.wait_ge(S["consts_loaded"], 16 * NCONST)
            act_chain.link(act.activation(small[0:DH, 0:2], vec[:, :, VEC["alpha"]], ACT.Tanh))
            for name, fn, bias, dst in [("weff", ACT.Copy, None, None), ("loc", ACT.Gelu, "pl_b", img_a),
                                        ("glob1", ACT.Gelu, "pg_b1", img_b), ("pl_pw", ACT.Identity, "pl_pwb", loc),
                                        ("pg_pw", ACT.Gelu, "pg_pwb", g2), ("pg_w2", ACT.Identity, "pg_b2", glob),
                                        ("f1", ACT.Relu, "f1_pwb", img_b), ("f2", ACT.Relu, "f2_pwb", g2)]:
                if name == "loc":
                    act.wait_ge(S["zeroed"], 3)
                if name == "f1":
                    act.wait_ge(S["dw_done"], 3)
                for i in range(TOK.count(name)):
                    act.wait_ge(S["tok_mm"], t + 1)
                    o = ps[:, t % 8, :]
                    if name == "weff":
                        ins = act.activation(weff[:, i, :], o[:, 0:D], fn)
                    else:
                        oh, nh = i // 2, i % 2
                        y0, ny = YS[nh]
                        src = o[0:DH, 0:ny * RB]
                        if dst is img_a or dst is img_b:
                            ins = act.activation(window(dst, oh, y0=y0, ny=ny), spread(src), fn, bias=col(bias, oh))
                        else:
                            ins = act.activation(dst[:, oh, y0 * RB:(y0 + ny) * RB], src, fn, bias=col(bias, oh))
                    ins.then_inc(S["tok_ev"], 1)
                    t += 1

        def tokenizer_dve(v):
            link = dve_chain.link
            v.wait_ge(S["consts_loaded"], 16 * NCONST)
            v.wait_ge(S["zeroed"], 3)

            def depthwise(img, taps, dst):
                for tap in range(9):
                    dy, dx = divmod(tap, 3)
                    for half in range(2):
                        src = window(img, half, dy, dx)
                        w = vec[:, half, TAPS[taps] + tap:TAPS[taps] + tap + 1]
                        if tap == 0:
                            ins = v.tensor_scalar(dst[half], src, w, None, ALU.mult)
                        else:
                            ins = v.scalar_tensor_tensor(dst[half], src, w, dst[half], ALU.mult, ALU.add)
                        if half == 0:
                            dve_chain.n += 1
                            ins.then_inc(S["dve_chain"], 1)
                        elif tap < 8:
                            link(ins)
                        else:
                            ins.then_inc(S["dw_done"], 1)

            def flat(d):
                return [spread(d[:, half, :]) for half in range(2)]
            v.wait_ge(S["tok_ev"], FIRST["glob1"])
            depthwise(img_a, "pl", flat(dwo[0]))
            v.wait_ge(S["tok_ev"], FIRST["pl_pw"])
            depthwise(img_b, "pg", flat(dwo[1]))
            gate, keep = small[0:DH, 2:4], small[0:DH, 4:6]
            v.wait_ge(S["act_chain"], 1)
            link(v.tensor_scalar(gate, small[0:DH, 0:2], 1.0, 0.5, ALU.add, ALU.mult))
            link(v.tensor_scalar(keep, gate, -1.0, 1.0, ALU.mult, ALU.add))
            v.wait_ge(S["tok_ev"], FIRST["f1"])
            for half in range(2):
                link(v.tensor_scalar(glob[:, half, :], glob[:, half, :], gate[:, half:half + 1], None, ALU.mult))
                link(v.scalar_tensor_tensor(window(img_a, half), spread(loc[:, half, :]), keep[:, half:half + 1],
                                            spread(glob[:, half, :]), ALU.mult, ALU.add))
            depthwise(img_a, "f1", flat(dwo[0]))
            v.wait_ge(S["tok_ev"], FIRST["f2"])
            depthwise(img_b, "f2", flat(dwo[1]))
            v.wait_ge(S["tok_ev"], len(TOK))
            for half in range(2):
                link(v.tensor_tensor(window(img_a, half), spread(loc[:, half, :]), spread(g2[:, half, :]),
                                     ALU.add))
            depthwise(img_a, "f3", flat(dwo[0]))
            v.wait_ge(S["dw_done"], 5)
            for half in range(2):
                v.tensor_copy(tok(dw3[:, half, :])[:, :, 2:2 + NP],
                              dwo[0][:, half, :].rearrange("p (t b) -> p b t", b=NB)).then_inc(S["tok_mix"], 1)
            for j in range(NJ):
                v.wait_ge(S["f3_mm"], j + 1)
                ins = v.tensor_tensor(xn[:, j, :], ps[:, j, 0:D], row("f3_pwb"), ALU.add)
            link(ins)
            normalize_dve(v, xn, -1)
            wide = [128, NJ, D]
            link(v.tensor_tensor(xn[:, :, :], xn[:, :, :], row("ln_g").unsqueeze(1).to_broadcast(wide), ALU.mult))
            link(v.tensor_tensor(xn[:, :, :], xn[:, :, :], row("ln_b").unsqueeze(1).to_broadcast(wide), ALU.add))
            link(v.scalar_tensor_tensor(h[:, :, :], xn[:, :, :], live[:, 0:1],
                                        clsrow[:, :].unsqueeze(1).to_broadcast(wide), ALU.mult, ALU.add))

        def normalize_dve(v, src, n):
            link = dve_chain.link
            for j in range(NJ):
                ins = v.bn_stats(stats[:, j, :], src[:, j, :])
            link(ins)
            for j in range(NJ):
                ins = v.bn_aggr(mv[:, j, :], stats[:, j, :])
            ins.then_inc(S["ln_stat"], 1)
            v.wait_ge(S["ln_std"], n + 2)
            link(v.reciprocal(rstd[:, :], std[:, :]))
            link(v.tensor_scalar(rstd[:, :], rstd[:, :], live[:, 1:2], None, ALU.mult))
            for j in range(NJ):
                ins = v.tensor_scalar(xn[:, j, :], src[:, j, :], mv[:, j, 0:1], rstd[:, j:j + 1],
                                      ALU.subtract, ALU.mult)
                ins.then_inc(S["ln_xn"], 1)
            v.wait_ge(S["ln_xn"], NJ * (n + 2))

        def normalize_act(act, n):
            act.wait_ge(S["ln_stat"], n + 2)
            act.activation(std[:, :], mv[:, :, 1], ACT.Sqrt, bias=eps[:, 0:1]).then_inc(S["ln_std"], 1)

        def layernorm_dve(v, n):
            normalize_dve(v, h, n)
            for q in range(2):
                v.wait_ge(S["ln_tp"], 4 * n + 3 + q)
                v.tensor_copy(xt[:, 1, 512 * q:512 * q + 512], ps[0:DH, 2 + q, :]).then_inc(S["ln_xt_dve"], 1)
            v.wait_ge(S["ln_xt_dve"], 2 * (n + 1))

        def layernorm_act(act, n):
            normalize_act(act, n)
            for q in range(2):
                act.wait_ge(S["ln_tp"], 4 * n + 1 + q)
                act.activation(xt[:, 0, 512 * q:512 * q + 512], ps[0:DH, q, :], ACT.Copy)\
                    .then_inc(S["ln_xt_act"], 1)

        def layernorm_pe(pe, n):
            if n == 0:
                pe.wait_ge(S["consts_loaded"], 16 * NCONST)
            for half in range(2):
                for q in range(2):
                    for i in range(4):
                        j = 4 * q + i
                        pe.wait_ge(S["ln_xn"], NJ * (n + 1) + j + 1)
                        m = pe.transpose(ps[0:DH, 2 * half + q, 128 * i:128 * i + 128],
                                         xn[:, j, half * DH:half * DH + DH], ident[:, :])
                    m.then_inc(S["ln_tp"], 1)
            xt_ready(pe, n)

        def xt_ready(eng, n):
            eng.wait_ge(S["ln_xt_act"], 2 * (n + 1))
            eng.wait_ge(S["ln_xt_dve"], 2 * (n + 1))

        PROJECTIONS = [0, 1, 2, 4, 6]

        def project_pe(pe, n, chunks):
            for j in range(NJ):
                if j >= 2:
                    pe.wait_ge(S["resid"], NJ * n + j - 1)
                for c, (lhs, w) in enumerate(chunks):
                    m = pe.matmul(ps[:, 6 + j % 2, 0:D], lhs[:, 128 * j:128 * j + 128], w,
                                  start=c == 0, stop=c == len(chunks) - 1)
                m.then_inc(S["proj_mm"], 1)

        def residual_dve(v, n, bias=None):
            for j in range(NJ):
                v.wait_ge(S["proj_mm"], NJ * PROJECTIONS.index(n) + j + 1)
                if bias is not None and j == 0:
                    dve_chain.link(v.tensor_tensor(h[:, :, :], h[:, :, :],
                                                   row(bias).unsqueeze(1).to_broadcast([128, NJ, D]), ALU.add))
                v.tensor_tensor(h[:, j, :], h[:, j, :], ps[:, 6 + j % 2, 0:D], ALU.add).then_inc(S["resid"], 1)
            v.wait_ge(S["resid"], NJ * (n + 1))

        w_kvro = cut(wb, 0, 4, 2, D, rows=DH)
        w_in = cut(wb, 1536, 2, 768, rows=DH)
        w_out = cut(wb, 3072, 6, D)
        N51 = HALF * T
        SL = T + 1
        mixed = cut(s, 0, 3, 2, NB * T, rows=DH)
        seq = [cut(s, 4896 + 2 * NB * SL * i, 2, NB, SL, rows=DH) for i in range(10)]
        kk, vv, sr, wst, omax, ea, eb, e1, e2, bv = seq
        pst, qst = [cut(s, 2 * NB * SL * i, 2, NB, SL, rows=DH) for i in range(2)]
        z = ht[0:DH, 0:2, :]

        def line(view):
            return view.rearrange("p a b c -> p (a b c)")

        def rwkv_pe(pe):
            for m3 in range(3):
                for oh in range(2):
                    for nh in range(2):
                        i = 4 * m3 + 2 * oh + nh
                        if i == 0:
                            pe.wait_ge(S["l0_loaded"], 48)
                        pe.wait_ge(S["mix_ready"], m3 + 1)
                        if i >= 4:
                            pe.wait_ge(S["kvr_ev"], i - 3)
                        for k in range(2):
                            m = pe.matmul(ps[0:DH, i % 4, 0:N51], w_kvro[:, m3, k, oh * DH:oh * DH + DH],
                                          mixed[:, m3, k, nh * N51:nh * N51 + N51], start=k == 0, stop=k == 1)
                        m.then_inc(S["kvr_mm"], 1)
            pe.wait_ge(S["z_ready"], 1)
            project_pe(pe, 0, [(z[:, k, :], w_kvro[:, 3, k, :]) for k in range(2)])

        def rwkv_act(act):
            for m3, dst in enumerate((kk, vv, sr)):
                for oh in range(2):
                    for nh in range(2):
                        i = 4 * m3 + 2 * oh + nh
                        act.wait_ge(S["kvr_mm"], i + 1)
                        act.activation(dst[:, oh, nh * HALF:nh * HALF + HALF, 1:SL],
                                       ps[0:DH, i % 4, 0:N51].rearrange("p (b t) -> p b t", t=T),
                                       ACT.Sigmoid if m3 == 2 else ACT.Copy).then_inc(S["kvr_ev"], 1)
            for i, x in enumerate((ea, eb, e1, e2)):
                act.wait_ge(S["wkv_arg"], i + 1)
                for oh in range(2):
                    ins = act.activation(x[:, oh, :, 1:SL], x[:, oh, :, 1:SL], ACT.Exp)
                ins.then_inc(S["wkv_exp"], 1)

        def rwkv_dve(v):
            link = dve_chain.link
            xt_ready(v, 0)
            for half in range(2):
                for i, m in enumerate(("mk", "mv", "mr")):
                    o = small[0:DH, 8 + 3 * half + i:9 + 3 * half + i]
                    ins = v.tensor_scalar(o, col(m, half), -1.0, 1.0, ALU.mult, ALU.add)
            link(ins)
            for i, m in enumerate(("mk", "mv", "mr")):
                for half in range(2):
                    o = mixed[:, i, half, :].rearrange("p (b t) -> p b t", t=T)
                    link(v.tensor_scalar(o, tok(xt[:, half, :])[:, :, 0:T], col(m, half), None, ALU.mult))
                    ins = v.scalar_tensor_tensor(o, tok(xtp[:, half, :])[:, :, 0:T],
                                                 small[0:DH, 8 + 3 * half + i:9 + 3 * half + i], o,
                                                 ALU.mult, ALU.add)
                    if half == 0:
                        link(ins)
                    else:
                        ins.then_inc(S["mix_ready"], 1)
            v.memset(kk[:, :, :, 0:1], NEG)
            v.memset(wst[:, :, :, 0:1], NEG)
            for x in (ea, eb, bv):
                v.memset(x[:, :, :, 0:1], 0.0)
            for oh in range(2):
                ins = v.tensor_scalar(wst[:, oh, :, 1:SL], tok(xt[:, oh, :])[:, :, 0:T], 0.0, col("decay", oh),
                                      ALU.mult, ALU.add)
            link(ins)
            v.wait_ge(S["kvr_ev"], 4)
            link(v.tensor_tensor_scan(line(omax), line(wst), line(kk), 0.0, ALU.add, ALU.max))
            o0, o1 = omax[:, :, :, 0:T], omax[:, :, :, 1:SL]
            k1, v1 = kk[:, :, :, 1:SL], vv[:, :, :, 1:SL]
            for oh in range(2):
                ins = v.scalar_tensor_tensor(ea[:, oh, :, 1:SL], o0[:, oh], col("decay", oh), o1[:, oh],
                                             ALU.add, ALU.subtract)
            ins.then_inc(S["wkv_arg"], 1)
            for oh in range(2):
                ins = v.tensor_tensor(eb[:, oh, :, 1:SL], k1[:, oh], o1[:, oh], ALU.subtract)
            ins.then_inc(S["wkv_arg"], 1)
            no = wst
            for oh in range(2):
                ins = v.scalar_tensor_tensor(no[:, oh, :, 1:SL], k1[:, oh], col("first", oh), o0[:, oh],
                                             ALU.add, ALU.max)
            link(ins)
            for oh in range(2):
                ins = v.tensor_tensor(e1[:, oh, :, 1:SL], o0[:, oh], no[:, oh, :, 1:SL], ALU.subtract)
            ins.then_inc(S["wkv_arg"], 1)
            for oh in range(2):
                ins = v.scalar_tensor_tensor(e2[:, oh, :, 1:SL], k1[:, oh], col("first", oh), no[:, oh, :, 1:SL],
                                             ALU.add, ALU.subtract)
            ins.then_inc(S["wkv_arg"], 1)
            v.wait_ge(S["kvr_ev"], 12)
            v.wait_ge(S["wkv_exp"], 2)
            for oh in range(2):
                ins = v.tensor_tensor(bv[:, oh, :, 1:SL], eb[:, oh, :, 1:SL], v1[:, oh], ALU.mult)
            link(ins)
            v.tensor_tensor_scan(line(pst), line(ea), line(bv), 0.0, ALU.mult, ALU.add)
            link(v.tensor_tensor_scan(line(qst), line(ea), line(eb), 0.0, ALU.mult, ALU.add))
            v.wait_ge(S["wkv_exp"], 4)
            A, B = e1[:, :, :, 1:SL], e2[:, :, :, 1:SL]
            num, den = ea[:, :, :, 1:SL], eb[:, :, :, 1:SL]
            for oh in range(2):
                v.tensor_tensor(num[:, oh], A[:, oh], pst[:, oh, :, 0:T], ALU.mult)
                v.tensor_tensor(den[:, oh], A[:, oh], qst[:, oh, :, 0:T], ALU.mult)
                link(v.tensor_tensor(v1[:, oh], v1[:, oh], B[:, oh], ALU.mult))
                v.tensor_tensor(num[:, oh], num[:, oh], v1[:, oh], ALU.add)
                link(v.tensor_tensor(den[:, oh], den[:, oh], B[:, oh], ALU.add))
                v.tensor_tensor(num[:, oh], num[:, oh], sr[:, oh, :, 1:SL], ALU.mult)
                link(v.reciprocal(den[:, oh], den[:, oh]))
                ins = v.tensor_tensor(tok(z[:, oh, :])[:, :, 0:T], num[:, oh], den[:, oh], ALU.mult)
            ins.then_inc(S["z_ready"], 1)
            residual_dve(v, 0)

        def ffn0_pe(pe):
            for m6 in range(6):
                for nh in range(2):
                    i = 2 * m6 + nh
                    if i >= 4:
                        pe.wait_ge(S["ffn_ev"], i - 3)
                    for k in range(2):
                        m = pe.matmul(ps[:, i % 4, 0:N51], w_in[:, k, 128 * m6:128 * m6 + 128],
                                      tok(xt[:, k, :])[:, nh * HALF:nh * HALF + HALF, 0:T],
                                      start=k == 0, stop=k == 1)
                    m.then_inc(S["ffn_mm"], 1)
            pe.wait_ge(S["ffn_ev"], 12)
            project_pe(pe, 1, [(ht[:, c, :], w_out[:, c, :]) for c in range(6)])

        def ffn0_act(act):
            for i in range(12):
                act.wait_ge(S["ffn_mm"], i + 1)
                m6, nh = divmod(i, 2)
                act.activation(tok(ht[:, m6, :])[:, nh * HALF:nh * HALF + HALF, 0:T],
                               ps[:, i % 4, 0:N51].rearrange("p (b t) -> p b t", t=T), ACT.Gelu,
                               bias=inb[:, m6:m6 + 1]).then_inc(S["ffn_ev"], 1)

        class Attn:
            def __init__(self, n, tag, groups, per, rows, nq, nk, nch, vw, units, scale, weights_at, wo):
                self.n, self.tag, self.groups, self.per, self.rows = n, tag, groups, per, rows
                self.nq, self.nk, self.nch, self.vw, self.units, self.scale = nq, nk, nch, vw, units, scale
                self.stride = 128 // groups
                at = 0
                self.w_q = cut(wa, at, 2, nq * nch, 128, rows=DH)
                at += 2 * nq * nch * 128
                self.w_k = cut(wa, at, 2, nk * nch, 128, rows=DH)
                at += 2 * nk * nch * 128
                self.w_v = cut(wa, at, 2, 2, vw, rows=DH)
                at += 4 * vw
                self.w_o = cut(wa, at, wo[1], D, rows=wo[0])
                at = 0
                self.q = cut(s, at, nq * nch, NB * TP)
                at += nq * nch * NB * TP
                self.k = cut(s, at, nk, nch, NB * T)
                at += nk * nch * NB * T
                self.v = cut(s, at, NB, vw)
                at += NB * vw
                self.p = [cut(s, at + i * units * 128, units, 2, TP) for i in range(2)]
                self.p_all = cut(s, at, 2 * units * 128)
                at += 2 * units * 128
                self.pt = cut(s, at, units, 128)
                at += units * 128
                self.o = [cut(s, at + i * D, D) for i in range(2)]
                assert at + 2 * D <= 22700
                self.sems = {name: sem(f"{tag}_{name}") for name in
                             "loaded qk_mm qk_ev v_mm v_ev p_zero s_mm arg exp p_ready ring_mm ring_ev pv_mm o_ev"
                             .split()}

        def attn_pe(pe, c):
            m = None
            pe.wait_ge(c.sems["loaded"], 16 * 4)
            for i in range((c.nq + c.nk) * c.nch):
                for nh in range(2):
                    t = 2 * i + nh
                    if t >= 4:
                        pe.wait_ge(c.sems["qk_ev"], t - 3)
                    isq = i < c.nq * c.nch
                    for k in range(2):
                        if isq:
                            m = pe.matmul(ps[:, t % 4, 0:512], c.w_q[:, k, i, :], xt[:, k, 512 * nh:512 * nh + 512],
                                          start=k == 0, stop=k == 1)
                        else:
                            m = pe.matmul(ps[:, t % 4, 0:N51], c.w_k[:, k, i - c.nq * c.nch, :],
                                          tok(xt[:, k, :])[:, nh * HALF:nh * HALF + HALF, 0:T],
                                          start=k == 0, stop=k == 1)
                    m.then_inc(c.sems["qk_mm"], 1)
            for j in range(NJ):
                if j >= 2:
                    pe.wait_ge(c.sems["v_ev"], j - 1)
                for par in range(2):
                    for k in range(2):
                        m = pe.matmul(ps[:, 4 + 2 * (j % 2) + par, 0:c.vw], xt[:, k, 128 * j:128 * j + 128],
                                      c.w_v[:, k, par, :], start=k == 0, stop=k == 1)
                m.then_inc(c.sems["v_mm"], 1)

            def scores(j):
                if j >= 1:
                    pe.wait_ge(c.sems["arg"], j)
                for g in range(c.groups):
                    at = slice(c.stride * g, c.stride * g + c.rows)
                    for e in range(2):
                        b = 2 * j + e
                        for ch in range(c.nch):
                            o = ps[64 * e:64 * e + 64, g, :]
                            ks = c.k[at, :, ch, T * b:T * b + T]
                            if c.nq == 2:
                                q4 = c.q[at, ch, TP * b:TP * b + TP]
                                q5 = c.q[at, c.nch + ch, TP * b:TP * b + TP]
                                pe.matmul(o[:, 255 * ch:255 * ch + 102], q4, ks[:, 0:2, :], start=True, stop=True)
                                m = pe.matmul(o[:, 255 * ch + 102:255 * ch + 255], q5, ks, start=True, stop=True)
                            else:
                                m = pe.matmul(o[:, T * ch:T * ch + T], c.q[at, ch, TP * b:TP * b + TP], ks[:, 0, :],
                                              start=True, stop=True)
                m.then_inc(c.sems["s_mm"], 1)

            r = 0

            def bank():
                nonlocal r
                if r >= 2:
                    pe.wait_ge(c.sems["ring_ev"], r - 1)
                r += 1
                return ps[:, 4 + (r - 1) % 2, :]

            def turn_out(j):
                pe.wait_ge(c.sems["o_ev"], j + 1)
                o = bank()
                for k in range(2):
                    m = pe.transpose(o[0:DH, 128 * k:128 * k + 128], c.o[j % 2][:, k * DH:k * DH + DH], ident[:, :])
                m.then_inc(c.sems["ring_mm"], 1)

            pe.wait_ge(c.sems["qk_ev"], 2 * (c.nq + c.nk) * c.nch)
            pe.wait_ge(c.sems["v_ev"], NJ)
            scores(0)
            for j in range(NJ):
                if j + 1 < NJ:
                    scores(j + 1)
                pe.wait_ge(c.sems["exp"] if c.nq == 2 else c.sems["p_ready"], j + 1)
                for u in range(0, c.units, 4):
                    o = bank()
                    for i in range(u, min(u + 4, c.units)):
                        m = pe.transpose(o[:, 128 * (i - u):128 * (i - u) + 128],
                                         c.p[j % 2][:, i, :, :].rearrange("p s t -> p (s t)"), ident[:, :])
                    m.then_inc(c.sems["ring_mm"], 1)
                if j >= 1 and c.tag != "a2":
                    turn_out(j - 1)
                pe.wait_ge(c.sems["ring_ev"], r - (1 if j >= 1 and c.tag != "a2" else 0))
                if j >= 1:
                    pe.wait_ge(c.sems["o_ev"], j)
                for u in range(c.units):
                    for e in range(2):
                        b = 2 * j + e
                        if c.tag == "a1":
                            m = pe.matmul(ps[64 * e:64 * e + 64, 6, 8 * u:8 * u + 8], c.pt[:, u, 64 * e:64 * e + 64],
                                          c.v[:, b, 8 * u:8 * u + 8], start=True, stop=True)
                        else:
                            for par in range(2):
                                at = slice(64 * par, 64 * par + 64)
                                slot = 2 * u + par
                                if c.tag == "a2":
                                    g, ch = divmod(slot, c.per)
                                    m = pe.matmul(ps[64 * g:64 * g + 64, 6 + par,
                                                     128 * (ch // 2) + 64 * e:128 * (ch // 2) + 64 * e + 64],
                                                  c.v[at, b, 64 * u:64 * u + 64], c.pt[at, u, 64 * e:64 * e + 64],
                                                  start=True, stop=True)
                                else:
                                    m = pe.matmul(ps[64 * e:64 * e + 64, 6 + par, 16 * u:16 * u + 16],
                                                  c.pt[at, u, 64 * e:64 * e + 64], c.v[at, b, 16 * u:16 * u + 16],
                                                  start=True, stop=True)
                m.then_inc(c.sems["pv_mm"], 1)
            if c.tag != "a2":
                turn_out(NJ - 1)
                pe.wait_ge(c.sems["ring_ev"], r)
                project_pe(pe, c.n, [(ht[0:DH, k, :], c.w_o[:, k, :]) for k in range(2)])
            else:
                pe.wait_ge(c.sems["o_ev"], NJ)
                project_pe(pe, c.n, [(ht[:, k, :], c.w_o[:, k, :]) for k in range(6)])

        def attn_act(act, c):
            for i in range((c.nq + c.nk) * c.nch):
                for nh in range(2):
                    t = 2 * i + nh
                    act.wait_ge(c.sems["qk_mm"], t + 1)
                    if i < c.nq * c.nch:
                        ins = act.activation(c.q[:, i, 512 * nh:512 * nh + 512], ps[:, t % 4, :], ACT.Copy)
                    else:
                        kt, ch = divmod(i - c.nq * c.nch, c.nch)
                        ins = act.activation(c.k[:, kt, ch, N51 * nh:N51 * nh + N51], ps[:, t % 4, 0:N51], ACT.Copy)
                    ins.then_inc(c.sems["qk_ev"], 1)
            r = 0

            def turn_out(j):
                act.wait_ge(c.sems["ring_mm"], r + 1)
                act.activation(ht[0:DH, 0:2, 128 * j:128 * j + 128],
                               ps[0:DH, 4 + r % 2, 0:256].rearrange("p (k t) -> p k t", k=2), ACT.Copy)\
                    .then_inc(c.sems["ring_ev"], 1)

            for j in range(NJ):
                act.wait_ge(c.sems["arg"], j + 1)
                x = c.p[j % 2].rearrange("p u s t -> p (u s) t")[:, :, 0:T]
                act.activation(x, x, ACT.Exp, scale=c.scale).then_inc(c.sems["exp"], 1)
                for u in range(0, c.units, 4):
                    nu = min(4, c.units - u)
                    act.wait_ge(c.sems["ring_mm"], r + 1)
                    if u == 0 and j >= 1:
                        act.wait_ge(c.sems["pv_mm"], j)
                    act.activation(c.pt[:, u:u + nu, :].rearrange("p u t -> p (u t)"), ps[:, 4 + r % 2, 0:128 * nu],
                                   ACT.Copy).then_inc(c.sems["ring_ev"], 1)
                    r += 1
                if j >= 1 and c.tag != "a2":
                    turn_out(j - 1)
                    r += 1
            if c.tag != "a2":
                turn_out(NJ - 1)

        def attn_dve(v, c):
            link = dve_chain.link
            for j in range(NJ):
                v.wait_ge(c.sems["v_mm"], j + 1)
                for e in range(2):
                    for par in range(2):
                        ins = v.tensor_copy(c.v[64 * par:64 * par + 64, 2 * j + e, :],
                                            ps[64 * e:64 * e + 64, 4 + 2 * (j % 2) + par, 0:c.vw])
                ins.then_inc(c.sems["v_ev"], 1)
            v.wait_ge(c.sems["p_zero"], 1)
            bmax, mx = small[:, 32:72], small[:, 72:96]
            total = [small[:, 96 + 24 * i:120 + 24 * i] for i in range(2)]
            nmx = 24 if c.tag == "a1" else 12

            def out_dve(j):
                v.wait_ge(c.sems["pv_mm"], j + 1)
                if c.tag == "a1":
                    v.tensor_tensor(c.o[j % 2].rearrange("p (u d) -> p u d", d=8),
                                    ps[:, 6, 0:D].rearrange("p (u d) -> p u d", d=8),
                                    total[j % 2].unsqueeze(2).to_broadcast([128, 24, 8]), ALU.mult)\
                        .then_inc(c.sems["o_ev"], 1)
                elif c.tag == "a2":
                    for par in range(2):
                        ins = v.tensor_copy(ht[:, par:6:2, 128 * j:128 * j + 128],
                                            ps[:, 6 + par, 0:384].rearrange("p (u t) -> p u t", u=3))
                    ins.then_inc(c.sems["o_ev"], 1)
                else:
                    for par in range(2):
                        ins = v.tensor_copy(c.o[j % 2][:, 96 * par:96 * par + 96], ps[:, 6 + par, 0:96])
                    ins.then_inc(c.sems["o_ev"], 1)

            for j in range(NJ):
                v.wait_ge(c.sems["s_mm"], j + 1)
                if j >= 2:
                    v.wait_ge(c.sems["pv_mm"], j - 1)
                p = c.p[j % 2]
                if c.tag == "a1":
                    for g in range(4):
                        ins = v.tensor_reduce(bmax[:, 10 * g:10 * g + 10],
                                              ps[:, g, 0:510].rearrange("p (c t) -> p c t", t=T), AX.X, ALU.max)
                    link(ins)
                    bm = bmax.rearrange("p (g c k) -> p c g k", g=4, c=2)
                    for a3, (k0, k1) in enumerate(((0, 1), (2, 4), (3, 4))):
                        ins = v.tensor_tensor(mx[:, 8 * a3:8 * a3 + 8].rearrange("p (c g) -> p c g", c=2),
                                              bm[:, :, :, k0], bm[:, :, :, k1], ALU.max)
                    link(ins)
                    for g in range(4):
                        sv = ps[:, g, 0:510].rearrange("p (c k t) -> p c k t", c=2, k=5)
                        for a3, ks in enumerate((slice(0, 2), slice(2, 5, 2), slice(3, 5))):
                            top = mx[:, 8 * a3 + g:8 * a3 + 8:4].unsqueeze(2).unsqueeze(3).to_broadcast([128, 2, 2, T])
                            ins = v.tensor_tensor(p[:, 8 * a3 + g:8 * a3 + 8:4, :, 0:T], sv[:, :, ks, :], top,
                                                  ALU.subtract)
                    ins.then_inc(c.sems["arg"], 1)
                else:
                    ph = p.rearrange("p u s t -> p (u s) t")[:, :, 0:T]
                    per = c.per
                    for g in range(c.groups):
                        sv = ps[:, g, 0:per * T].rearrange("p (c t) -> p c t", t=T)
                        if c.tag == "a2":
                            ins = v.tensor_reduce(mx[:, per * g:per * g + per], sv, AX.X, ALU.max)
                        else:
                            ins = v.tensor_tensor(ph[:, per * g:per * g + per, :], sv,
                                                  cmask[:, :].unsqueeze(1).to_broadcast([128, per, T]), ALU.add)
                    link(ins)
                    top = mx[:, 0:12].unsqueeze(2).to_broadcast([128, 12, T])
                    if c.tag == "a2":
                        for g in range(c.groups):
                            sv = ps[:, g, 0:per * T].rearrange("p (c t) -> p c t", t=T)
                            ins = v.tensor_tensor(ph[:, per * g:per * g + per, :], sv,
                                                  top[:, per * g:per * g + per, :], ALU.subtract)
                    else:
                        link(v.tensor_reduce(mx[:, 0:12], ph, AX.X, ALU.max))
                        ins = v.tensor_tensor(ph, ph, top, ALU.subtract)
                    ins.then_inc(c.sems["arg"], 1)
                if j >= 1:
                    out_dve(j - 1)
                v.wait_ge(c.sems["exp"], j + 1)
                tot = total[j % 2][:, 0:nmx]
                if c.tag == "a1":
                    link(v.tensor_reduce(tot, p[:, :, :, 0:T], AX.XY, ALU.add))
                    link(v.reciprocal(tot, tot))
                else:
                    link(v.tensor_reduce(tot, ph, AX.X, ALU.add))
                    link(v.reciprocal(tot, tot))
                    v.tensor_tensor(ph, ph, tot.unsqueeze(2).to_broadcast([128, 12, T]), ALU.mult)\
                        .then_inc(c.sems["p_ready"], 1)
            out_dve(NJ - 1)
            residual_dve(v, c.n, {"a1": "l1_b", "a2": "l2_b", "a3": None}[c.tag])

        att1 = Attn(2, "a1", 4, 2, 8, 2, 3, 2, 192, 24, 24.0 ** -0.5, 0, (DH, 2))
        att2 = Attn(4, "a2", 2, 6, 64, 1, 1, 6, 384, 6, 0.125, 0, (128, 6))
        att3 = Attn(6, "a3", 4, 3, 16, 1, 1, 3, 96, 6, 4.0, 0, (DH, 2))

        class Moe:
            def __init__(self, n, tag, col0, nr, experts):
                self.n, self.tag, self.col0, self.nr, self.experts = n, tag, col0, nr, experts
                self.w = []
                for rows_, nc_, at, _ in experts:
                    hid = rows_ * nc_
                    self.w.append((cut(wb, at, 2, hid, rows=DH), cut(wb, at + 2 * hid, 2, hid, rows=DH),
                                   cut(wb, at + 4 * hid, nc_, D, rows=rows_)))
                self.items = [2 * nc_ * i for i, (_, nc_, _, _) in enumerate(experts)]
                t = 0
                self.first = []
                for _, nc_, _, _ in experts:
                    self.first.append(t)
                    t += 2 * nc_
                self.first.append(t)
                self.lg = cut(s, 0, NJ, nr)
                self.pr = cut(s, 80, NJ, 8)
                self.one = cut(s, 144, NJ, 8)
                self.two = cut(s, 208, NJ, 8)
                self.gates = cut(s, 272, NJ, 9)
                self.top = cut(s, 352, 4, NJ)
                self.acc = cut(s, 400, NJ, D)
                self.accb = cut(s, 2000, NJ * D // 2).bitcast(BF16).rearrange("p (j d) -> p j d", d=D)
                self.sil = [cut(s, 2800 + N51 * i, N51) for i in range(2)]
                self.sems = {name: sem(f"{tag}_{name}") for name in
                             "loaded0 loaded1 loaded_shared r_mm r_arg r_exp hid_mm silu hid_ev down_mm acc_ev".split()}

        def moe_pe(pe, c):
            for j in range(NJ):
                for k in range(2):
                    m = pe.matmul(ps[:, 7, c.nr * j:c.nr * j + c.nr], xt[:, k, 128 * j:128 * j + 128],
                                  wrouter[:, k, c.col0:c.col0 + c.nr], start=k == 0, stop=k == 1)
            m.then_inc(c.sems["r_mm"], 1)

            def hidden(i):
                rows_, nc_, _, _ = c.experts[i]
                if i == 8:
                    pe.wait_ge(c.sems["loaded_shared"], 48)
                else:
                    pe.wait_ge(c.sems[f"loaded{i % 2}"], 48 * (i // 2 + 1))
                for m4 in range(nc_):
                    for nh in range(2):
                        t = c.first[i] + 2 * m4 + nh
                        if t >= 2:
                            pe.wait_ge(c.sems["hid_ev"], t - 1)
                        for w in range(2):
                            for k in range(2):
                                m = pe.matmul(ps[0:rows_, 2 * (t % 2) + w, 0:N51],
                                              c.w[i][w][:, k, rows_ * m4:rows_ * m4 + rows_],
                                              tok(xt[:, k, :])[:, nh * HALF:nh * HALF + HALF, 0:T],
                                              start=k == 0, stop=k == 1)
                        m.then_inc(c.sems["hid_mm"], 1)

            hidden(0)
            for i, (rows_, nc_, _, slots_) in enumerate(c.experts):
                if i + 1 < len(c.experts):
                    hidden(i + 1)
                pe.wait_ge(c.sems["hid_ev"], c.first[i + 1])
                for j in range(NJ):
                    jj = NJ * i + j
                    if jj >= 3:
                        pe.wait_ge(c.sems["acc_ev"], jj - 2)
                    for m4 in range(nc_):
                        m = pe.matmul(ps[:, 4 + jj % 3, 0:D], ht[0:rows_, slots_[m4], 128 * j:128 * j + 128],
                                      c.w[i][2][:, m4, :], start=m4 == 0, stop=m4 == nc_ - 1)
                    m.then_inc(c.sems["down_mm"], 1)

        def moe_act(act, c):
            act.wait_ge(c.sems["r_arg"], 1)
            act.activation(c.lg[:, :, 0:8], c.lg[:, :, 0:8], ACT.Exp).then_inc(c.sems["r_exp"], 1)
            if c.nr == 9:
                act.activation(c.gates[:, :, 8], c.lg[:, :, 8], ACT.Sigmoid).then_inc(c.sems["r_exp"], 1)
            for i, (rows_, nc_, _, _) in enumerate(c.experts):
                for t in range(c.first[i], c.first[i + 1]):
                    act.wait_ge(c.sems["hid_mm"], t + 1)
                    if t >= 2:
                        act.wait_ge(c.sems["hid_ev"], t - 1)
                    act.activation(c.sil[t % 2][0:rows_, :], ps[0:rows_, 2 * (t % 2), 0:N51], ACT.Silu)\
                        .then_inc(c.sems["silu"], 1)

        def moe_dve(v, c):
            link = dve_chain.link
            v.wait_ge(c.sems["r_mm"], 1)
            r = ps[:, 7, 0:NJ * c.nr].rearrange("p (j r) -> p j r", r=c.nr)
            bias = row("router_b").unsqueeze(1).to_broadcast([128, NJ, 8])

            def over(x):
                return x.unsqueeze(2).to_broadcast([128, NJ, 8])
            if c.tag == "m1":
                link(v.tensor_tensor(c.lg, r, bias, ALU.add))
            else:
                v.tensor_scalar(c.lg[:, :, 8], r[:, :, 8], row("sg_b"), None, ALU.add)
                link(v.tensor_copy(c.lg[:, :, 0:8], r[:, :, 0:8]))
            m0, m1, m2, m3 = (c.top[:, i, :] for i in range(4))
            link(v.tensor_reduce(m0, c.lg[:, :, 0:8], AX.X, ALU.max))
            v.tensor_tensor(c.lg[:, :, 0:8], c.lg[:, :, 0:8], over(m0), ALU.subtract).then_inc(c.sems["r_arg"], 1)
            v.wait_ge(c.sems["r_exp"], 1)
            link(v.tensor_reduce(m1, c.lg[:, :, 0:8], AX.X, ALU.add))
            link(v.reciprocal(m1, m1))
            link(v.tensor_tensor(c.pr, c.lg[:, :, 0:8], over(m1), ALU.mult))
            rank = row("rank").unsqueeze(1).to_broadcast([128, NJ, 8])

            def best(value, dst):
                link(v.tensor_reduce(value, c.pr, AX.X, ALU.max))
                link(v.tensor_tensor(dst, c.pr, over(value), ALU.is_equal))
                link(v.tensor_tensor(dst, dst, rank, ALU.mult))
                link(v.tensor_reduce(m0, dst, AX.X, ALU.max))
                link(v.tensor_tensor(dst, dst, over(m0), ALU.is_equal))
            best(m1, c.one)
            if c.tag == "m1":
                link(v.tensor_copy(c.gates[:, :, 0:8], c.one))
            else:
                link(v.scalar_tensor_tensor(c.pr, c.one, -2.0, c.pr, ALU.mult, ALU.add))
                best(m2, c.two)
                v.tensor_tensor(c.one, c.one, over(m1), ALU.mult)
                v.tensor_tensor(c.two, c.two, over(m2), ALU.mult)
                link(v.tensor_tensor(m3, m1, m2, ALU.add))
                v.tensor_tensor(c.one, c.one, c.two, ALU.add)
                link(v.reciprocal(m3, m3))
                v.wait_ge(c.sems["r_exp"], 2)
                link(v.tensor_scalar(m0, c.gates[:, :, 8], -1.0, 1.0, ALU.mult, ALU.add))
                link(v.tensor_tensor(m3, m3, m0, ALU.mult))
                link(v.tensor_tensor(c.gates[:, :, 0:8], c.one, over(m3), ALU.mult))

            def gated(i):
                rows_, nc_, _, slots_ = c.experts[i]
                if i >= 2:
                    v.wait_ge(c.sems["down_mm"], NJ * (i - 1))
                for m4 in range(nc_):
                    for nh in range(2):
                        t = c.first[i] + 2 * m4 + nh
                        v.wait_ge(c.sems["silu"], t + 1)
                        v.tensor_tensor(tok(ht[0:rows_, slots_[m4], :])[:, nh * HALF:nh * HALF + HALF, 0:T],
                                        c.sil[t % 2][0:rows_, :].rearrange("p (b t) -> p b t", t=T),
                                        ps[0:rows_, 2 * (t % 2) + 1, 0:N51].rearrange("p (b t) -> p b t", t=T),
                                        ALU.mult).then_inc(c.sems["hid_ev"], 1)
            gated(0)
            for i in range(len(c.experts)):
                if i + 1 < len(c.experts):
                    gated(i + 1)
                for j in range(NJ):
                    jj = NJ * i + j
                    v.wait_ge(c.sems["down_mm"], jj + 1)
                    o = ps[:, 4 + jj % 3, 0:D]
                    if i == 0:
                        ins = v.tensor_scalar(c.acc[:, j, :], o, c.gates[:, j, i:i + 1], None, ALU.mult)
                    else:
                        v.wait_ge(c.sems["acc_ev"], jj - NJ + 1)
                        ins = v.scalar_tensor_tensor(c.acc[:, j, :], o, c.gates[:, j, i:i + 1], c.acc[:, j, :],
                                                     ALU.mult, ALU.add)
                    ins.then_inc(c.sems["acc_ev"], 1)
            v.wait_ge(c.sems["acc_ev"], NJ * len(c.experts))
            if c.tag == "m1":
                link(v.tensor_copy(c.accb, c.acc))
            for j in range(NJ):
                if c.tag == "m1":
                    ins = v.scalar_tensor_tensor(h[:, j, :], c.accb[:, j, :], m1[:, j:j + 1], h[:, j, :],
                                                 ALU.mult, ALU.add)
                else:
                    ins = v.tensor_tensor(h[:, j, :], h[:, j, :], c.acc[:, j, :], ALU.add)
                ins.then_inc(S["resid"], 1)
            v.wait_ge(S["resid"], NJ * (c.n + 1))

        moe1 = Moe(3, "m1", 0, 8, [(128, 4, 2816 * (e % 2), [4 * (e % 2) + m for m in range(4)]) for e in range(8)])
        moe3 = Moe(7, "m3", 8, 9, [(DH, 2, 1152 * (e % 2), [2 * (e % 2), 2 * (e % 2) + 1]) for e in range(8)] +
                   [(128, 6, 2304, [0, 1, 4, 5, 6, 7])])

        NE, NS, HID = 4, 256, 768
        phi = cut(wb, 5376, 2, NE * NS, rows=DH)
        soft_w = [(cut(wb, 2688 * i, 2, HID, rows=DH + 1), cut(wb, 2688 * i + 2 * HID, 6, D)) for i in range(2)]
        dt = cut(s, 0, NJ, NE * NS)
        ct = cut(s, 8192, 8, NB * TP)
        dbuf = [cut(s, 16384 + 1024 * i, NB, TP) for i in range(2)]
        cbuf = [cut(s, 18432 + 1024 * i, NE * NS) for i in range(2)]
        xw = [cut(s, 16384 + HID * i, HID) for i in range(2)]
        ub = [cut(s, 17920 + HID * i, 6, 2 * TP) for i in range(2)]
        sacc = cut(s, 20480, NJ, D)
        hb = [ht[:, :, :].rearrange("p a b -> p (a b)")[:, HID * i:HID * i + HID] for i in range(4)]
        SS = {name: sem(f"soft_{name}") for name in
              "phi loaded0 loaded1 zero dl_mm dl_arg d_exp d_ready cl_mm c_max c_exp t_mm t_ev xw_mm xw_ev f1_mm f1_ev "
              "u_mm u_ev f2_mm acc_ev".split()}
        NQ = NE * NJ
        cmax, crs, csum = small[:, 0:16], small[:, 16:24], small[:, 96:96 + 4 * NJ]
        dmx, dsum = small[:, 48:64], small[:, 64:80]

        def soft_pe(pe):
            pe.wait_ge(SS["phi"], 16)
            r = 0

            def turn(src, n):
                nonlocal r
                for u in range(0, n, 4):
                    if r >= 4:
                        pe.wait_ge(SS["t_ev"], r - 3)
                    for i in range(4):
                        m = pe.transpose(ps[:, 4 + r % 4, 128 * i:128 * i + 128], src[:, 128 * (u + i):128 * (u + i) + 128],
                                         ident[:, :])
                    m.then_inc(SS["t_mm"], 1)
                    r += 1

            def dispatch_logits(ch):
                if ch >= 2:
                    pe.wait_ge(SS["dl_arg"], ch - 1)
                for nh in range(2):
                    for k in range(2):
                        m = pe.matmul(ps[:, 2 * (ch % 2) + nh, 0:N51], phi[:, k, 128 * ch:128 * ch + 128],
                                      tok(xt[:, k, :])[:, nh * HALF:nh * HALF + HALF, 0:T], start=k == 0, stop=k == 1)
                m.then_inc(SS["dl_mm"], 1)

            def combine_logits(j):
                if j == 0:
                    pe.wait_ge(SS["dl_arg"], 7)
                elif j == 1:
                    pe.wait_ge(SS["dl_arg"], 8)
                else:
                    pe.wait_ge(SS["c_exp"], j - 1)
                for q in range(2):
                    for k in range(2):
                        m = pe.matmul(ps[:, 2 * (j % 2) + q, :], xt[:, k, 128 * j:128 * j + 128],
                                      phi[:, k, 512 * q:512 * q + 512], start=k == 0, stop=k == 1)
                m.then_inc(SS["cl_mm"], 1)

            dispatch_logits(0)
            for ch in range(8):
                if ch < 7:
                    dispatch_logits(ch + 1)
                else:
                    combine_logits(0)
                pe.wait_ge(SS["d_ready"], ch + 1)
                turn(dbuf[ch % 2].rearrange("p b t -> p (b t)"), 8)
            for j in range(NJ):
                if j < 7:
                    combine_logits(j + 1)
                pe.wait_ge(SS["c_exp"], j + 1)
                turn(cbuf[j % 2], 8)
            pe.wait_ge(SS["t_ev"], 32)

            def up(q):
                e, j = divmod(q, NJ)
                if j == 0:
                    pe.wait_ge(SS[f"loaded{e % 2}"], 32 * (e // 2 + 1))
                if q >= 1:
                    pe.wait_ge(SS["xw_ev"], q)
                for part in range(2):
                    for k in range(2):
                        m = pe.matmul(ps[:, 4 + part, 0:384], xt97[:, k, 128 * j:128 * j + 128],
                                      soft_w[e % 2][0][:, k, 384 * part:384 * part + 384], start=k == 0, stop=k == 1)
                m.then_inc(SS["xw_mm"], 1)

            def hidden(q, par, sc):
                e, j = divmod(q, NJ)
                i = 4 * q + 2 * par + sc
                if i >= 2:
                    pe.wait_ge(SS["f1_ev"], i - 1)
                at = slice(64 * par, 64 * par + 64)
                c0 = NS * e + 128 * sc
                for part in range(2):
                    m = pe.matmul(ps[:, 2 * (i % 2) + part, 0:384], dt[at, j, c0:c0 + 128],
                                  xw[q % 2][at, 384 * part:384 * part + 384], start=True, stop=True)
                m.then_inc(SS["f1_mm"], 1)

            def combine(q, par):
                e, j = divmod(q, NJ)
                i = 2 * q + par
                pe.wait_ge(SS["f1_ev"], 2 * i + 2)
                if i >= 1:
                    pe.wait_ge(SS["u_ev"], i)
                for m6 in range(6):
                    for sc in range(2):
                        m = pe.matmul(ps[:, 6, TP * m6:TP * m6 + T], hb[(2 * i + sc) % 4][:, 128 * m6:128 * m6 + 128],
                                      ct[:, 2 * e + sc, 128 * j + 64 * par:128 * j + 64 * par + T],
                                      start=sc == 0, stop=sc == 1)
                m.then_inc(SS["u_mm"], 1)

            def down(q):
                e, j = divmod(q, NJ)
                pe.wait_ge(SS["u_ev"], 2 * q + 2)
                if q >= 1:
                    pe.wait_ge(SS["acc_ev"], q)
                for m6 in range(6):
                    m = pe.matmul(ps[:, 7, 0:D], ub[q % 2][:, m6, :], soft_w[e % 2][1][:, m6, :],
                                  start=m6 == 0, stop=m6 == 5)
                m.then_inc(SS["f2_mm"], 1)

            up(0)
            for q in range(NQ):
                if q + 1 < NQ:
                    up(q + 1)
                pe.wait_ge(SS["xw_ev"], q + 1)
                hidden(q, 0, 0)
                hidden(q, 0, 1)
                if q >= 1:
                    combine(q - 1, 1)
                hidden(q, 1, 0)
                hidden(q, 1, 1)
                combine(q, 0)
                if q >= 1:
                    down(q - 1)
            combine(NQ - 1, 1)
            down(NQ - 1)

        def soft_act(act):
            r = 0

            def turned(dst):
                nonlocal r
                act.wait_ge(SS["t_mm"], r + 1)
                act.activation(dst, ps[:, 4 + r % 4, :].rearrange("p (a b) -> p a b", a=4), ACT.Copy)\
                    .then_inc(SS["t_ev"], 1)
                r += 1
            for ch in range(8):
                act.wait_ge(SS["dl_arg"], ch + 1)
                x = dbuf[ch % 2][:, :, 0:T]
                act.activation(x, x, ACT.Exp).then_inc(SS["d_exp"], 1)
                for u in range(2):
                    turned(dt[:, 4 * u:4 * u + 4, 128 * ch:128 * ch + 128])
            for j in range(NJ):
                act.wait_ge(SS["c_max"], j + 1)
                for e in range(NE):
                    ins = act.activation(cbuf[j % 2][:, NS * e:NS * e + NS],
                                         ps[:, 2 * (j % 2) + e // 2, NS * (e % 2):NS * (e % 2) + NS], ACT.Exp,
                                         bias=cmax[:, j:j + 1], accum_out=csum[:, NE * j + e:NE * j + e + 1])
                ins.then_inc(SS["c_exp"], 1)
                for u in range(2):
                    turned(ct[:, 4 * u:4 * u + 4, 128 * j:128 * j + 128])
            for i in range(4 * NQ):
                act.wait_ge(SS["f1_mm"], i + 1)
                if i >= 4:
                    act.wait_ge(SS["u_mm"], i // 2 - 1)
                b2_ = 2 * (i % 2)
                act.activation(hb[i % 4].rearrange("p (a n) -> p a n", a=2), ps[:, b2_:b2_ + 2, 0:384],
                               ACT.Gelu_apprx_tanh).then_inc(SS["f1_ev"], 1)

        def soft_dve(v):
            link = dve_chain.link
            v.wait_ge(SS["zero"], 3)
            for ch in range(8):
                v.wait_ge(SS["dl_mm"], ch + 1)
                if ch >= 2:
                    v.wait_ge(SS["t_mm"], 2 * (ch - 1))
                d = dbuf[ch % 2]
                for nh in range(2):
                    o = ps[:, 2 * (ch % 2) + nh, 0:N51].rearrange("p (b t) -> p b t", t=T)
                    ins = v.tensor_reduce(dmx[:, 8 * nh:8 * nh + 8], o, AX.X, ALU.max)
                link(ins)
                for nh in range(2):
                    o = ps[:, 2 * (ch % 2) + nh, 0:N51].rearrange("p (b t) -> p b t", t=T)
                    ins = v.tensor_tensor(d[:, 8 * nh:8 * nh + 8, 0:T], o,
                                          dmx[:, 8 * nh:8 * nh + 8].unsqueeze(2).to_broadcast([128, 8, T]), ALU.subtract)
                ins.then_inc(SS["dl_arg"], 1)
                v.wait_ge(SS["d_exp"], ch + 1)
                link(v.tensor_reduce(dsum, d[:, :, 0:T], AX.X, ALU.add))
                link(v.reciprocal(dsum, dsum))
                v.tensor_tensor(d[:, :, 0:T], d[:, :, 0:T], dsum.unsqueeze(2).to_broadcast([128, NB, T]), ALU.mult)\
                    .then_inc(SS["d_ready"], 1)
            for j in range(NJ):
                v.wait_ge(SS["cl_mm"], j + 1)
                if j >= 2:
                    v.wait_ge(SS["t_mm"], 16 + 2 * (j - 1))
                v.tensor_reduce(cmax[:, j:j + 1], ps[:, 2 * (j % 2):2 * (j % 2) + 2, :], AX.XY, ALU.max, negate=True)\
                    .then_inc(SS["c_max"], 1)
            v.wait_ge(SS["c_exp"], NJ)
            link(v.tensor_reduce(crs, csum.rearrange("p (j e) -> p j e", e=NE), AX.X, ALU.add))
            link(v.reciprocal(crs, crs))
            v.wait_ge(SS["t_mm"], 32)
            v.memset(sacc[:, :, :], 0.0)
            for x in ub:
                ins = v.memset(x, 0.0)
            link(ins)

            def up_ready(q):
                v.wait_ge(SS["xw_mm"], q + 1)
                if q >= 2:
                    v.wait_ge(SS["f1_mm"], 4 * (q - 1))
                v.tensor_copy(xw[q % 2].rearrange("p (a n) -> p a n", a=2), ps[:, 4:6, 0:384]).then_inc(SS["xw_ev"], 1)

            def combined(q, par):
                v.wait_ge(SS["u_mm"], 2 * q + par + 1)
                if q >= 2 and par == 0:
                    v.wait_ge(SS["f2_mm"], q - 1)
                v.tensor_copy(ub[q % 2][:, :, 64 * par:64 * par + T],
                              ps[:, 6, 0:384].rearrange("p (m t) -> p m t", t=TP)[:, :, 0:T]).then_inc(SS["u_ev"], 1)

            def accumulate(q):
                e, j = divmod(q, NJ)
                a_ = sacc[:, j, :]
                link(v.scalar_tensor_tensor(a_, row("l2_b2")[:, D * e:D * e + D], csum[:, NE * j + e:NE * j + e + 1], a_,
                                            ALU.mult, ALU.add))
                v.wait_ge(SS["f2_mm"], q + 1)
                v.tensor_tensor(a_, a_, ps[:, 7, 0:D], ALU.add).then_inc(SS["acc_ev"], 1)

            up_ready(0)
            for q in range(NQ):
                if q + 1 < NQ:
                    up_ready(q + 1)
                if q >= 1:
                    combined(q - 1, 1)
                combined(q, 0)
                if q >= 1:
                    accumulate(q - 1)
            combined(NQ - 1, 1)
            accumulate(NQ - 1)
            v.wait_ge(SS["acc_ev"], NQ)
            for j in range(NJ):
                v.scalar_tensor_tensor(h[:, j, :], sacc[:, j, :], crs[:, j:j + 1], h[:, j, :], ALU.mult, ALU.add)\
                    .then_inc(S["resid"], 1)
            v.wait_ge(S["resid"], NJ * 6)

        consts = [(ident[:, :], a["ident"]), (rows[:, :], a["rows"].partition_broadcast(128)), (vec[:, :, :], a["vec"]),
                  (clsrow[0:1, :], a["cls"][0:1, :]), (clsrow[1:2, :], a["cls"][1:2, :]),
                  (clsrow[64:65, :], a["cls"][0:1, :]), (clsrow[65:66, :], a["cls"][1:2, :]),
                  (live[:, :], a["live"]), (xt97[DH:DH + 1, :, :], a["mark"]), (inb[:, :], a["inb"]), (b1[:, :], a["b1"]),
                  (wrouter[:, :, :], a["wrouter"]), (cmask[:, :], a["cmask"])]
        NCONST = len(consts)

        @block.sync
        def _(sp):
            sp.dma_start(haar, a["haar"]).then_inc(S["tok_loaded"], 16)
            sp.dma_start(pg_w1, a["pg_w1"]).then_inc(S["tok_loaded"], 16)
            sp.dma_start(pl_w, a["pl_w"]).then_inc(S["tok_loaded"], 16)
            sp.dma_start(patches[:, 0:3, :], a["patches"][:, 0:3, :]).then_inc(S["patches_loaded"], 16)
            sp.dma_start(patches[:, 3:6, :], a["patches"][:, 3:6, :]).then_inc(S["patches_loaded"], 16)
            sp.wait_ge(S["zeroed"], 3)
            for dst, src in consts:
                sp.dma_start(dst, src).then_inc(S["consts_loaded"], 16)
            sp.dma_start(pw, a["pw"]).then_inc(S["tok_loaded"], 16)
            sp.dma_start(w_kvro, a["w_kvro"]).then_inc(S["l0_loaded"], 16)
            sp.dma_start(w_in, a["w_in"]).then_inc(S["l0_loaded"], 16)
            sp.dma_start(w_out, a["w_out"]).then_inc(S["l0_loaded"], 16)
            def attention_weights(c, name):
                if c.n == 2:
                    sp.wait_ge(S["f3_mm"], NJ)
                else:
                    sp.wait_ge(S["resid"], NJ * (c.n - 1))
                sp.dma_start(c.w_q, a[name + "_q"]).then_inc(c.sems["loaded"], 16)
                sp.dma_start(c.w_k, a[name + "_k"]).then_inc(c.sems["loaded"], 16)
                sp.dma_start(c.w_v, a[name + "_v"]).then_inc(c.sems["loaded"], 16)
                sp.dma_start(c.w_o, a[name + "_o"]).then_inc(c.sems["loaded"], 16)

            def expert_weights(c, name):
                if c.tag == "m3":
                    sp.wait_ge(S["resid"], NJ * 6)
                    for i, part in enumerate(("_s1", "_s2", "_s3")):
                        sp.dma_start(c.w[8][i], a[name + part]).then_inc(c.sems["loaded_shared"], 16)
                else:
                    sp.wait_ge(S["resid"], NJ * 2)
                for e in range(8):
                    if e >= 2:
                        sp.wait_ge(c.sems["down_mm"], NJ * (e - 1))
                    for i, part in enumerate(("_w1", "_w2", "_w3")):
                        sp.dma_start(c.w[e][i], a[name + part][e]).then_inc(c.sems[f"loaded{e % 2}"], 16)

            if upto > 2:
                attention_weights(att1, "a1")
            if upto > 3:
                expert_weights(moe1, "m1")
            if upto > 4:
                attention_weights(att2, "a2")
            if upto > 5:
                sp.wait_ge(S["resid"], NJ * 4)
                sp.dma_start(phi, a["phi"]).then_inc(SS["phi"], 16)
                for e in range(NE):
                    if e >= 2:
                        sp.wait_ge(SS["f2_mm"], NJ * (e - 1))
                    sp.dma_start(soft_w[e % 2][0], a["soft_w1"][e]).then_inc(SS[f"loaded{e % 2}"], 16)
                    sp.dma_start(soft_w[e % 2][1], a["soft_w2"][e]).then_inc(SS[f"loaded{e % 2}"], 16)
            if upto > 6:
                attention_weights(att3, "a3")
            if upto > 7:
                expert_weights(moe3, "m3")
            sp.wait_ge(S["resid"], NJ * min(upto, 8))
            o = out.rearrange("(j i) t d -> i t j d", i=2)
            sp.dma_start(o[0], h[0:T, :, :]).then_inc(S["out_done"], 16)
            sp.dma_start(o[1], h[64:64 + T, :, :]).then_inc(S["out_done"], 16)
            sp.wait_ge(S["out_done"], 32)

        @block.gpsimd
        def _(pool):
            pool.memset(clsrow[:, :], 0.0)
            pool.memset(eps[:, :], EPS)
            pool.memset(xt_store[0:DH, :, 0:1], 0.0)
            pool.memset(cut(s, 4704, 2 * 2592, rows=DH), 0.0).then_inc(S["zeroed"], 1)
            pool.memset(dw3[:, :, :], 0.0).then_inc(S["zeroed"], 1)
            pool.memset(ht[:, :, :], 0.0).then_inc(S["zeroed"], 1)
            def clear(view, n, signal):
                pool.wait_ge(S["resid"], NJ * n)
                pool.memset(view, 0.0).then_inc(signal, 1)

            if upto > 2:
                clear(att1.p_all, 2, att1.sems["p_zero"])
            if upto > 4:
                clear(att2.p_all, 4, att2.sems["p_zero"])
            if upto > 5:
                clear(cut(s, 16384, 2048), 5, SS["zero"])
                pool.wait_ge(SS["zero"], 1)
                for d in dbuf:
                    pool.memset(d[:, :, T:T + 1], 1.0).then_inc(SS["zero"], 1)
            if upto > 6:
                clear(att3.p_all, 6, att3.sems["p_zero"])

        @block.tensor
        def _(pe):
            tokenizer_pe(pe)
            if upto >= 1:
                layernorm_pe(pe, 0)
                rwkv_pe(pe)
            if upto >= 2:
                layernorm_pe(pe, 1)
                ffn0_pe(pe)
            if upto >= 3:
                layernorm_pe(pe, 2)
                attn_pe(pe, att1)
            if upto >= 4:
                layernorm_pe(pe, 3)
                moe_pe(pe, moe1)
            if upto >= 5:
                layernorm_pe(pe, 4)
                attn_pe(pe, att2)
            if upto >= 6:
                layernorm_pe(pe, 5)
                soft_pe(pe)
            if upto >= 7:
                layernorm_pe(pe, 6)
                attn_pe(pe, att3)
            if upto >= 8:
                layernorm_pe(pe, 7)
                moe_pe(pe, moe3)

        @block.scalar
        def _(act):
            tokenizer_act(act)
            normalize_act(act, -1)
            if upto >= 1:
                layernorm_act(act, 0)
                rwkv_act(act)
            if upto >= 2:
                layernorm_act(act, 1)
                ffn0_act(act)
            if upto >= 3:
                layernorm_act(act, 2)
                attn_act(act, att1)
            if upto >= 4:
                layernorm_act(act, 3)
                moe_act(act, moe1)
            if upto >= 5:
                layernorm_act(act, 4)
                attn_act(act, att2)
            if upto >= 6:
                layernorm_act(act, 5)
                soft_act(act)
            if upto >= 7:
                layernorm_act(act, 6)
                attn_act(act, att3)
            if upto >= 8:
                layernorm_act(act, 7)
                moe_act(act, moe3)

        @block.vector
        def _(v):
            tokenizer_dve(v)
            if upto >= 1:
                layernorm_dve(v, 0)
                rwkv_dve(v)
            if upto >= 2:
                layernorm_dve(v, 1)
                residual_dve(v, 1)
            if upto >= 3:
                layernorm_dve(v, 2)
                attn_dve(v, att1)
            if upto >= 4:
                layernorm_dve(v, 3)
                moe_dve(v, moe1)
            if upto >= 5:
                layernorm_dve(v, 4)
                attn_dve(v, att2)
            if upto >= 6:
                layernorm_dve(v, 5)
                soft_dve(v)
            if upto >= 7:
                layernorm_dve(v, 6)
                attn_dve(v, att3)
            if upto >= 8:
                layernorm_dve(v, 7)
                moe_dve(v, moe3)


def weights(w, kc):
    return w.reshape(w.shape[0] // kc, kc, w.shape[1]).transpose(1, 0, 2)


def haar_matrix():
    m = np.ones((256, 256), np.float32)
    for band in range(256):
        for level in range(4):
            digit = (band >> (2 * (3 - level))) & 3
            for pixel in range(256):
                y, x = divmod(pixel, 16)
                if (digit >> 1) & (x >> level) & 1:
                    m[band, pixel] *= -1
                if digit & (y >> level) & 1:
                    m[band, pixel] *= -1
    return m / 16


def lay_out(i):
    sq = {k: np.asarray(v, np.float32) for k, v in i.items()}
    o = {}
    x = sq["x"].reshape(NB, 3, SIDE, 16, SIDE, 16).transpose(1, 3, 5, 2, 4, 0).reshape(768, NB * NP)
    o["patches"] = weights(x, 128)
    o["pl_w"] = weights(sq["L0_tok_pl_w"].reshape(D, 768).T, 128)
    pg = sq["L0_tok_pg_w1"].reshape(D, 256, 3).transpose(1, 2, 0)
    o["pg_w1"] = pg.reshape(2, 128, 3, D).transpose(1, 0, 2, 3)
    o["haar"] = haar_matrix().reshape(2, 128, 256).transpose(1, 0, 2)
    o["pw"] = np.stack([weights(sq[f"L0_tok_{n}"].reshape(D, D).T, DH)
                        for n in ("pl_pw", "pg_pw", "pg_w2", "f1_pw", "f2_pw", "f3_pw")], 1)
    names = {"pl_b": "L0_tok_pl_b", "pl_pwb": "L0_tok_pl_pwb", "pg_b1": "L0_tok_pg_b1", "pg_pwb": "L0_tok_pg_pwb",
             "pg_b2": "L0_tok_pg_b2", "alpha": "L0_tok_alpha", "f1_pwb": "L0_tok_f1_pwb", "f2_pwb": "L0_tok_f2_pwb",
             "decay": "L0_attn_time_decay", "first": "L0_attn_time_first", "mk": "L0_attn_time_mix_k",
             "mv": "L0_attn_time_mix_v", "mr": "L0_attn_time_mix_r"}
    vec = np.zeros((D, NVEC), np.float32)
    for n, c in VEC.items():
        vec[:, c] = sq[names[n]].reshape(D)
    for n, c in TAPS.items():
        vec[:, c:c + 9] = sq[f"L0_tok_{n}_dw"].reshape(D, 9)
    o["vec"] = weights(vec, DH)
    rows = {"f3_pwb": "L0_tok_f3_pwb", "ln_g": "L0_tok_ln_g", "ln_b": "L0_tok_ln_b", "l1_b": "L1_attn_b_proj",
            "l2_b": "L2_attn_b_o", "l2_b2": "L2_ffn_b2", "router_b": "L1_ffn_router_b", "sg_b": "L3_ffn_sg_b"}
    sq["rank"] = np.arange(8, 0, -1, dtype=np.float32)
    rows["rank"] = "rank"
    o["rows"] = np.concatenate([sq[rows[n]].reshape(-1) for n in ROWS])
    o["cls"] = np.stack([sq["cls_tok"].reshape(D), sq["L0_tok_cls"].reshape(D)])
    live = np.zeros((2, TP, 2), np.float32)
    live[:, 2:T, 0] = 1
    live[:, 0:T, 1] = 1
    o["live"] = live.reshape(128, 2)
    mark = np.zeros((1, 2, NB, TP), np.float32)
    mark[:, 0, :, T] = 1
    o["mark"] = mark.reshape(1, 2, NB * TP)
    o["ident"] = np.eye(128, dtype=np.float32)
    o["inb"] = sq["L0_ffn_in_bias"].reshape(6, 128).T
    o["b1"] = sq["L2_ffn_b1"].reshape(24, 128).T
    o["wrouter"] = weights(np.concatenate([sq["L1_ffn_router_w"], sq["L3_ffn_router_w"], sq["L3_ffn_sg_w"]], 1), DH)
    q = np.arange(128)[:, None] % TP
    o["cmask"] = np.where(np.arange(T)[None, :] <= q, 0.0, -1e30).astype(np.float32)
    o["w_kvro"] = np.stack([weights(sq[f"L0_attn_W{n}"].T, DH) for n in "kvro"], 1)
    o["w_in"] = weights(sq["L0_ffn_in_weight"].T, DH)
    o["w_out"] = weights(sq["L0_ffn_out_weight"], 128)
    third = sq["L1_attn_w_qkv"].reshape(3, 8, 3, 8, D)

    def slots(w):
        p = np.zeros((8, 32, D), np.float32)
        p[:, :8] = w
        return p.reshape(256, D).T

    o["a1_q"] = weights(np.concatenate([slots(third[0, :, t]) for t in (1, 2)], 1), DH).reshape(DH, 2, 4, 128)
    o["a1_k"] = weights(np.concatenate([slots(third[1, :, t]) for t in (0, 1, 2)], 1), DH).reshape(DH, 2, 6, 128)
    v3, v4, v5 = (third[2, :, t].reshape(64, D).T for t in range(3))
    o["a1_v"] = weights(np.concatenate([v3, v3, v4, v4, v5, v5], 1), DH).reshape(DH, 2, 2, 192)
    o["a1_o"] = weights(sq["L1_attn_w_proj"].T, DH)
    o["a2_q"] = weights(sq["L2_attn_w_q"], DH).reshape(DH, 2, 6, 128)
    o["a2_k"] = weights(sq["L2_attn_w_k"], DH).reshape(DH, 2, 6, 128)

    def parities(w, groups):
        per = 12 // groups
        heads = [groups * (n % per) + n // per for n in range(12)]
        return np.stack([w[:, heads[par::2]] for par in range(2)], 1).reshape(D, -1), heads[0::2] + heads[1::2]

    o["a2_v"] = weights(parities(sq["L2_attn_w_v"].reshape(D, 12, 64), 2)[0], DH).reshape(DH, 2, 2, 384)
    o["a2_o"] = weights(sq["L2_attn_w_o"], 128)

    def wide(w):
        p = np.zeros((D, 12, 32), np.float32)
        p[:, :, :16] = w
        return p.reshape(D, 384)

    o["a3_q"] = weights(wide(sq["L3_attn_query_mat"]), DH).reshape(DH, 2, 3, 128)
    o["a3_k"] = weights(wide(sq["L3_attn_key_mat"]), DH).reshape(DH, 2, 3, 128)
    vals, order = parities(sq["L3_attn_value_mat"], 4)
    o["a3_v"] = weights(vals, DH).reshape(DH, 2, 2, 96)
    o["a3_o"] = weights(sq["L3_attn_linear_m1"].reshape(12, 16, D)[order].reshape(D, D), DH)

    def experts(w, kc):
        return np.stack([weights(x, kc) for x in w])

    for n, (x1, x2, x3), kc in (("m1", ("L1_ffn_w1", "L1_ffn_w2", "L1_ffn_w3"), 128),
                                ("m3", ("L3_ffn_w_gate", "L3_ffn_w_up", "L3_ffn_w_down"), DH)):
        o[n + "_w1"], o[n + "_w2"], o[n + "_w3"] = experts(sq[x1], DH), experts(sq[x2], DH), experts(sq[x3], kc)
    o["m3_s1"] = weights(sq["L3_ffn_ws_gate"], DH)
    o["m3_s2"] = weights(sq["L3_ffn_ws_up"], DH)
    o["m3_s3"] = weights(sq["L3_ffn_ws_down"], 128)
    o["phi"] = weights(sq["L2_ffn_phi"].reshape(4 * 256, D).T, DH)
    bias = np.stack([sq["L2_ffn_b1"], np.zeros_like(sq["L2_ffn_b1"])], 1)[:, None]
    o["soft_w1"] = np.concatenate([experts(sq["L2_ffn_w1"], DH), bias], 1)
    o["soft_w2"] = experts(sq["L2_ffn_w2"], 128)
    return {k: np.ascontiguousarray(v) for k, v in o.items()}


def kernel(**inputs):
    import concourse.bacc as bacc
    from concourse.bass_utils import run_bass_kernel_spmd

    nc = bacc.Bacc("TRN2", target_bir_lowering=False, num_devices=1)
    arrays = lay_out(inputs)
    aps = {n: nc.dram_tensor(f"in_{n}", v.shape, F32, kind="ExternalInput").ap() for n, v in arrays.items()}
    out = nc.dram_tensor("tokens", (NB, T, D), F32, kind="ExternalOutput").ap()
    vit_tower(nc, aps, out)
    return run_bass_kernel_spmd(nc, [{f"in_{n}": v for n, v in arrays.items()}], core_ids=[0]).results[0]["tokens"]
```

```python
from contextlib import ExitStack

import numpy as np
import concourse.bass as bass
from concourse import mybir

F32 = mybir.dt.float32
F32R = mybir.dt.float32r
BF16 = mybir.dt.bfloat16
ALU = mybir.AluOpType
ACT = mybir.ActivationFunctionType
AX = mybir.AxisListType

NB = 16
SIDE = 7
NP = SIDE * SIDE
T = NP + 2
TP = 64
NJ = NB // 2
D = 192
DH = D // 2
HALF = NB // 2
NEG = -1e38
EPS = 1e-5
SCRATCH = 22704

VEC = {n: i for i, n in enumerate(
    ["pl_b", "pl_pwb", "pg_b1", "pg_pwb", "pg_b2", "alpha", "f1_pwb", "f2_pwb", "decay", "first", "mk", "mv", "mr"])}
TAPS = {n: len(VEC) + 9 * i for i, n in enumerate(["pl", "pg", "f1", "f2", "f3"])}
NVEC = len(VEC) + 45
ROWS = {}
_at = 0
for _n, _w in [("f3_pwb", D), ("ln_g", D), ("ln_b", D), ("l1_b", D), ("l2_b", D), ("l2_b2", 4 * D),
               ("router_b", 8), ("sg_b", 1), ("rank", 8)]:
    ROWS[_n] = (_at, _w)
    _at += _w
NROW = _at


def cut(area, at, *dims, rows=128):
    size = int(np.prod(dims))
    v = area[0:rows, at:at + size]
    if len(dims) == 1:
        return v
    names = "abcde"[:len(dims)]
    return v.rearrange(f"p ({' '.join(names)}) -> p {' '.join(names)}", **dict(zip(names, dims)))


class Chain:

    def __init__(self, eng, sem):
        self.eng, self.sem, self.n = eng, sem, 0

    def link(self, ins):
        self.n += 1
        ins.then_inc(self.sem, 1)
        self.eng.wait_ge(self.sem, self.n)


def vit_tower(nc, a, out):
    ctx = ExitStack()
    with ctx:
        def sb(name, *shape):
            return ctx.enter_context(nc.sbuf_tensor(name, list(shape), F32))

        def sem(name):
            return ctx.enter_context(nc.semaphore(name))

        ps = ctx.enter_context(nc.psum_tensor("ps", [128, 8, 512], F32))
        s = sb("s", 128, SCRATCH)
        s_at = nc.sbuf_base - 4 * SCRATCH
        h = sb("h", 128, NJ, D)
        xn = sb("xn", 128, NJ, D)
        XT = NB * TP + 4
        xt_store = sb("xt_store", DH + 1, 2, XT)
        xt_at = nc.sbuf_base - 4 * 2 * XT
        ht = sb("ht", 128, 8, NB * TP)
        wa = sb("wa", 128, 5800)
        wa_at = nc.sbuf_base - 4 * 5800
        wb = sb("wb", 128, 7680)
        ident = sb("ident", 128, 128)
        rows = sb("rows", 128, NROW)
        vec = sb("vec", DH, 2, NVEC)
        clsrow = sb("clsrow", 128, D)
        live = sb("live", 128, 2)
        inb = sb("inb", 128, 6)
        b1 = sb("b1", 128, 24)
        wrouter = sb("wrouter", DH, 2, 17)
        cmask = sb("cmask", 128, T)
        eps = sb("eps", 128, 1)
        stats = sb("stats", 128, NJ, 6)
        mv = sb("mv", 128, NJ, 2)
        warm = sb("warm", 128, 32)
        warm_column = iter(range(32))
        std = sb("std", 128, NJ)
        rstd = sb("rstd", 128, NJ)
        small = sb("small", 128, 640)

        xt = xt_store[0:DH, :, 1:1 + NB * TP]
        xt97 = xt_store[:, :, 1:1 + NB * TP]
        xtp = xt_store[0:DH, :, 0:NB * TP]

        def parts(name, at, size, base=s_at, rows_in=128):
            return nc.alloc_sbuf_tensor_at(name, [rows_in, size], F32R, offset=base + 4 * at)[:, :]

        def tok(view):
            return view.rearrange("p (b t) -> p b t", t=TP)

        def row(name):
            at, w = ROWS[name]
            return rows[:, at:at + w]

        def col(name, half):
            return vec[:, half, VEC[name]:VEC[name] + 1]

        S = {n: sem(n) for n in (
            "consts_loaded tok_loaded patches_loaded l0_loaded zeroed dve_chain act_chain "
            "tok_mm tok_ev dw_done diagonal_ready img_mixed tok_mix f3_mm "
            "ln_stat ln_std ln_xn ln_tp ln_xt_act ln_xt_dve proj_mm resid "
            "mix_ready kvr_mm kvr_ev wkv_arg wkv_exp z_ready ffn_mm ffn_ev out_done").split()}

        block = ctx.enter_context(nc.Block())
        dve_chain = Chain(nc.vector, S["dve_chain"])
        act_chain = Chain(nc.scalar, S["act_chain"])

        pl_w = cut(wa, 0, 6, D)
        pg_w1 = cut(wa, 1152, 2, 3, D)
        haar = cut(wa, 2304, 2, 256)
        pw = cut(wa, 2816, 6, 2, D, rows=DH)
        patches = cut(s, 0, 6, NB * NP)
        img_a = cut(s, 4704, 2, 9, 9 * NB, rows=DH)
        img_b = cut(s, 7296, 2, 9, 9 * NB, rows=DH)
        dwo = [cut(s, 9888 + 1568 * i, 2, NB * NP, rows=DH) for i in range(2)]
        loc = cut(s, 13024, 2, NB * NP, rows=DH)
        g2 = cut(s, 14592, 2, NB * NP, rows=DH)
        glob = cut(s, 16160, 2, NB * NP, rows=DH)
        weff = cut(s, 17728, 6, D)
        dw3 = cut(s, 18880, 2, NB * TP, rows=DH)
        DEPTHWISE = ["pg", "f1", "f2", "f3"]
        diagonal = {n: cut(ht[:, :, :].rearrange("p a b -> p (a b)"), 1728 * i, 9, 2, DH, rows=DH)
                    for i, n in enumerate(DEPTHWISE)}
        RB = SIDE * NB
        YS = [(0, 4), (4, 3)]

        def window(img, half, dy=1, dx=1, y0=0, ny=SIDE):
            return img[:, half, dy + y0:dy + y0 + ny, dx * NB:dx * NB + RB]

        def spread(view):
            return view.rearrange("p (y c) -> p y c", c=RB)

        TOK = ["weff"] * 6 + ["loc"] * 4 + ["glob1"] * 4 + ["dw_pg"] * 2 + ["pl_pw"] * 4 + ["pg_pw"] * 4 + \
              ["pg_w2"] * 4 + ["dw_f1"] * 2 + ["f1"] * 4 + ["dw_f2"] * 2 + ["f2"] * 4 + ["dw_f3"] * 2
        FIRST = {n: TOK.index(n) for n in TOK}

        def tokenizer_pe(pe):
            t = 0

            def bank():
                if t >= 8:
                    pe.wait_ge(S["tok_ev"], t - 7)
                return ps[:, t % 8, :]
            pe.wait_ge(S["tok_loaded"], 16 * 4)
            for c in range(3):
                for half in range(2):
                    o = bank()
                    for k in range(2):
                        m = pe.matmul(o[:, 0:D], haar[:, k, half * 128:half * 128 + 128], pg_w1[:, k, c, :],
                                      start=k == 0, stop=k == 1)
                    m.then_inc(S["tok_mm"], 1)
                    t += 1
            pe.wait_ge(S["patches_loaded"], 32)
            for w, need in ((pl_w, 0), (weff, 6)):
                if need:
                    pe.wait_ge(S["tok_ev"], need)
                for oh in range(2):
                    for nh in range(2):
                        o = bank()
                        y0, ny = YS[nh]
                        for k in range(6):
                            m = pe.matmul(o[0:DH, 0:ny * RB], w[:, k, oh * DH:oh * DH + DH],
                                          patches[:, k, y0 * RB:(y0 + ny) * RB], start=k == 0, stop=k == 5)
                        m.then_inc(S["tok_mm"], 1)
                        t += 1

            def depthwise(img, name):
                nonlocal t
                pe.wait_ge(S["diagonal_ready"], DEPTHWISE.index(name) + 1)
                for half in range(2):
                    o = bank()
                    for tap in range(9):
                        dy, dx = divmod(tap, 3)
                        m = pe.matmul(o[0:DH, 0:YS[1][1] * RB], diagonal[name][:, tap, half, :],
                                      window(img, half, dy, dx, *YS[1]), start=tap == 0, stop=tap == 8)
                    m.then_inc(S["tok_mm"], 1)
                    t += 1

            pe.wait_ge(S["tok_ev"], FIRST["dw_pg"])
            depthwise(img_b, "pg")
            for i, (src, dws, evs) in enumerate([(dwo[0], 1, 0), (dwo[1], 2, FIRST["pl_pw"]),
                                                 (g2, 2, FIRST["pg_w2"]), (dwo[0], 3, FIRST["f1"]),
                                                 (dwo[1], 4, FIRST["f2"])]):
                if i == 3:
                    pe.wait_ge(S["img_mixed"], 2)
                    depthwise(img_a, "f1")
                if i == 4:
                    pe.wait_ge(S["tok_ev"], FIRST["dw_f2"])
                    depthwise(img_b, "f2")
                pe.wait_ge(S["dw_done"], dws)
                if evs:
                    pe.wait_ge(S["tok_ev"], evs)
                for oh in range(2):
                    for nh in range(2):
                        o = bank()
                        y0, ny = YS[nh]
                        for k in range(2):
                            m = pe.matmul(o[0:DH, 0:ny * RB], pw[:, i, k, oh * DH:oh * DH + DH],
                                          src[:, k, y0 * RB:(y0 + ny) * RB], start=k == 0, stop=k == 1)
                        m.then_inc(S["tok_mm"], 1)
                        t += 1
            pe.wait_ge(S["img_mixed"], 4)
            depthwise(img_a, "f3")
            pe.wait_ge(S["tok_mix"], 2)
            pe.wait_ge(S["tok_ev"], len(TOK))
            for j in range(NJ):
                for k in range(2):
                    m = pe.matmul(ps[:, j, 0:D], dw3[:, k, 2 * TP * j:2 * TP * j + 128], pw[:, 5, k, :],
                                  start=k == 0, stop=k == 1)
                m.then_inc(S["f3_mm"], 1)

        def tokenizer_act(act):
            t = 0
            act.wait_ge(S["consts_loaded"], 16 * NCONST)
            act_chain.link(act.activation(small[0:DH, 0:2], vec[:, :, VEC["alpha"]], ACT.Tanh))
            for name, fn, bias, dst in [("weff", ACT.Copy, None, None), ("loc", ACT.Gelu, "pl_b", img_a),
                                        ("glob1", ACT.Gelu, "pg_b1", img_b),
                                        ("dw_pg", ACT.Copy, None, dwo[1]), ("pl_pw", ACT.Identity, "pl_pwb", loc),
                                        ("pg_pw", ACT.Gelu, "pg_pwb", g2), ("pg_w2", ACT.Identity, "pg_b2", glob),
                                        ("dw_f1", ACT.Copy, None, dwo[0]), ("f1", ACT.Relu, "f1_pwb", img_b),
                                        ("dw_f2", ACT.Copy, None, dwo[1]), ("f2", ACT.Relu, "f2_pwb", g2),
                                        ("dw_f3", ACT.Copy, None, dwo[0])]:
                if name == "loc":
                    act.wait_ge(S["zeroed"], 3)
                if name == "f1":
                    act.wait_ge(S["dw_done"], 3)
                for i in range(TOK.count(name)):
                    act.wait_ge(S["tok_mm"], t + 1)
                    o = ps[:, t % 8, :]
                    if name == "weff":
                        ins = act.activation(weff[:, i, :], o[:, 0:D], fn)
                    elif name[0:2] == "dw":
                        y0, ny = YS[1]
                        ins = act.activation(dst[:, i, y0 * RB:(y0 + ny) * RB], o[0:DH, 0:ny * RB], fn)
                    else:
                        oh, nh = i // 2, i % 2
                        y0, ny = YS[nh]
                        src = o[0:DH, 0:ny * RB]
                        if dst is img_a or dst is img_b:
                            ins = act.activation(window(dst, oh, y0=y0, ny=ny), spread(src), fn, bias=col(bias, oh))
                        else:
                            ins = act.activation(dst[:, oh, y0 * RB:(y0 + ny) * RB], src, fn, bias=col(bias, oh))
                    ins.then_inc(S["tok_ev"], 1)
                    t += 1

        def tokenizer_pool(pool):
            pool.wait_ge(S["zeroed"], 3)
            pool.wait_ge(S["consts_loaded"], 16 * NCONST)
            for name in DEPTHWISE:
                for tap in range(9):
                    for half in range(2):
                        w = vec[:, half, TAPS[name] + tap:TAPS[name] + tap + 1]
                        ins = pool.tensor_scalar(diagonal[name][:, tap, half, :], ident[0:DH, 0:DH], w, None, ALU.mult)
                ins.then_inc(S["diagonal_ready"], 1)

        def tokenizer_dve(v):
            link = dve_chain.link
            v.wait_ge(S["consts_loaded"], 16 * NCONST)
            v.wait_ge(S["zeroed"], 3)

            def conv(img, name, dst):
                for tap in range(9):
                    dy, dx = divmod(tap, 3)
                    for half in range(2):
                        y0, ny = YS[0] if name in DEPTHWISE else (0, SIDE)
                        x = window(img, half, dy, dx, y0, ny)
                        o = spread(dst[:, half, y0 * RB:(y0 + ny) * RB])
                        w = vec[:, half, TAPS[name] + tap:TAPS[name] + tap + 1]
                        if tap == 0:
                            ins = v.tensor_scalar(o, x, w, None, ALU.mult)
                        else:
                            ins = v.scalar_tensor_tensor(o, x, w, o, ALU.mult, ALU.add)
                        if half == 0:
                            dve_chain.n += 1
                            ins.then_inc(S["dve_chain"], 1)
                        elif tap < 8:
                            link(ins)
                        else:
                            ins.then_inc(S["dw_done"], 1)

            v.wait_ge(S["tok_ev"], FIRST["glob1"])
            conv(img_a, "pl", dwo[0])
            v.wait_ge(S["tok_ev"], FIRST["dw_pg"])
            conv(img_b, "pg", dwo[1])
            gate, keep = small[0:DH, 2:4], small[0:DH, 4:6]
            v.wait_ge(S["act_chain"], 1)
            link(v.tensor_scalar(gate, small[0:DH, 0:2], 1.0, 0.5, ALU.add, ALU.mult))
            link(v.tensor_scalar(keep, gate, -1.0, 1.0, ALU.mult, ALU.add))
            v.wait_ge(S["tok_ev"], FIRST["dw_f1"])
            for half in range(2):
                link(v.tensor_scalar(glob[:, half, :], glob[:, half, :], gate[:, half:half + 1], None, ALU.mult))
                v.scalar_tensor_tensor(window(img_a, half), spread(loc[:, half, :]), keep[:, half:half + 1],
                                       spread(glob[:, half, :]), ALU.mult, ALU.add).then_inc(S["img_mixed"], 1)
            v.wait_ge(S["img_mixed"], 2)
            conv(img_a, "f1", dwo[0])
            v.wait_ge(S["tok_ev"], FIRST["dw_f2"])
            conv(img_b, "f2", dwo[1])
            v.wait_ge(S["tok_ev"], FIRST["dw_f3"])
            for half in range(2):
                v.tensor_tensor(window(img_a, half), spread(loc[:, half, :]), spread(g2[:, half, :]),
                                ALU.add).then_inc(S["img_mixed"], 1)
            v.wait_ge(S["img_mixed"], 4)
            conv(img_a, "f3", dwo[0])
            v.wait_ge(S["dw_done"], 5)
            v.wait_ge(S["tok_ev"], len(TOK))
            for half in range(2):
                v.tensor_copy(tok(dw3[:, half, :])[:, :, 2:2 + NP],
                              dwo[0][:, half, :].rearrange("p (t b) -> p b t", b=NB)).then_inc(S["tok_mix"], 1)
            for j in range(NJ):
                v.wait_ge(S["f3_mm"], j + 1)
                ins = v.tensor_tensor(xn[:, j, :], ps[:, j, 0:D], row("f3_pwb"), ALU.add)
            link(ins)
            normalize_dve(v, xn, -1)
            wide = [128, NJ, D]
            link(v.tensor_tensor(xn[:, :, :], xn[:, :, :], row("ln_g").unsqueeze(1).to_broadcast(wide), ALU.mult))
            link(v.tensor_tensor(xn[:, :, :], xn[:, :, :], row("ln_b").unsqueeze(1).to_broadcast(wide), ALU.add))
            link(v.scalar_tensor_tensor(h[:, :, :], xn[:, :, :], live[:, 0:1],
                                        clsrow[:, :].unsqueeze(1).to_broadcast(wide), ALU.mult, ALU.add))

        def normalize_dve(v, src, n):
            link = dve_chain.link
            if n - 1 not in PROJECTIONS:
                for j in range(NJ):
                    ins = v.bn_stats(stats[:, j, :], src[:, j, :])
                link(ins)
            for j in range(NJ):
                ins = v.bn_aggr(mv[:, j, :], stats[:, j, :])
            ins.then_inc(S["ln_stat"], 1)
            v.wait_ge(S["ln_std"], n + 2)
            link(v.reciprocal(rstd[:, :], std[:, :]))
            link(v.tensor_scalar(rstd[:, :], rstd[:, :], live[:, 1:2], None, ALU.mult))
            for j in range(NJ):
                ins = v.tensor_scalar(xn[:, j, :], src[:, j, :], mv[:, j, 0:1], rstd[:, j:j + 1],
                                      ALU.subtract, ALU.mult)
                ins.then_inc(S["ln_xn"], 1)
            v.wait_ge(S["ln_xn"], NJ * (n + 2))

        def load_table(act, fn):
            c = next(warm_column)
            act.activation(warm[:, c:c + 1], eps[:, 0:1], fn)

        def normalize_act(act, n):
            load_table(act, ACT.Sqrt)
            act.wait_ge(S["ln_stat"], n + 2)
            act.activation(std[:, :], mv[:, :, 1], ACT.Sqrt, bias=eps[:, 0:1]).then_inc(S["ln_std"], 1)

        def layernorm_dve(v, n):
            normalize_dve(v, h, n)
            for q in range(2):
                v.wait_ge(S["ln_tp"], 4 * n + 3 + q)
                v.tensor_copy(xt[:, 1, 512 * q:512 * q + 512], ps[0:DH, 2 + q, :]).then_inc(S["ln_xt_dve"], 1)
            v.wait_ge(S["ln_xt_dve"], 2 * (n + 1))

        def layernorm_act(act, n):
            normalize_act(act, n)
            for q in range(2):
                act.wait_ge(S["ln_tp"], 4 * n + 1 + q)
                act.activation(xt[:, 0, 512 * q:512 * q + 512], ps[0:DH, q, :], ACT.Copy)\
                    .then_inc(S["ln_xt_act"], 1)

        def layernorm_pe(pe, n):
            if n == 0:
                pe.wait_ge(S["consts_loaded"], 16 * NCONST)
            for half in range(2):
                for q in range(2):
                    for i in range(4):
                        j = 4 * q + i
                        pe.wait_ge(S["ln_xn"], NJ * (n + 1) + j + 1)
                        m = pe.transpose(ps[0:DH, 2 * half + q, 128 * i:128 * i + 128],
                                         xn[:, j, half * DH:half * DH + DH], ident[:, :])
                    m.then_inc(S["ln_tp"], 1)
            xt_ready(pe, n)

        def xt_ready(eng, n):
            eng.wait_ge(S["ln_xt_act"], 2 * (n + 1))
            eng.wait_ge(S["ln_xt_dve"], 2 * (n + 1))

        PROJECTIONS = [0, 1, 2, 4, 6]

        def project_pe(pe, n, chunks):
            for j in range(NJ):
                if j >= 2:
                    pe.wait_ge(S["resid"], NJ * n + j - 1)
                for c, (lhs, w) in enumerate(chunks):
                    m = pe.matmul(ps[:, 6 + j % 2, 0:D], lhs[:, 128 * j:128 * j + 128], w,
                                  start=c == 0, stop=c == len(chunks) - 1)
                m.then_inc(S["proj_mm"], 1)

        def residual_dve(v, n, bias=None):
            if bias is not None:
                dve_chain.link(v.tensor_tensor(h[:, :, :], h[:, :, :],
                                               row(bias).unsqueeze(1).to_broadcast([128, NJ, D]), ALU.add))
            for j in range(NJ + 1):
                if j < NJ:
                    v.wait_ge(S["proj_mm"], NJ * PROJECTIONS.index(n) + j + 1)
                    v.tensor_tensor(h[:, j, :], h[:, j, :], ps[:, 6 + j % 2, 0:D], ALU.add).then_inc(S["resid"], 1)
                if j >= 1:
                    v.wait_ge(S["resid"], NJ * n + j)
                    ins = v.bn_stats(stats[:, j - 1, :], h[:, j - 1, :])
            dve_chain.link(ins)

        w_kvro = cut(wb, 0, 4, 2, D, rows=DH)
        w_in = cut(wb, 1536, 2, 768, rows=DH)
        w_out = cut(wb, 3072, 6, D)
        N51 = HALF * T
        SL = T + 1
        mixed = cut(s, 0, 3, 2, NB * T, rows=DH)
        seq = [cut(s, 4896 + 2 * NB * SL * i, 2, NB, SL, rows=DH) for i in range(10)]
        kk, vv, sr, wst, omax, ea, eb, e1, e2, bv = seq
        pst, qst = [cut(s, 2 * NB * SL * i, 2, NB, SL, rows=DH) for i in range(2)]
        z = ht[0:DH, 0:2, :]

        def line(view):
            return view.rearrange("p a b c -> p (a b c)")

        def rwkv_pe(pe):
            for m3 in range(3):
                for oh in range(2):
                    for nh in range(2):
                        i = 4 * m3 + 2 * oh + nh
                        if i == 0:
                            pe.wait_ge(S["l0_loaded"], 48)
                        pe.wait_ge(S["mix_ready"], m3 + 1)
                        if i >= 4:
                            pe.wait_ge(S["kvr_ev"], i - 3)
                        for k in range(2):
                            m = pe.matmul(ps[0:DH, i % 4, 0:N51], w_kvro[:, m3, k, oh * DH:oh * DH + DH],
                                          mixed[:, m3, k, nh * N51:nh * N51 + N51], start=k == 0, stop=k == 1)
                        m.then_inc(S["kvr_mm"], 1)
            pe.wait_ge(S["z_ready"], 1)
            project_pe(pe, 0, [(z[:, k, :], w_kvro[:, 3, k, :]) for k in range(2)])

        def rwkv_act(act):
            for m3, dst in enumerate((kk, vv, sr)):
                for oh in range(2):
                    for nh in range(2):
                        i = 4 * m3 + 2 * oh + nh
                        act.wait_ge(S["kvr_mm"], i + 1)
                        act.activation(dst[:, oh, nh * HALF:nh * HALF + HALF, 1:SL],
                                       ps[0:DH, i % 4, 0:N51].rearrange("p (b t) -> p b t", t=T),
                                       ACT.Sigmoid if m3 == 2 else ACT.Copy).then_inc(S["kvr_ev"], 1)
            load_table(act, ACT.Exp)
            for i, x in enumerate((ea, eb, e1, e2)):
                act.wait_ge(S["wkv_arg"], i + 1)
                for oh in range(2):
                    ins = act.activation(x[:, oh, :, 1:SL], x[:, oh, :, 1:SL], ACT.Exp)
                ins.then_inc(S["wkv_exp"], 1)

        def rwkv_dve(v):
            link = dve_chain.link
            xt_ready(v, 0)
            for half in range(2):
                for i, m in enumerate(("mk", "mv", "mr")):
                    o = small[0:DH, 8 + 3 * half + i:9 + 3 * half + i]
                    ins = v.tensor_scalar(o, col(m, half), -1.0, 1.0, ALU.mult, ALU.add)
            link(ins)
            for i, m in enumerate(("mk", "mv", "mr")):
                for half in range(2):
                    o = mixed[:, i, half, :].rearrange("p (b t) -> p b t", t=T)
                    link(v.tensor_scalar(o, tok(xt[:, half, :])[:, :, 0:T], col(m, half), None, ALU.mult))
                    ins = v.scalar_tensor_tensor(o, tok(xtp[:, half, :])[:, :, 0:T],
                                                 small[0:DH, 8 + 3 * half + i:9 + 3 * half + i], o,
                                                 ALU.mult, ALU.add)
                    if half == 0:
                        link(ins)
                    else:
                        ins.then_inc(S["mix_ready"], 1)
            v.memset(kk[:, :, :, 0:1], NEG)
            v.memset(wst[:, :, :, 0:1], NEG)
            for x in (ea, eb, bv):
                v.memset(x[:, :, :, 0:1], 0.0)
            for oh in range(2):
                ins = v.tensor_scalar(wst[:, oh, :, 1:SL], tok(xt[:, oh, :])[:, :, 0:T], 0.0, col("decay", oh),
                                      ALU.mult, ALU.add)
            link(ins)
            v.wait_ge(S["kvr_ev"], 4)
            link(v.tensor_tensor_scan(line(omax), line(wst), line(kk), 0.0, ALU.add, ALU.max))
            o0, o1 = omax[:, :, :, 0:T], omax[:, :, :, 1:SL]
            k1, v1 = kk[:, :, :, 1:SL], vv[:, :, :, 1:SL]
            for oh in range(2):
                ins = v.scalar_tensor_tensor(ea[:, oh, :, 1:SL], o0[:, oh], col("decay", oh), o1[:, oh],
                                             ALU.add, ALU.subtract)
            ins.then_inc(S["wkv_arg"], 1)
            for oh in range(2):
                ins = v.tensor_tensor(eb[:, oh, :, 1:SL], k1[:, oh], o1[:, oh], ALU.subtract)
            ins.then_inc(S["wkv_arg"], 1)
            no = wst
            for oh in range(2):
                ins = v.scalar_tensor_tensor(no[:, oh, :, 1:SL], k1[:, oh], col("first", oh), o0[:, oh],
                                             ALU.add, ALU.max)
            link(ins)
            for oh in range(2):
                ins = v.tensor_tensor(e1[:, oh, :, 1:SL], o0[:, oh], no[:, oh, :, 1:SL], ALU.subtract)
            ins.then_inc(S["wkv_arg"], 1)
            for oh in range(2):
                ins = v.scalar_tensor_tensor(e2[:, oh, :, 1:SL], k1[:, oh], col("first", oh), no[:, oh, :, 1:SL],
                                             ALU.add, ALU.subtract)
            ins.then_inc(S["wkv_arg"], 1)
            v.wait_ge(S["kvr_ev"], 12)
            v.wait_ge(S["wkv_exp"], 2)
            for oh in range(2):
                ins = v.tensor_tensor(bv[:, oh, :, 1:SL], eb[:, oh, :, 1:SL], v1[:, oh], ALU.mult)
            link(ins)
            v.tensor_tensor_scan(line(pst), line(ea), line(bv), 0.0, ALU.mult, ALU.add)
            link(v.tensor_tensor_scan(line(qst), line(ea), line(eb), 0.0, ALU.mult, ALU.add))
            v.wait_ge(S["wkv_exp"], 4)
            A, B = e1[:, :, :, 1:SL], e2[:, :, :, 1:SL]
            num, den = ea[:, :, :, 1:SL], eb[:, :, :, 1:SL]
            for oh in range(2):
                v.tensor_tensor(num[:, oh], A[:, oh], pst[:, oh, :, 0:T], ALU.mult)
                v.tensor_tensor(den[:, oh], A[:, oh], qst[:, oh, :, 0:T], ALU.mult)
                link(v.tensor_tensor(v1[:, oh], v1[:, oh], B[:, oh], ALU.mult))
                v.tensor_tensor(num[:, oh], num[:, oh], v1[:, oh], ALU.add)
                link(v.tensor_tensor(den[:, oh], den[:, oh], B[:, oh], ALU.add))
                v.tensor_tensor(num[:, oh], num[:, oh], sr[:, oh, :, 1:SL], ALU.mult)
                link(v.reciprocal(den[:, oh], den[:, oh]))
                ins = v.tensor_tensor(tok(z[:, oh, :])[:, :, 0:T], num[:, oh], den[:, oh], ALU.mult)
            ins.then_inc(S["z_ready"], 1)
            residual_dve(v, 0)

        def ffn0_pe(pe):
            for m6 in range(6):
                for nh in range(2):
                    i = 2 * m6 + nh
                    if i >= 4:
                        pe.wait_ge(S["ffn_ev"], i - 3)
                    for k in range(2):
                        m = pe.matmul(ps[:, i % 4, 0:N51], w_in[:, k, 128 * m6:128 * m6 + 128],
                                      tok(xt[:, k, :])[:, nh * HALF:nh * HALF + HALF, 0:T],
                                      start=k == 0, stop=k == 1)
                    m.then_inc(S["ffn_mm"], 1)
            pe.wait_ge(S["ffn_ev"], 12)
            project_pe(pe, 1, [(ht[:, c, :], w_out[:, c, :]) for c in range(6)])

        def ffn0_act(act):
            load_table(act, ACT.Gelu)
            for i in range(12):
                act.wait_ge(S["ffn_mm"], i + 1)
                m6, nh = divmod(i, 2)
                act.activation(tok(ht[:, m6, :])[:, nh * HALF:nh * HALF + HALF, 0:T],
                               ps[:, i % 4, 0:N51].rearrange("p (b t) -> p b t", t=T), ACT.Gelu,
                               bias=inb[:, m6:m6 + 1]).then_inc(S["ffn_ev"], 1)

        class Attn:
            def __init__(self, n, tag, groups, per, rows, nq, nk, nch, vw, units, scale, wo):
                self.n, self.tag, self.groups, self.per, self.rows = n, tag, groups, per, rows
                self.nq, self.nk, self.nch, self.vw, self.units, self.scale = nq, nk, nch, vw, units, scale
                self.stride = 128 // groups
                at = 0
                self.w_q = cut(wa, at, 2, nq * nch, 128, rows=DH)
                at += 2 * nq * nch * 128
                self.w_k = cut(wa, at, 2, nk * nch, 128, rows=DH)
                at += 2 * nk * nch * 128
                self.w_v = cut(wa, at, 2, 2, vw, rows=DH)
                at += 4 * vw
                self.w_o = cut(wa, at, wo[1], D, rows=wo[0])
                at = 0
                self.q = cut(s, at, nq * nch, NB * TP)
                at += nq * nch * NB * TP
                self.k = cut(s, at, nk, nch, NB * T)
                at += nk * nch * NB * T
                self.v = cut(s, at, NB, 2 * vw if tag == "a3" else vw)
                if tag == "a3":
                    self.v_all = cut(s, at, NB * 2 * vw)
                at += NB * (2 * vw if tag == "a3" else vw)
                self.np = 3 if tag == "a3" else 2
                self.p = [cut(s, at + i * units * 128, units, 2, TP) for i in range(self.np)]
                self.p_all = cut(s, at, self.np * units * 128)
                at += self.np * units * 128
                self.pt = cut(s, at, units, 128)
                at += units * 128
                self.o = [cut(s, at + i * D, D) for i in range(2)]
                assert at + 2 * D <= SCRATCH
                self.sems = {name: sem(f"{tag}_{name}") for name in
                             "loaded qk_mm qk_ev v_mm v_ev v_zero p_zero s_mm arg exp p_ready ring_mm ring_ev pv_mm o_ev"
                             .split()}

            def turned(self, j):
                return -(-self.units // 4) * (j + 1) + (0 if self.tag == "a2" else max(j - 1, 0))

        def attn_pe(pe, c):
            pe.wait_ge(c.sems["loaded"], 16 * 4)
            for i in range((c.nq + c.nk) * c.nch):
                for nh in range(2):
                    t = 2 * i + nh
                    if t >= 4:
                        pe.wait_ge(c.sems["qk_ev"], t - 3)
                    isq = i < c.nq * c.nch
                    for k in range(2):
                        if isq:
                            m = pe.matmul(ps[:, t % 4, 0:512], c.w_q[:, k, i, :], xt[:, k, 512 * nh:512 * nh + 512],
                                          start=k == 0, stop=k == 1)
                        else:
                            m = pe.matmul(ps[:, t % 4, 0:N51], c.w_k[:, k, i - c.nq * c.nch, :],
                                          tok(xt[:, k, :])[:, nh * HALF:nh * HALF + HALF, 0:T],
                                          start=k == 0, stop=k == 1)
                    m.then_inc(c.sems["qk_mm"], 1)
            for j in range(NJ):
                if j >= 2:
                    pe.wait_ge(c.sems["v_ev"], j - 1)
                for par in range(2):
                    for k in range(2):
                        m = pe.matmul(ps[:, 4 + 2 * (j % 2) + par, 0:c.vw], xt[:, k, 128 * j:128 * j + 128],
                                      c.w_v[:, k, par, :], start=k == 0, stop=k == 1)
                m.then_inc(c.sems["v_mm"], 1)

            def scores(j):
                if j >= 1:
                    pe.wait_ge(c.sems["arg"], j)
                for e in range(2):
                    b = 2 * j + e
                    for ch in range(c.nch):
                        for g in range(c.groups):
                            at = slice(c.stride * g, c.stride * g + c.rows)
                            o = ps[64 * e:64 * e + 64, g, :]
                            ks = c.k[at, :, ch, T * b:T * b + T]
                            if c.nq == 2:
                                q4 = c.q[at, ch, TP * b:TP * b + TP]
                                q5 = c.q[at, c.nch + ch, TP * b:TP * b + TP]
                                pe.matmul(o[:, 255 * ch:255 * ch + 102], q4, ks[:, 0:2, :], start=True, stop=True)
                                m = pe.matmul(o[:, 255 * ch + 102:255 * ch + 255], q5, ks, start=True, stop=True)
                            else:
                                m = pe.matmul(o[:, T * ch:T * ch + T], c.q[at, ch, TP * b:TP * b + TP], ks[:, 0, :],
                                              start=True, stop=True)
                m.then_inc(c.sems["s_mm"], 1)

            r = 0

            def bank():
                nonlocal r
                if r >= 2:
                    pe.wait_ge(c.sems["ring_ev"], r - 1)
                r += 1
                return ps[:, 4 + (r - 1) % 2, :]

            def turn_out(j):
                pe.wait_ge(c.sems["o_ev"], j + 1)
                o = bank()
                for k in range(2):
                    m = pe.transpose(o[0:DH, 128 * k:128 * k + 128], c.o[j % 2][:, k * DH:k * DH + DH], ident[:, :])
                m.then_inc(c.sems["ring_mm"], 1)

            pe.wait_ge(c.sems["qk_ev"], 2 * (c.nq + c.nk) * c.nch)
            pe.wait_ge(c.sems["v_ev"], NJ)
            scores(0)
            scores(1)
            for j in range(NJ):
                if j + 2 < NJ and c.np == 3:
                    scores(j + 2)
                pe.wait_ge(c.sems["exp"] if c.nq == 2 else c.sems["p_ready"], j + 1)
                for u in range(0, c.units, 4):
                    o = bank()
                    for i in range(u, min(u + 4, c.units)):
                        m = pe.transpose(o[:, 128 * (i - u):128 * (i - u) + 128],
                                         c.p[j % c.np][:, i, :, :].rearrange("p s t -> p (s t)"), ident[:, :])
                    m.then_inc(c.sems["ring_mm"], 1)
                if j + 2 < NJ and c.np == 2:
                    scores(j + 2)
                if j >= 1 and c.tag != "a2":
                    turn_out(j - 1)
                pe.wait_ge(c.sems["ring_ev"], r - (1 if j >= 1 and c.tag != "a2" else 0))
                if j >= 1:
                    pe.wait_ge(c.sems["o_ev"], j)
                for u in range(c.units):
                    for e in range(2):
                        b = 2 * j + e
                        if c.tag == "a1":
                            m = pe.matmul(ps[64 * e:64 * e + 64, 6, 8 * u:8 * u + 8], c.pt[:, u, 64 * e:64 * e + 64],
                                          c.v[:, b, 8 * u:8 * u + 8], start=True, stop=True)
                        elif c.tag == "a3":
                            m = pe.matmul(ps[64 * e:64 * e + 64, 6, 32 * u:32 * u + 32],
                                          c.pt[:, u, 64 * e:64 * e + 64], c.v[:, b, 32 * u:32 * u + 32],
                                          start=True, stop=True)
                        else:
                            for par in range(2):
                                at = slice(64 * par, 64 * par + 64)
                                g, ch = divmod(2 * u + par, c.per)
                                m = pe.matmul(ps[64 * g:64 * g + 64, 6 + par,
                                                 128 * (ch // 2) + 64 * e:128 * (ch // 2) + 64 * e + 64],
                                              c.v[at, b, 64 * u:64 * u + 64], c.pt[at, u, 64 * e:64 * e + 64],
                                              start=True, stop=True)
                m.then_inc(c.sems["pv_mm"], 1)
            if c.tag != "a2":
                turn_out(NJ - 1)
                pe.wait_ge(c.sems["ring_ev"], r)
                project_pe(pe, c.n, [(ht[0:DH, k, :], c.w_o[:, k, :]) for k in range(2)])
            else:
                pe.wait_ge(c.sems["o_ev"], NJ)
                project_pe(pe, c.n, [(ht[:, k, :], c.w_o[:, k, :]) for k in range(6)])

        def attn_act(act, c):
            for i in range((c.nq + c.nk) * c.nch):
                for nh in range(2):
                    t = 2 * i + nh
                    act.wait_ge(c.sems["qk_mm"], t + 1)
                    if i < c.nq * c.nch:
                        ins = act.activation(c.q[:, i, 512 * nh:512 * nh + 512], ps[:, t % 4, :], ACT.Copy)
                    else:
                        kt, ch = divmod(i - c.nq * c.nch, c.nch)
                        ins = act.activation(c.k[:, kt, ch, N51 * nh:N51 * nh + N51], ps[:, t % 4, 0:N51], ACT.Copy)
                    ins.then_inc(c.sems["qk_ev"], 1)
            load_table(act, ACT.Exp)
            r = 0

            def turn_out(j):
                act.wait_ge(c.sems["ring_mm"], r + 1)
                act.activation(ht[0:DH, 0:2, 128 * j:128 * j + 128],
                               ps[0:DH, 4 + r % 2, 0:256].rearrange("p (k t) -> p k t", k=2), ACT.Copy)\
                    .then_inc(c.sems["ring_ev"], 1)

            def exponential(j):
                act.wait_ge(c.sems["arg"], j + 1)
                x = c.p[j % c.np].rearrange("p u s t -> p (u s) t")[:, :, 0:T]
                act.activation(x, x, ACT.Exp, scale=c.scale).then_inc(c.sems["exp"], 1)

            exponential(0)
            for j in range(NJ):
                if j + 1 < NJ:
                    exponential(j + 1)
                for u in range(0, c.units, 4):
                    nu = min(4, c.units - u)
                    act.wait_ge(c.sems["ring_mm"], r + 1)
                    if u == 0 and j >= 1:
                        act.wait_ge(c.sems["pv_mm"], j)
                    act.activation(c.pt[:, u:u + nu, :].rearrange("p u t -> p (u t)"), ps[:, 4 + r % 2, 0:128 * nu],
                                   ACT.Copy).then_inc(c.sems["ring_ev"], 1)
                    r += 1
                if j >= 1 and c.tag != "a2":
                    turn_out(j - 1)
                    r += 1
            if c.tag != "a2":
                turn_out(NJ - 1)

        def attn_dve(v, c):
            link = dve_chain.link
            if c.tag == "a3":
                v.wait_ge(c.sems["v_zero"], 1)
            for j in range(NJ):
                v.wait_ge(c.sems["v_mm"], j + 1)
                for e in range(2):
                    for par in range(2):
                        dst = c.v[64 * par:64 * par + 64, 2 * j + e, :]
                        src = ps[64 * e:64 * e + 64, 4 + 2 * (j % 2) + par, 0:c.vw]
                        if c.tag == "a3":
                            dst = dst.rearrange("p (u s d) -> p u s d", s=2, d=16)[:, :, par, :]
                            src = src.rearrange("p (u d) -> p u d", d=16)
                        ins = v.tensor_copy(dst, src)
                ins.then_inc(c.sems["v_ev"], 1)
            v.wait_ge(c.sems["p_zero"], 1)
            bmax, mx = small[:, 32:72], small[:, 72:96]
            total = [small[:, 96 + 24 * i:120 + 24 * i] for i in range(2)]
            nmx = 24 if c.tag == "a1" else 12

            def out_dve(j):
                v.wait_ge(c.sems["pv_mm"], j + 1)
                if c.tag == "a1":
                    v.tensor_tensor(c.o[j % 2].rearrange("p (u d) -> p u d", d=8),
                                    ps[:, 6, 0:D].rearrange("p (u d) -> p u d", d=8),
                                    total[j % 2].unsqueeze(2).to_broadcast([128, 24, 8]), ALU.mult)\
                        .then_inc(c.sems["o_ev"], 1)
                elif c.tag == "a2":
                    for par in range(2):
                        ins = v.tensor_copy(ht[:, par:6:2, 128 * j:128 * j + 128],
                                            ps[:, 6 + par, 0:384].rearrange("p (u t) -> p u t", u=3))
                    ins.then_inc(c.sems["o_ev"], 1)
                else:
                    v.tensor_copy(c.o[j % 2].rearrange("p (s u d) -> p u s d", s=2, d=16),
                                  ps[:, 6, 0:D].rearrange("p (u s d) -> p u s d", s=2, d=16))\
                        .then_inc(c.sems["o_ev"], 1)

            def arguments(j):
                v.wait_ge(c.sems["s_mm"], j + 1)
                if j >= 1:
                    v.wait_ge(c.sems["arg"], j)
                if j >= c.np:
                    v.wait_ge(c.sems["ring_mm"], c.turned(j - c.np))
                p = c.p[j % c.np]
                if c.tag == "a1":
                    for g in range(4):
                        ins = v.tensor_reduce(bmax[:, 10 * g:10 * g + 10],
                                              ps[:, g, 0:510].rearrange("p (c t) -> p c t", t=T), AX.X, ALU.max)
                    link(ins)
                    bm = bmax.rearrange("p (g c k) -> p c g k", g=4, c=2)
                    for a3, (k0, k1) in enumerate(((0, 1), (2, 4), (3, 4))):
                        ins = v.tensor_tensor(mx[:, 8 * a3:8 * a3 + 8].rearrange("p (c g) -> p c g", c=2),
                                              bm[:, :, :, k0], bm[:, :, :, k1], ALU.max)
                    link(ins)
                    for g in range(4):
                        sv = ps[:, g, 0:510].rearrange("p (c k t) -> p c k t", c=2, k=5)
                        for a3, ks in enumerate((slice(0, 2), slice(2, 5, 2), slice(3, 5))):
                            top = mx[:, 8 * a3 + g:8 * a3 + 8:4].unsqueeze(2).unsqueeze(3).to_broadcast([128, 2, 2, T])
                            ins = v.tensor_tensor(p[:, 8 * a3 + g:8 * a3 + 8:4, :, 0:T], sv[:, :, ks, :], top,
                                                  ALU.subtract)
                    ins.then_inc(c.sems["arg"], 1)
                else:
                    ph = p.rearrange("p u s t -> p (u s) t")[:, :, 0:T]
                    per = c.per
                    for g in range(c.groups):
                        sv = ps[:, g, 0:per * T].rearrange("p (c t) -> p c t", t=T)
                        if c.tag == "a2":
                            ins = v.tensor_reduce(mx[:, per * g:per * g + per], sv, AX.X, ALU.max)
                        else:
                            ins = v.tensor_tensor(ph[:, per * g:per * g + per, :], sv,
                                                  cmask[:, :].unsqueeze(1).to_broadcast([128, per, T]), ALU.add)
                    link(ins)
                    top = mx[:, 0:12].unsqueeze(2).to_broadcast([128, 12, T])
                    if c.tag == "a2":
                        for g in range(c.groups):
                            sv = ps[:, g, 0:per * T].rearrange("p (c t) -> p c t", t=T)
                            ins = v.tensor_tensor(ph[:, per * g:per * g + per, :], sv,
                                                  top[:, per * g:per * g + per, :], ALU.subtract)
                    else:
                        link(v.tensor_reduce(mx[:, 0:12], ph, AX.X, ALU.max))
                        ins = v.tensor_tensor(ph, ph, top, ALU.subtract)
                    ins.then_inc(c.sems["arg"], 1)

            def sums(j):
                p = c.p[j % c.np]
                ph = p.rearrange("p u s t -> p (u s) t")[:, :, 0:T]
                v.wait_ge(c.sems["exp"], j + 1)
                if j >= 2:
                    v.wait_ge(c.sems["o_ev" if c.tag == "a1" else "p_ready"], j - 1)
                tot = total[j % 2][:, 0:nmx]
                if c.tag == "a1":
                    link(v.tensor_reduce(tot, p[:, :, :, 0:T], AX.XY, ALU.add))
                    link(v.reciprocal(tot, tot))
                else:
                    link(v.tensor_reduce(tot, ph, AX.X, ALU.add))
                    link(v.reciprocal(tot, tot))
                    v.tensor_tensor(ph, ph, tot.unsqueeze(2).to_broadcast([128, 12, T]), ALU.mult)\
                        .then_inc(c.sems["p_ready"], 1)

            arguments(0)
            for j in range(NJ):
                if j + 1 < NJ:
                    arguments(j + 1)
                sums(j)
                if j >= 1:
                    out_dve(j - 1)
            out_dve(NJ - 1)
            residual_dve(v, c.n, {"a1": "l1_b", "a2": "l2_b", "a3": None}[c.tag])

        att1 = Attn(2, "a1", 4, 2, 8, 2, 3, 2, 192, 24, 24.0 ** -0.5, (DH, 2))
        att2 = Attn(4, "a2", 2, 6, 64, 1, 1, 6, 384, 6, 0.125, (128, 6))
        att3 = Attn(6, "a3", 4, 3, 16, 1, 1, 3, 96, 6, 4.0, (DH, 2))

        class Moe:
            def __init__(self, n, tag, col0, nr, experts):
                self.n, self.tag, self.col0, self.nr, self.experts = n, tag, col0, nr, experts
                self.w, self.raw, self.hi, self.lo = [], [], [], []
                self.xs = parts(f"{tag}_x", 3712, 3 * NB * T).rearrange("p (a n) -> p a n", a=3)
                first = experts[0][0] * experts[0][1]
                most = max(r_ * n_ for r_, n_, _, _ in experts)
                ws = parts(f"{tag}_w", 3712 + 3 * NB * T, 16 * first + (8 * most if len(experts) > 8 else 0))
                for i, (rows_, nc_, at, _) in enumerate(experts):
                    hid = rows_ * nc_
                    self.w.append((cut(wb, at, 2, hid), cut(wb, at + 2 * hid, 2, hid),
                                   cut(wb, at + 4 * hid, nc_, D, rows=rows_)))
                    self.raw.append(cut(wb, at, 4 * hid))
                    to = 8 * first * (i % 2 if i < 8 else 2)
                    self.hi.append(cut(ws, to, 2, 2, hid))
                    self.lo.append(cut(ws, to + 4 * hid, 2, 2, hid))
                t = 0
                self.first = []
                for _, nc_, _, _ in experts:
                    self.first.append(t)
                    t += 2 * nc_
                self.first.append(t)
                self.lg = cut(s, 0, NJ, nr)
                self.pr = cut(s, 80, NJ, 8)
                self.one = cut(s, 144, NJ, 8)
                self.two = cut(s, 208, NJ, 8)
                self.gates = cut(s, 272, NJ, 9)
                self.top = cut(s, 352, 4, NJ)
                self.acc = cut(s, 400, NJ, D)
                self.accb = cut(s, 2000, NJ * D // 2).bitcast(BF16).rearrange("p (j d) -> p j d", d=D)
                self.sil = [cut(s, 2800 + N51 * i, N51) for i in range(2)]
                self.sems = {name: sem(f"{tag}_{name}") for name in
                             "loaded0 loaded1 loaded_down0 loaded_down1 loaded_shared x_tp x_hi x_lo w_hi w_lo "
                             "r_mm r_arg r_exp hid_mm silu hid_ev down_mm acc_ev".split()}

        def channels(c):
            return [(part, q, ps[:, 4 + 2 * part + q, :].rearrange("p (b t) -> p b t", t=TP)[:, :, 0:T],
                     c.xs[:, 2 * part, N51 * q:N51 * q + N51].rearrange("p (b t) -> p b t", t=T))
                    for part in range(2) for q in range(2)]

        def moe_pool(pool, c):
            pool.wait_ge(S["resid"], NJ * c.n)
            for i, (rows_, nc_, _, _) in enumerate(c.experts):
                await_weights(pool, c, i)
                if 2 <= i < 8:
                    pool.wait_ge(c.sems["hid_mm"], c.first[i - 1])
                flat = "p a b n -> p (a b n)"
                pool.tensor_copy(c.hi[i].rearrange(flat), c.raw[i]).then_inc(c.sems["w_hi"], 1)
                pool.wait_ge(c.sems["w_hi"], i + 1)
                pool.tensor_tensor(c.lo[i].rearrange(flat), c.raw[i], c.hi[i].rearrange(flat), ALU.subtract)\
                    .then_inc(c.sems["w_lo"], 1)

        def await_weights(eng, c, i):
            if i == 8:
                eng.wait_ge(c.sems["loaded_shared"], 48)
            else:
                eng.wait_ge(c.sems[f"loaded{i % 2}"], 32 * (i // 2 + 1))

        def moe_pe(pe, c):
            for part in range(2):
                for q in range(2):
                    for i in range(4):
                        if part == 0:
                            m = pe.transpose(ps[:, 4 + q, 128 * i:128 * i + 128], xn[:, 4 * q + i, 0:128], ident[:, :])
                        else:
                            for at in (0, 64):
                                m = pe.matmul(ps[at:at + 64, 6 + q, 128 * i:128 * i + 128],
                                              xn[:, 4 * q + i, 128:192], ident[:, :], start=True, stop=True)
                    m.then_inc(c.sems["x_tp"], 1)
            pe.wait_ge(c.sems["x_hi"], 4)
            pe.wait_ge(c.sems["x_lo"], 4)
            for j in range(NJ):
                for k in range(2):
                    m = pe.matmul(ps[:, 7, c.nr * j:c.nr * j + c.nr], xt[:, k, 128 * j:128 * j + 128],
                                  wrouter[:, k, c.col0:c.col0 + c.nr], start=k == 0, stop=k == 1)
            m.then_inc(c.sems["r_mm"], 1)

            def hidden(i):
                rows_, nc_, _, _ = c.experts[i]
                pe.wait_ge(c.sems["w_hi"], i + 1)
                pe.wait_ge(c.sems["w_lo"], i + 1)
                for m4 in range(nc_):
                    for nh in range(2):
                        t = c.first[i] + 2 * m4 + nh
                        if t >= 2:
                            pe.wait_ge(c.sems["hid_ev"], t - 1)
                        for w in range(2):
                            wm, xm = slice(rows_ * m4, rows_ * m4 + rows_), slice(nh * N51, nh * N51 + N51)
                            hi, lo = c.hi[i][:, w, :, wm], c.lo[i][:, w, :, wm]
                            o = ps[0:rows_, 2 * (t % 2) + w, 0:N51]
                            pe.matmul(o, hi[:, 0, :], c.xs[:, 0, xm], start=True, stop=False)
                            pe.matmul(o, hi[:, 0, :], c.xs[:, 1, xm], start=False, stop=False)
                            pe.matmul(o, hi[:, 1, :], c.xs[:, 2, xm], start=False, stop=False)
                            pe.matmul(o, lo[:, 0, :], c.xs[:, 0, xm], start=False, stop=False)
                            m = pe.matmul(o, lo[0:64, 1, :], c.xs[0:64, 2, xm], start=False, stop=True)
                        m.then_inc(c.sems["hid_mm"], 1)

            hidden(0)
            for i, (rows_, nc_, _, slots_) in enumerate(c.experts):
                if i + 1 < len(c.experts):
                    hidden(i + 1)
                pe.wait_ge(c.sems["hid_ev"], c.first[i + 1])
                if i < 8:
                    pe.wait_ge(c.sems[f"loaded_down{i % 2}"], 16 * (i // 2 + 1))
                else:
                    pe.wait_ge(c.sems["loaded_shared"], 48)
                for j in range(NJ):
                    jj = NJ * i + j
                    if jj >= 3:
                        pe.wait_ge(c.sems["acc_ev"], jj - 2)
                    for m4 in range(nc_):
                        m = pe.matmul(ps[:, 4 + jj % 3, 0:D], ht[0:rows_, slots_[m4], 128 * j:128 * j + 128],
                                      c.w[i][2][:, m4, :], start=m4 == 0, stop=m4 == nc_ - 1)
                    m.then_inc(c.sems["down_mm"], 1)

        def moe_act(act, c):
            for i, (_, _, x, hi) in enumerate(channels(c)):
                act.wait_ge(c.sems["x_tp"], i + 1)
                act.activation(hi, x, ACT.Copy).then_inc(c.sems["x_hi"], 1)

            def router_exp():
                act.wait_ge(c.sems["r_arg"], 1)
                act.activation(c.lg[:, :, 0:8], c.lg[:, :, 0:8], ACT.Exp).then_inc(c.sems["r_exp"], 1)
                if c.nr == 9:
                    act.activation(c.gates[:, :, 8], c.lg[:, :, 8], ACT.Sigmoid).then_inc(c.sems["r_exp"], 1)

            load_table(act, ACT.Silu)
            for i, (rows_, nc_, _, _) in enumerate(c.experts):
                for t in range(c.first[i], c.first[i + 1]):
                    if t == 3:
                        router_exp()
                    act.wait_ge(c.sems["hid_mm"], t + 1)
                    if t >= 2:
                        act.wait_ge(c.sems["hid_ev"], t - 1)
                    act.activation(c.sil[t % 2][0:rows_, :], ps[0:rows_, 2 * (t % 2), 0:N51], ACT.Silu)\
                        .then_inc(c.sems["silu"], 1)

        def moe_dve(v, c):
            link = dve_chain.link
            for i, (part, q, x, hi) in enumerate(channels(c)):
                v.wait_ge(c.sems["x_hi"], i + 1)
                if part == 0:
                    low = c.xs[:, 1, N51 * q:N51 * q + N51].rearrange("p (b t) -> p b t", t=T)
                    ins = v.tensor_tensor(low, x, hi, ALU.subtract)
                else:
                    ins = v.tensor_tensor(hi[64:128], x[64:128], hi[64:128], ALU.subtract)
                ins.then_inc(c.sems["x_lo"], 1)
            r = ps[:, 7, 0:NJ * c.nr].rearrange("p (j r) -> p j r", r=c.nr)
            bias = row("router_b").unsqueeze(1).to_broadcast([128, NJ, 8])
            rank = row("rank").unsqueeze(1).to_broadcast([128, NJ, 8])
            m0, m1, m2, m3 = (c.top[:, i, :] for i in range(4))

            def over(x):
                return x.unsqueeze(2).to_broadcast([128, NJ, 8])

            def router_logits():
                v.wait_ge(c.sems["r_mm"], 1)
                if c.tag == "m1":
                    link(v.tensor_tensor(c.lg, r, bias, ALU.add))
                else:
                    v.tensor_scalar(c.lg[:, :, 8], r[:, :, 8], row("sg_b"), None, ALU.add)
                    link(v.tensor_copy(c.lg[:, :, 0:8], r[:, :, 0:8]))
                link(v.tensor_reduce(m0, c.lg[:, :, 0:8], AX.X, ALU.max))
                v.tensor_tensor(c.lg[:, :, 0:8], c.lg[:, :, 0:8], over(m0), ALU.subtract)\
                    .then_inc(c.sems["r_arg"], 1)

            def router_probabilities():
                v.wait_ge(c.sems["r_exp"], 1)
                link(v.tensor_reduce(m1, c.lg[:, :, 0:8], AX.X, ALU.add))
                link(v.reciprocal(m1, m1))
                link(v.tensor_tensor(c.pr, c.lg[:, :, 0:8], over(m1), ALU.mult))

            def best(value, dst):
                link(v.tensor_reduce(value, c.pr, AX.X, ALU.max))
                link(v.tensor_tensor(dst, c.pr, over(value), ALU.is_equal))
                link(v.tensor_tensor(dst, dst, rank, ALU.mult))
                link(v.tensor_reduce(m0, dst, AX.X, ALU.max))
                link(v.tensor_tensor(dst, dst, over(m0), ALU.is_equal))

            def router_gates():
                if c.tag == "m1":
                    link(v.tensor_copy(c.gates[:, :, 0:8], c.one))
                    return
                v.tensor_tensor(c.one, c.one, over(m1), ALU.mult)
                v.tensor_tensor(c.two, c.two, over(m2), ALU.mult)
                link(v.tensor_tensor(m3, m1, m2, ALU.add))
                v.tensor_tensor(c.one, c.one, c.two, ALU.add)
                link(v.reciprocal(m3, m3))
                v.wait_ge(c.sems["r_exp"], 2)
                link(v.tensor_scalar(m0, c.gates[:, :, 8], -1.0, 1.0, ALU.mult, ALU.add))
                link(v.tensor_tensor(m3, m3, m0, ALU.mult))
                link(v.tensor_tensor(c.gates[:, :, 0:8], c.one, over(m3), ALU.mult))

            def router(t):
                if t == 1:
                    router_logits()
                elif t == 4:
                    router_probabilities()
                elif t == 5:
                    best(m1, c.one)
                elif t == 6 and c.tag == "m3":
                    link(v.scalar_tensor_tensor(c.pr, c.one, -2.0, c.pr, ALU.mult, ALU.add))
                    best(m2, c.two)
                elif t == 7:
                    router_gates()

            def gated(i):
                rows_, nc_, _, slots_ = c.experts[i]
                if i >= 2:
                    v.wait_ge(c.sems["down_mm"], NJ * (i - 1))
                for m4 in range(nc_):
                    for nh in range(2):
                        t = c.first[i] + 2 * m4 + nh
                        router(t)
                        v.wait_ge(c.sems["silu"], t + 1)
                        v.tensor_tensor(tok(ht[0:rows_, slots_[m4], :])[:, nh * HALF:nh * HALF + HALF, 0:T],
                                        c.sil[t % 2][0:rows_, :].rearrange("p (b t) -> p b t", t=T),
                                        ps[0:rows_, 2 * (t % 2) + 1, 0:N51].rearrange("p (b t) -> p b t", t=T),
                                        ALU.mult).then_inc(c.sems["hid_ev"], 1)
            gated(0)
            for i in range(len(c.experts)):
                if i + 1 < len(c.experts):
                    gated(i + 1)
                for j in range(NJ):
                    jj = NJ * i + j
                    v.wait_ge(c.sems["down_mm"], jj + 1)
                    o = ps[:, 4 + jj % 3, 0:D]
                    if i == 0:
                        ins = v.tensor_scalar(c.acc[:, j, :], o, c.gates[:, j, i:i + 1], None, ALU.mult)
                    else:
                        v.wait_ge(c.sems["acc_ev"], jj - NJ + 1)
                        ins = v.scalar_tensor_tensor(c.acc[:, j, :], o, c.gates[:, j, i:i + 1], c.acc[:, j, :],
                                                     ALU.mult, ALU.add)
                    ins.then_inc(c.sems["acc_ev"], 1)
            v.wait_ge(c.sems["acc_ev"], NJ * len(c.experts))
            if c.tag == "m1":
                link(v.tensor_copy(c.accb, c.acc))
            for j in range(NJ):
                if c.tag == "m1":
                    ins = v.scalar_tensor_tensor(h[:, j, :], c.accb[:, j, :], m1[:, j:j + 1], h[:, j, :],
                                                 ALU.mult, ALU.add)
                else:
                    ins = v.tensor_tensor(h[:, j, :], h[:, j, :], c.acc[:, j, :], ALU.add)
                ins.then_inc(S["resid"], 1)
            v.wait_ge(S["resid"], NJ * (c.n + 1))

        moe1 = Moe(3, "m1", 0, 8, [(128, 4, 2816 * (e % 2), [4 * (e % 2) + m for m in range(4)]) for e in range(8)])
        moe3 = Moe(7, "m3", 8, 9, [(DH, 2, 1152 * (e % 2), [2 * (e % 2), 2 * (e % 2) + 1]) for e in range(8)] +
                   [(128, 6, 2304, [0, 1, 4, 5, 6, 7])])

        NE, NS, HID = 4, 256, 768
        phi = cut(wb, 5376, 2, NE * NS, rows=DH)
        soft_w = [(cut(wb, 2688 * i, 2, HID, rows=DH + 1), cut(wb, 2688 * i + 2 * HID, 6, D)) for i in range(2)]
        dt_hi, dt_lo = [parts(f"dispatch_{n}", 8192 * i, NJ * NE * NS).rearrange("p (j n) -> p j n", j=NJ)
                        for i, n in enumerate(("high", "low"))]
        xw_hi, xw_lo = [[parts(f"xw_{n}{i}", 16384 + HID * (2 * i + at), HID) for i in range(2)]
                        for at, n in enumerate(("high", "low"))]
        halves = "p (a n) -> p a n"
        x_hi = parts("soft_x_high", 0, 2 * NB * TP, wa_at, DH + 1).rearrange(halves, a=2)
        x_lo = parts("soft_x_low", 0, 2 * XT, xt_at, DH + 1).rearrange(halves, a=2)[:, :, 1:1 + NB * TP]
        w1_hi, w1_lo = [parts(f"soft_w1_{n}", 2 * NB * TP + 2 * HID * i, 2 * HID, wa_at, DH + 1).rearrange(halves, a=2)
                        for i, n in enumerate(("high", "low"))]
        ct = ht
        dbuf = [cut(s, 16384 + 1024 * i, NB, TP) for i in range(2)]
        cbuf = [cut(s, 18432 + 1024 * i, NE * NS) for i in range(2)]
        ub = [cut(s, 19456 + HID * i, 6, 2 * TP) for i in range(2)]
        sacc = xn
        hb = [cut(s, 20992 + HID * i, HID) for i in range(2)] + \
             [cut(wb, 5376 + HID * i, HID) for i in range(2)]
        SS = {name: sem(f"soft_{name}") for name in
              "phi loaded0 loaded1 x_hi x_lo w_hi w_lo zero dl_mm dl_arg d_exp d_ready cl_mm c_max c_exp t_mm t_ev t_lo "
              "xw_mm xw_hi xw_ev f1_mm f1_ev "
              "u_mm u_ev f2_mm acc_ev".split()}
        NQ = NE * NJ
        cmax, crs, csum = small[:, 0:16], small[:, 16:24], small[:, 96:96 + 4 * NJ]
        dmx, dsum = small[:, 48:64], small[:, 64:80]

        def soft_pe(pe):
            pe.wait_ge(SS["phi"], 16)
            r = 0

            def turn(src, n):
                nonlocal r
                for u in range(0, n, 4):
                    if r >= 4:
                        pe.wait_ge(SS["t_ev"], r - 3)
                        pe.wait_ge(SS["t_lo"], min(r - 3, 16))
                    for i in range(4):
                        m = pe.transpose(ps[:, 4 + r % 4, 128 * i:128 * i + 128], src[:, 128 * (u + i):128 * (u + i) + 128],
                                         ident[:, :])
                    m.then_inc(SS["t_mm"], 1)
                    r += 1

            def dispatch_logits(ch):
                if ch >= 2:
                    pe.wait_ge(SS["dl_arg"], ch - 1)
                for nh in range(2):
                    for k in range(2):
                        m = pe.matmul(ps[:, 2 * (ch % 2) + nh, 0:N51], phi[:, k, 128 * ch:128 * ch + 128],
                                      tok(xt[:, k, :])[:, nh * HALF:nh * HALF + HALF, 0:T], start=k == 0, stop=k == 1)
                m.then_inc(SS["dl_mm"], 1)

            def combine_logits(j):
                if j == 0:
                    pe.wait_ge(SS["dl_arg"], 7)
                elif j == 1:
                    pe.wait_ge(SS["dl_arg"], 8)
                else:
                    pe.wait_ge(SS["c_exp"], j - 1)
                for q in range(2):
                    for k in range(2):
                        m = pe.matmul(ps[:, 2 * (j % 2) + q, :], xt[:, k, 128 * j:128 * j + 128],
                                      phi[:, k, 512 * q:512 * q + 512], start=k == 0, stop=k == 1)
                m.then_inc(SS["cl_mm"], 1)

            dispatch_logits(0)
            for ch in range(8):
                if ch < 7:
                    dispatch_logits(ch + 1)
                else:
                    combine_logits(0)
                pe.wait_ge(SS["d_ready"], ch + 1)
                turn(dbuf[ch % 2].rearrange("p b t -> p (b t)"), 8)
            for j in range(NJ):
                if j < 7:
                    combine_logits(j + 1)
                pe.wait_ge(SS["c_exp"], j + 1)
                turn(cbuf[j % 2], 8)
            pe.wait_ge(SS["t_ev"], 32)

            def up(q):
                e, j = divmod(q, NJ)
                if j == 0:
                    pe.wait_ge(SS["w_hi"], e + 1)
                    pe.wait_ge(SS["w_lo"], e + 1)
                if q >= 1:
                    pe.wait_ge(SS["xw_ev"], q)
                for part in range(2):
                    o, cols = ps[:, 4 + part, 0:384], slice(384 * part, 384 * part + 384)
                    for k in range(2):
                        xh, xl = x_hi[:, k, 128 * j:128 * j + 128], x_lo[:, k, 128 * j:128 * j + 128]
                        pe.matmul(o, xh, w1_hi[:, k, cols], start=k == 0, stop=False)
                        pe.matmul(o, xh, w1_lo[:, k, cols], start=False, stop=False)
                        m = pe.matmul(o, xl, w1_hi[:, k, cols], start=False, stop=k == 1)
                m.then_inc(SS["xw_mm"], 1)

            def hidden(q, par, sc):
                e, j = divmod(q, NJ)
                i = 4 * q + 2 * par + sc
                if i >= 2:
                    pe.wait_ge(SS["f1_ev"], i - 1)
                at = slice(64 * par, 64 * par + 64)
                c0 = NS * e + 128 * sc
                dh, dl = dt_hi[at, j, c0:c0 + 128], dt_lo[at, j, c0:c0 + 128]
                for part in range(2):
                    o, cols = ps[:, 2 * (i % 2) + part, 0:384], slice(384 * part, 384 * part + 384)
                    pe.matmul(o, dh, xw_hi[q % 2][at, cols], start=True, stop=False)
                    pe.matmul(o, dh, xw_lo[q % 2][at, cols], start=False, stop=False)
                    m = pe.matmul(o, dl, xw_hi[q % 2][at, cols], start=False, stop=True)
                m.then_inc(SS["f1_mm"], 1)

            def combine(q, par):
                e, j = divmod(q, NJ)
                i = 2 * q + par
                pe.wait_ge(SS["f1_ev"], 2 * i + 2)
                if i >= 1:
                    pe.wait_ge(SS["u_ev"], i)
                for m6 in range(6):
                    for sc in range(2):
                        m = pe.matmul(ps[:, 6, TP * m6:TP * m6 + T], hb[(2 * i + sc) % 4][:, 128 * m6:128 * m6 + 128],
                                      ct[:, 2 * e + sc, 128 * j + 64 * par:128 * j + 64 * par + T],
                                      start=sc == 0, stop=sc == 1)
                m.then_inc(SS["u_mm"], 1)

            def down(q):
                e, j = divmod(q, NJ)
                if j == 0:
                    pe.wait_ge(SS[f"loaded{e % 2}"], 32 * (e // 2 + 1))
                pe.wait_ge(SS["u_ev"], 2 * q + 2)
                if q >= 1:
                    pe.wait_ge(SS["acc_ev"], q)
                for m6 in range(6):
                    m = pe.matmul(ps[:, 7, 0:D], ub[q % 2][:, m6, :], soft_w[e % 2][1][:, m6, :],
                                  start=m6 == 0, stop=m6 == 5)
                m.then_inc(SS["f2_mm"], 1)

            pe.wait_ge(SS["x_hi"], 1)
            pe.wait_ge(SS["x_lo"], 1)
            up(0)
            for q in range(NQ):
                pe.wait_ge(SS["xw_ev"], q + 1)
                hidden(q, 0, 0)
                hidden(q, 0, 1)
                if q >= 1:
                    combine(q - 1, 1)
                hidden(q, 1, 0)
                hidden(q, 1, 1)
                if q + 1 < NQ:
                    up(q + 1)
                combine(q, 0)
                if q >= 1:
                    down(q - 1)
            combine(NQ - 1, 1)
            down(NQ - 1)

        def soft_pool(pool):
            xt_ready(pool, 5)
            pool.tensor_copy(x_hi, xt97).then_inc(SS["x_hi"], 1)
            for e in range(NE):
                pool.wait_ge(SS[f"loaded{e % 2}"], 32 * (e // 2 + 1))
                if e >= 1:
                    pool.wait_ge(SS["xw_mm"], NJ * e)
                w1 = soft_w[e % 2][0]
                pool.tensor_copy(w1_hi, w1).then_inc(SS["w_hi"], 1)
                pool.wait_ge(SS["w_hi"], e + 1)
                pool.tensor_tensor(w1_lo, w1, w1_hi, ALU.subtract).then_inc(SS["w_lo"], 1)

        def soft_act(act):
            r = 0

            def turned(dst):
                nonlocal r
                act.wait_ge(SS["t_mm"], r + 1)
                act.activation(dst, ps[:, 4 + r % 4, :].rearrange("p (a b) -> p a b", a=4), ACT.Copy)\
                    .then_inc(SS["t_ev"], 1)
                r += 1
            load_table(act, ACT.Exp)
            for ch in range(8):
                act.wait_ge(SS["dl_arg"], ch + 1)
                x = dbuf[ch % 2][:, :, 0:T]
                act.activation(x, x, ACT.Exp).then_inc(SS["d_exp"], 1)
                for u in range(2):
                    turned(dt_hi[:, 4 * u:4 * u + 4, 128 * ch:128 * ch + 128])
            for j in range(NJ):
                act.wait_ge(SS["c_max"], j + 1)
                for e in range(NE):
                    ins = act.activation(cbuf[j % 2][:, NS * e:NS * e + NS],
                                         ps[:, 2 * (j % 2) + e // 2, NS * (e % 2):NS * (e % 2) + NS], ACT.Exp,
                                         bias=cmax[:, j:j + 1], accum_out=csum[:, NE * j + e:NE * j + e + 1])
                ins.then_inc(SS["c_exp"], 1)
                for u in range(2):
                    turned(ct[:, 4 * u:4 * u + 4, 128 * j:128 * j + 128])
            load_table(act, ACT.Gelu_apprx_tanh)
            for i in range(4 * NQ):
                act.wait_ge(SS["f1_mm"], i + 1)
                if i >= 4:
                    act.wait_ge(SS["u_mm"], i // 2 - 1)
                b2_ = 2 * (i % 2)
                act.activation(hb[i % 4].rearrange("p (a n) -> p a n", a=2), ps[:, b2_:b2_ + 2, 0:384],
                               ACT.Gelu_apprx_tanh).then_inc(SS["f1_ev"], 1)

        def soft_dve(v):
            link = dve_chain.link
            v.wait_ge(SS["zero"], 3)

            def dispatch_low(ch):
                for u in range(2):
                    r = 2 * ch + u
                    v.wait_ge(SS["t_ev"], r + 1)
                    at = (slice(None), slice(4 * u, 4 * u + 4), slice(128 * ch, 128 * ch + 128))
                    v.tensor_tensor(dt_lo[at], ps[:, 4 + r % 4, :].rearrange("p (a b) -> p a b", a=4), dt_hi[at],
                                    ALU.subtract).then_inc(SS["t_lo"], 1)
            for ch in range(8):
                v.wait_ge(SS["dl_mm"], ch + 1)
                if ch >= 2:
                    v.wait_ge(SS["t_mm"], 2 * (ch - 1))
                d = dbuf[ch % 2]
                for nh in range(2):
                    o = ps[:, 2 * (ch % 2) + nh, 0:N51].rearrange("p (b t) -> p b t", t=T)
                    ins = v.tensor_reduce(dmx[:, 8 * nh:8 * nh + 8], o, AX.X, ALU.max)
                link(ins)
                for nh in range(2):
                    o = ps[:, 2 * (ch % 2) + nh, 0:N51].rearrange("p (b t) -> p b t", t=T)
                    ins = v.tensor_tensor(d[:, 8 * nh:8 * nh + 8, 0:T], o,
                                          dmx[:, 8 * nh:8 * nh + 8].unsqueeze(2).to_broadcast([128, 8, T]), ALU.subtract)
                ins.then_inc(SS["dl_arg"], 1)
                if ch >= 1:
                    dispatch_low(ch - 1)
                v.wait_ge(SS["d_exp"], ch + 1)
                link(v.tensor_reduce(dsum, d[:, :, 0:T], AX.X, ALU.add))
                link(v.reciprocal(dsum, dsum))
                v.tensor_tensor(d[:, :, 0:T], d[:, :, 0:T], dsum.unsqueeze(2).to_broadcast([128, NB, T]), ALU.mult)\
                    .then_inc(SS["d_ready"], 1)
            dispatch_low(7)
            for j in range(NJ):
                v.wait_ge(SS["cl_mm"], j + 1)
                if j >= 2:
                    v.wait_ge(SS["t_mm"], 16 + 2 * (j - 1))
                v.tensor_reduce(cmax[:, j:j + 1], ps[:, 2 * (j % 2):2 * (j % 2) + 2, :], AX.XY, ALU.max, negate=True)\
                    .then_inc(SS["c_max"], 1)
            v.wait_ge(SS["x_hi"], 1)
            v.tensor_tensor(x_lo, xt97, x_hi, ALU.subtract).then_inc(SS["x_lo"], 1)
            v.wait_ge(SS["c_exp"], NJ)
            link(v.tensor_reduce(crs, csum.rearrange("p (j e) -> p j e", e=NE), AX.X, ALU.add))
            link(v.reciprocal(crs, crs))
            v.wait_ge(SS["t_mm"], 32)
            v.memset(sacc[:, :, :], 0.0)
            for x in ub:
                ins = v.memset(x, 0.0)
            link(ins)

            def up_ready(q):
                v.wait_ge(SS["xw_mm"], q + 1)
                if q >= 2:
                    v.wait_ge(SS["f1_mm"], 4 * (q - 1))
                hi, lo = (x[q % 2].rearrange("p (a n) -> p a n", a=2) for x in (xw_hi, xw_lo))
                v.tensor_copy(hi, ps[:, 4:6, 0:384]).then_inc(SS["xw_hi"], 1)
                v.wait_ge(SS["xw_hi"], q + 1)
                v.tensor_tensor(lo, ps[:, 4:6, 0:384], hi, ALU.subtract).then_inc(SS["xw_ev"], 1)

            def combined(q, par):
                v.wait_ge(SS["u_mm"], 2 * q + par + 1)
                if q >= 2 and par == 0:
                    v.wait_ge(SS["f2_mm"], q - 1)
                v.tensor_copy(ub[q % 2][:, :, 64 * par:64 * par + T],
                              ps[:, 6, 0:384].rearrange("p (m t) -> p m t", t=TP)[:, :, 0:T]).then_inc(SS["u_ev"], 1)

            def accumulate(q):
                e, j = divmod(q, NJ)
                a_ = sacc[:, j, :]
                link(v.scalar_tensor_tensor(a_, row("l2_b2")[:, D * e:D * e + D], csum[:, NE * j + e:NE * j + e + 1], a_,
                                            ALU.mult, ALU.add))
                v.wait_ge(SS["f2_mm"], q + 1)
                v.tensor_tensor(a_, a_, ps[:, 7, 0:D], ALU.add).then_inc(SS["acc_ev"], 1)

            up_ready(0)
            for q in range(NQ):
                if q >= 1:
                    combined(q - 1, 1)
                if q + 1 < NQ:
                    up_ready(q + 1)
                combined(q, 0)
                if q >= 1:
                    accumulate(q - 1)
            combined(NQ - 1, 1)
            accumulate(NQ - 1)
            v.wait_ge(SS["acc_ev"], NQ)
            for j in range(NJ):
                v.scalar_tensor_tensor(h[:, j, :], sacc[:, j, :], crs[:, j:j + 1], h[:, j, :], ALU.mult, ALU.add)\
                    .then_inc(S["resid"], 1)
            v.wait_ge(S["resid"], NJ * 6)

        consts = [(ident[:, :], a["ident"]), (rows[:, :], a["rows"].partition_broadcast(128)), (vec[:, :, :], a["vec"]),
                  (clsrow[0:1, :], a["cls"][0:1, :]), (clsrow[1:2, :], a["cls"][1:2, :]),
                  (clsrow[64:65, :], a["cls"][0:1, :]), (clsrow[65:66, :], a["cls"][1:2, :]),
                  (live[:, :], a["live"]), (xt97[DH:DH + 1, :, :], a["mark"]), (inb[:, :], a["inb"]), (b1[:, :], a["b1"]),
                  (wrouter[:, :, :], a["wrouter"]), (cmask[:, :], a["cmask"])]
        NCONST = len(consts)

        @block.sync
        def _(sp):
            sp.dma_start(haar, a["haar"]).then_inc(S["tok_loaded"], 16)
            sp.dma_start(pg_w1, a["pg_w1"]).then_inc(S["tok_loaded"], 16)
            sp.dma_start(pl_w, a["pl_w"]).then_inc(S["tok_loaded"], 16)
            sp.dma_start(patches[:, 0:3, :], a["patches"][:, 0:3, :]).then_inc(S["patches_loaded"], 16)
            sp.dma_start(patches[:, 3:6, :], a["patches"][:, 3:6, :]).then_inc(S["patches_loaded"], 16)
            sp.wait_ge(S["zeroed"], 3)
            for dst, src in consts:
                sp.dma_start(dst, src).then_inc(S["consts_loaded"], 16)
            sp.dma_start(pw, a["pw"]).then_inc(S["tok_loaded"], 16)
            sp.dma_start(w_kvro, a["w_kvro"]).then_inc(S["l0_loaded"], 16)
            sp.dma_start(w_in, a["w_in"]).then_inc(S["l0_loaded"], 16)
            sp.dma_start(w_out, a["w_out"]).then_inc(S["l0_loaded"], 16)
            def attention_weights(c, name):
                if c.n == 2:
                    sp.wait_ge(S["f3_mm"], NJ)
                else:
                    sp.wait_ge(S["resid"], NJ * (c.n - 1 if c.n == 4 else c.n))
                sp.dma_start(c.w_q, a[name + "_q"]).then_inc(c.sems["loaded"], 16)
                sp.dma_start(c.w_k, a[name + "_k"]).then_inc(c.sems["loaded"], 16)
                sp.dma_start(c.w_v, a[name + "_v"]).then_inc(c.sems["loaded"], 16)
                sp.dma_start(c.w_o, a[name + "_o"]).then_inc(c.sems["loaded"], 16)

            def expert_weights(c, name):
                def up(e):
                    if e >= 2:
                        sp.wait_ge(c.sems["w_lo"], e - 1)
                    for i, part in enumerate(("_w1", "_w2")):
                        sp.dma_start(c.w[e][i], a[name + part][e]).then_inc(c.sems[f"loaded{e % 2}"], 16)

                sp.wait_ge(S["resid"], NJ * (2 if c.tag == "m1" else 6))
                up(0)
                for e in range(8):
                    if e < 7:
                        up(e + 1)
                    if e >= 2:
                        sp.wait_ge(c.sems["down_mm"], NJ * (e - 1))
                    sp.dma_start(c.w[e][2], a[name + "_w3"][e]).then_inc(c.sems[f"loaded_down{e % 2}"], 16)
                    if e == 1 and c.tag == "m3":
                        for i, part in enumerate(("_s1", "_s2")):
                            sp.dma_start(c.w[8][i], a[name + part]).then_inc(c.sems["loaded_shared"], 16)
                        sp.dma_start(c.w[8][2], a[name + "_s3"]).then_inc(c.sems["loaded_shared"], 16)

            attention_weights(att1, "a1")
            expert_weights(moe1, "m1")
            attention_weights(att2, "a2")
            sp.wait_ge(S["resid"], NJ * 4)
            sp.dma_start(phi, a["phi"]).then_inc(SS["phi"], 16)
            for e in range(NE):
                if e >= 2:
                    sp.wait_ge(SS["f2_mm"], NJ * (e - 1))
                sp.dma_start(soft_w[e % 2][0], a["soft_w1"][e]).then_inc(SS[f"loaded{e % 2}"], 16)
                sp.dma_start(soft_w[e % 2][1], a["soft_w2"][e]).then_inc(SS[f"loaded{e % 2}"], 16)
            attention_weights(att3, "a3")
            expert_weights(moe3, "m3")
            sp.wait_ge(S["resid"], NJ * 8)
            o = out.rearrange("(j i) t d -> i t j d", i=2)
            sp.dma_start(o[0], h[0:T, :, :]).then_inc(S["out_done"], 16)
            sp.dma_start(o[1], h[64:64 + T, :, :]).then_inc(S["out_done"], 16)
            sp.wait_ge(S["out_done"], 32)

        @block.gpsimd
        def _(pool):
            pool.memset(clsrow[:, :], 0.0)
            pool.memset(eps[:, :], EPS)
            pool.memset(xt_store[0:DH, :, 0:1], 0.0)
            pool.memset(cut(s, 4704, 2 * 2592, rows=DH), 0.0).then_inc(S["zeroed"], 1)
            pool.memset(dw3[:, :, :], 0.0).then_inc(S["zeroed"], 1)
            pool.memset(ht[:, :, :], 0.0).then_inc(S["zeroed"], 1)
            tokenizer_pool(pool)
            def clear(view, n, signal):
                pool.wait_ge(S["resid"], NJ * n)
                pool.memset(view, 0.0).then_inc(signal, 1)

            clear(att1.p_all, 2, att1.sems["p_zero"])
            moe_pool(pool, moe1)
            clear(att2.p_all, 4, att2.sems["p_zero"])
            clear(cut(s, 16384, 2048), 5, SS["zero"])
            pool.wait_ge(SS["zero"], 1)
            for d in dbuf:
                pool.memset(d[:, :, T:T + 1], 1.0).then_inc(SS["zero"], 1)
            soft_pool(pool)
            clear(att3.v_all, 6, att3.sems["v_zero"])
            clear(att3.p_all, 6, att3.sems["p_zero"])
            moe_pool(pool, moe3)

        @block.tensor
        def _(pe):
            tokenizer_pe(pe)
            layernorm_pe(pe, 0)
            rwkv_pe(pe)
            layernorm_pe(pe, 1)
            ffn0_pe(pe)
            layernorm_pe(pe, 2)
            attn_pe(pe, att1)
            layernorm_pe(pe, 3)
            moe_pe(pe, moe1)
            layernorm_pe(pe, 4)
            attn_pe(pe, att2)
            layernorm_pe(pe, 5)
            soft_pe(pe)
            layernorm_pe(pe, 6)
            attn_pe(pe, att3)
            layernorm_pe(pe, 7)
            moe_pe(pe, moe3)

        @block.scalar
        def _(act):
            tokenizer_act(act)
            normalize_act(act, -1)
            layernorm_act(act, 0)
            rwkv_act(act)
            layernorm_act(act, 1)
            ffn0_act(act)
            layernorm_act(act, 2)
            attn_act(act, att1)
            layernorm_act(act, 3)
            moe_act(act, moe1)
            layernorm_act(act, 4)
            attn_act(act, att2)
            layernorm_act(act, 5)
            soft_act(act)
            layernorm_act(act, 6)
            attn_act(act, att3)
            layernorm_act(act, 7)
            moe_act(act, moe3)

        @block.vector
        def _(v):
            tokenizer_dve(v)
            layernorm_dve(v, 0)
            rwkv_dve(v)
            layernorm_dve(v, 1)
            residual_dve(v, 1)
            layernorm_dve(v, 2)
            attn_dve(v, att1)
            layernorm_dve(v, 3)
            moe_dve(v, moe1)
            layernorm_dve(v, 4)
            attn_dve(v, att2)
            layernorm_dve(v, 5)
            soft_dve(v)
            layernorm_dve(v, 6)
            attn_dve(v, att3)
            layernorm_dve(v, 7)
            moe_dve(v, moe3)


def weights(w, kc):
    return w.reshape(w.shape[0] // kc, kc, w.shape[1]).transpose(1, 0, 2)


def haar_matrix():
    m = np.ones((256, 256), np.float32)
    for band in range(256):
        for level in range(4):
            digit = (band >> (2 * (3 - level))) & 3
            for pixel in range(256):
                y, x = divmod(pixel, 16)
                if (digit >> 1) & (x >> level) & 1:
                    m[band, pixel] *= -1
                if digit & (y >> level) & 1:
                    m[band, pixel] *= -1
    return m / 16


def lay_out(i):
    sq = {k: np.asarray(v, np.float32) for k, v in i.items()}
    o = {}
    x = sq["x"].reshape(NB, 3, SIDE, 16, SIDE, 16).transpose(1, 3, 5, 2, 4, 0).reshape(768, NB * NP)
    o["patches"] = weights(x, 128)
    o["pl_w"] = weights(sq["L0_tok_pl_w"].reshape(D, 768).T, 128)
    pg = sq["L0_tok_pg_w1"].reshape(D, 256, 3).transpose(1, 2, 0)
    o["pg_w1"] = pg.reshape(2, 128, 3, D).transpose(1, 0, 2, 3)
    o["haar"] = haar_matrix().reshape(2, 128, 256).transpose(1, 0, 2)
    o["pw"] = np.stack([weights(sq[f"L0_tok_{n}"].reshape(D, D).T, DH)
                        for n in ("pl_pw", "pg_pw", "pg_w2", "f1_pw", "f2_pw", "f3_pw")], 1)
    names = {"pl_b": "L0_tok_pl_b", "pl_pwb": "L0_tok_pl_pwb", "pg_b1": "L0_tok_pg_b1", "pg_pwb": "L0_tok_pg_pwb",
             "pg_b2": "L0_tok_pg_b2", "alpha": "L0_tok_alpha", "f1_pwb": "L0_tok_f1_pwb", "f2_pwb": "L0_tok_f2_pwb",
             "decay": "L0_attn_time_decay", "first": "L0_attn_time_first", "mk": "L0_attn_time_mix_k",
             "mv": "L0_attn_time_mix_v", "mr": "L0_attn_time_mix_r"}
    vec = np.zeros((D, NVEC), np.float32)
    for n, c in VEC.items():
        vec[:, c] = sq[names[n]].reshape(D)
    for n, c in TAPS.items():
        vec[:, c:c + 9] = sq[f"L0_tok_{n}_dw"].reshape(D, 9)
    o["vec"] = weights(vec, DH)
    rows = {"f3_pwb": "L0_tok_f3_pwb", "ln_g": "L0_tok_ln_g", "ln_b": "L0_tok_ln_b", "l1_b": "L1_attn_b_proj",
            "l2_b": "L2_attn_b_o", "l2_b2": "L2_ffn_b2", "router_b": "L1_ffn_router_b", "sg_b": "L3_ffn_sg_b"}
    sq["rank"] = np.arange(8, 0, -1, dtype=np.float32)
    rows["rank"] = "rank"
    o["rows"] = np.concatenate([sq[rows[n]].reshape(-1) for n in ROWS])
    o["cls"] = np.stack([sq["cls_tok"].reshape(D), sq["L0_tok_cls"].reshape(D)])
    live = np.zeros((2, TP, 2), np.float32)
    live[:, 2:T, 0] = 1
    live[:, 0:T, 1] = 1
    o["live"] = live.reshape(128, 2)
    mark = np.zeros((1, 2, NB, TP), np.float32)
    mark[:, 0, :, T] = 1
    o["mark"] = mark.reshape(1, 2, NB * TP)
    o["ident"] = np.eye(128, dtype=np.float32)
    o["inb"] = sq["L0_ffn_in_bias"].reshape(6, 128).T
    o["b1"] = sq["L2_ffn_b1"].reshape(24, 128).T
    o["wrouter"] = weights(np.concatenate([sq["L1_ffn_router_w"], sq["L3_ffn_router_w"], sq["L3_ffn_sg_w"]], 1), DH)
    q = np.arange(128)[:, None] % TP
    o["cmask"] = np.where(np.arange(T)[None, :] <= q, 0.0, -1e30).astype(np.float32)
    o["w_kvro"] = np.stack([weights(sq[f"L0_attn_W{n}"].T, DH) for n in "kvro"], 1)
    o["w_in"] = weights(sq["L0_ffn_in_weight"].T, DH)
    o["w_out"] = weights(sq["L0_ffn_out_weight"], 128)
    third = sq["L1_attn_w_qkv"].reshape(3, 8, 3, 8, D)

    def slots(w):
        p = np.zeros((8, 32, D), np.float32)
        p[:, :8] = w
        return p.reshape(256, D).T

    o["a1_q"] = weights(np.concatenate([slots(third[0, :, t]) for t in (1, 2)], 1), DH).reshape(DH, 2, 4, 128)
    o["a1_k"] = weights(np.concatenate([slots(third[1, :, t]) for t in (0, 1, 2)], 1), DH).reshape(DH, 2, 6, 128)
    v3, v4, v5 = (third[2, :, t].reshape(64, D).T for t in range(3))
    o["a1_v"] = weights(np.concatenate([v3, v3, v4, v4, v5, v5], 1), DH).reshape(DH, 2, 2, 192)
    o["a1_o"] = weights(sq["L1_attn_w_proj"].T, DH)
    o["a2_q"] = weights(sq["L2_attn_w_q"], DH).reshape(DH, 2, 6, 128)
    o["a2_k"] = weights(sq["L2_attn_w_k"], DH).reshape(DH, 2, 6, 128)

    def parities(w, groups):
        per = 12 // groups
        heads = [groups * (n % per) + n // per for n in range(12)]
        return np.stack([w[:, heads[par::2]] for par in range(2)], 1).reshape(D, -1), heads[0::2] + heads[1::2]

    o["a2_v"] = weights(parities(sq["L2_attn_w_v"].reshape(D, 12, 64), 2)[0], DH).reshape(DH, 2, 2, 384)
    o["a2_o"] = weights(sq["L2_attn_w_o"], 128)

    def wide(w):
        p = np.zeros((D, 12, 32), np.float32)
        p[:, :, :16] = w
        return p.reshape(D, 384)

    o["a3_q"] = weights(wide(sq["L3_attn_query_mat"]), DH).reshape(DH, 2, 3, 128)
    o["a3_k"] = weights(wide(sq["L3_attn_key_mat"]), DH).reshape(DH, 2, 3, 128)
    vals, order = parities(sq["L3_attn_value_mat"], 4)
    o["a3_v"] = weights(vals, DH).reshape(DH, 2, 2, 96)
    o["a3_o"] = weights(sq["L3_attn_linear_m1"].reshape(12, 16, D)[order].reshape(D, D), DH)

    def experts(w, kc):
        return np.stack([weights(x, kc) for x in w])

    def twice(w):
        return np.stack([w[..., 0:128, :], np.concatenate([w[..., 128:192, :]] * 2, -2)], -2)

    for n, (x1, x2, x3), kc in (("m1", ("L1_ffn_w1", "L1_ffn_w2", "L1_ffn_w3"), 128),
                                ("m3", ("L3_ffn_w_gate", "L3_ffn_w_up", "L3_ffn_w_down"), DH)):
        o[n + "_w1"], o[n + "_w2"], o[n + "_w3"] = twice(sq[x1]), twice(sq[x2]), experts(sq[x3], kc)
    o["m3_s1"] = twice(sq["L3_ffn_ws_gate"])
    o["m3_s2"] = twice(sq["L3_ffn_ws_up"])
    o["m3_s3"] = weights(sq["L3_ffn_ws_down"], 128)
    o["phi"] = weights(sq["L2_ffn_phi"].reshape(4 * 256, D).T, DH)
    bias = np.stack([sq["L2_ffn_b1"], np.zeros_like(sq["L2_ffn_b1"])], 1)[:, None]
    o["soft_w1"] = np.concatenate([experts(sq["L2_ffn_w1"], DH), bias], 1)
    o["soft_w2"] = experts(sq["L2_ffn_w2"], 128)
    return {k: np.ascontiguousarray(v) for k, v in o.items()}


def kernel(**inputs):
    import concourse.bacc as bacc
    from concourse.bass_utils import run_bass_kernel_spmd

    nc = bacc.Bacc("TRN2", target_bir_lowering=False, num_devices=1)
    arrays = lay_out(inputs)
    aps = {n: nc.dram_tensor(f"in_{n}", v.shape, F32, kind="ExternalInput").ap() for n, v in arrays.items()}
    out = nc.dram_tensor("tokens", (NB, T, D), F32, kind="ExternalOutput").ap()
    vit_tower(nc, aps, out)
    return run_bass_kernel_spmd(nc, [{f"in_{n}": v for n, v in arrays.items()}], core_ids=[0]).results[0]["tokens"]
```
